# Optimizing a Trainium2 kernel written in Bass

```python
import numpy as np
import jax
import jax.numpy as jnp

def _softmax(x, axis=-1):
    return jax.nn.softmax(x, axis=axis)
def _gelu(x):
    return jax.nn.gelu(x, approximate=True)
def _silu(x):
    return jax.nn.silu(x)
def _sigmoid(x):
    return jax.nn.sigmoid(x)
def _layernorm(x, axis=-1, eps=1e-5):
    m = jnp.mean(x, axis=axis, keepdims=True)
    v = jnp.var(x, axis=axis, keepdims=True)
    return (x - m) / jnp.sqrt(v + eps)
def _scatter_add(tgt, idx, src, axis=0):
    return tgt.at[idx].add(src)
def _segment_sum(src, seg, n):
    return jax.ops.segment_sum(src, seg, n)

kernel_name = 'mk_conv_attn_hybrid_d2_conv_nhwc256_74fd65'

def setup_inputs(seed: int = 0):
    np.random.seed(seed)
    _w = jnp.asarray
    def _rec_inputs():
        import jax
        import jax.numpy as jnp
        _gk = jax.random.key(seed)
        x = -0.001003 + 1 * jax.random.normal(jax.random.fold_in(_gk, 1), (8, 12, 64, 256), jnp.float32)
        return x
    x = _rec_inputs()
    def _L0_conv_setup():
        import jax, jax.numpy as jnp
        import numpy as np
        from jax import lax
        B, O, T, DM = (8, 12, 64, 256)
        NL = 2
        EXP = 2
        DI = DM * EXP
        DS = 16
        DCONV = 4
        DTR = DM // 16

        def _layernorm(x, w, b, eps=1e-05):
            m = jnp.mean(x, axis=-1, keepdims=True)
            v = jnp.mean(jnp.square(x - m), axis=-1, keepdims=True)
            return (x - m) * lax.rsqrt(v + eps) * w + b

        def _selective_scan(xc, delta, Bm, Cm, A, Dpar):

            def step(h, t):
                d_t, B_t, C_t, x_t = t
                dA = jnp.exp(d_t[..., None] * A)
                h = dA * h + (d_t * x_t)[..., None] * B_t[:, None, :]
                y = jnp.einsum('bds,bs->bd', h, C_t)
                return (h, y)
            h0 = jnp.zeros((xc.shape[0], DI, DS), xc.dtype)
            tm = lambda a: jnp.swapaxes(a, 0, 1)
            _, ys = lax.scan(step, h0, (tm(delta), tm(Bm), tm(Cm), tm(xc)))
            return jnp.swapaxes(ys, 0, 1) + xc * Dpar

        def _mamba_dir(x, ip, cw, cb, xp, dw, db, alog, dpar, op):
            xz = x @ ip
            xin, z = jnp.split(xz, 2, axis=-1)
            conv = lax.conv_general_dilated(jnp.swapaxes(xin, 1, 2), cw[:, None, :], (1,), [(DCONV - 1, 0)], feature_group_count=DI)
            xc = jax.nn.silu(jnp.swapaxes(conv, 1, 2) + cb)
            dbl = xc @ xp
            dt, Bm, Cm = (dbl[..., :DTR], dbl[..., DTR:DTR + DS], dbl[..., DTR + DS:])
            delta = jax.nn.softplus(dt @ dw + db)
            A = -jnp.exp(alog)
            y = _selective_scan(xc, delta, Bm, Cm, A, dpar)
            return y * jax.nn.silu(z) @ op

        def _bimamba(x, params, l, blk):
            fwd = _mamba_dir(x, *[p[l, blk, 0] for p in params])
            bwd = _mamba_dir(x[:, ::-1], *[p[l, blk, 1] for p in params])[:, ::-1]
            return fwd + bwd

        def _forward(x, pe, ln_w, ln_b, in_proj, conv_w, conv_b, x_proj, dt_w, dt_b, A_log, Dp, out_proj):
            batch, no, nf, f = x.shape
            x = x + pe[:nf]
            params = (in_proj, conv_w, conv_b, x_proj, dt_w, dt_b, A_log, Dp, out_proj)
            for l in range(NL):
                s1 = _layernorm(_bimamba(x.reshape(batch, -1, f), params, l, 0), ln_w, ln_b)
                y = jnp.transpose(x, (0, 2, 1, 3))
                s2 = _layernorm(_bimamba(y.reshape(batch, -1, f), params, l, 1), ln_w, ln_b)
                out = (s1 + s2) / 2
                x = out.reshape(batch, no, nf, f) + x
            return x
        key = jax.random.key(seed)
        ks = jax.random.split(key, 10)
        s = 0.02
        shp = (NL, 2, 2)
        A_init = jnp.broadcast_to(jnp.log(jnp.arange(1, DS + 1, dtype=jnp.float32)), shp + (DI, DS))
        return {'x': jax.random.normal(ks[0], (B, O, T, DM), jnp.float32), 'pe': jax.random.normal(ks[1], (T, DM), jnp.float32) * s, 'ln_w': jnp.ones((DM,), jnp.float32), 'ln_b': jnp.zeros((DM,), jnp.float32), 'in_proj': jax.random.normal(ks[2], shp + (DM, 2 * DI)) * s, 'conv_w': jax.random.normal(ks[3], shp + (DI, DCONV)) * s, 'conv_b': jnp.zeros(shp + (DI,), jnp.float32), 'x_proj': jax.random.normal(ks[4], shp + (DI, DTR + 2 * DS)) * s, 'dt_w': jax.random.normal(ks[5], shp + (DTR, DI)) * s, 'dt_b': jax.random.normal(ks[6], shp + (DI,)) * s + 0.5, 'A_log': A_init, 'Dp': jnp.ones(shp + (DI,), jnp.float32), 'out_proj': jax.random.normal(ks[7], shp + (DI, DM)) * s}
    _L0_conv_all = _L0_conv_setup()
    _L0_conv_in = {k: v for k, v in _L0_conv_all.items() if k in ('pe', 'ln_w', 'ln_b', 'in_proj', 'conv_w', 'conv_b', 'x_proj', 'dt_w', 'dt_b', 'A_log', 'Dp', 'out_proj', )}
    del _L0_conv_all

    def _L1_attn_setup():
        import jax, jax.numpy as jnp
        import numpy as np
        ALPHA = 0.01
        key = jax.random.key(seed)
        k1, k2, k3 = jax.random.split(key, 3)
        B, N, F_in, F_out = (32, 1024, 256, 256)
        inp = jax.random.normal(k1, (B, N, F_in), dtype=jnp.float32)
        lim_W = 1.414 * np.sqrt(6.0 / (F_in + F_out))
        W = jax.random.uniform(k2, (F_in, F_out), dtype=jnp.float32, minval=-lim_W, maxval=lim_W)
        lim_a = 1.414 * np.sqrt(6.0 / (2 * F_out + 1))
        a = jax.random.uniform(k3, (2 * F_out, 1), dtype=jnp.float32, minval=-lim_a, maxval=lim_a)
        return {'inp': inp, 'W': W, 'a': a}
    _L1_attn_all = _L1_attn_setup()
    _L1_attn_in = {k: v for k, v in _L1_attn_all.items() if k in ('W', 'a', )}
    del _L1_attn_all

    def _L1_ffn_setup():
        import jax, jax.numpy as jnp
        import numpy as np
        NUM_EXPERTS = 8
        TOP_K = 2
        B, S, D = (8, 8192, 256)

        def _moe(tokens, router_w, w1, b1, w2, b2):
            N = tokens.shape[0]
            E = router_w.shape[0]
            logits = tokens.astype(jnp.float32) @ router_w.astype(jnp.float32).T
            probs = jax.nn.softmax(logits, axis=-1)
            rw, re = jax.lax.top_k(probs, TOP_K)
            if TOP_K > 1:
                rw = rw / jnp.maximum(rw.sum(-1, keepdims=True), 1e-12)
            rw = rw.astype(tokens.dtype)
            combine = jnp.zeros((N, E), tokens.dtype).at[jnp.arange(N)[:, None], re].set(rw)
            out = tokens
            for e in range(E):
                h = jax.nn.gelu(tokens @ w1[e] + b1[e], approximate=False)
                y = h @ w2[e] + b2[e]
                out = out + combine[:, e:e + 1] * y
            return out
        key = jax.random.key(seed)
        ks = jax.random.split(key, 4)
        scale = 1.0 / np.sqrt(D).astype(np.float32)
        return {'input_embeddings': jax.random.normal(ks[0], (B, S, D), jnp.float32), 'router_w': jax.random.normal(ks[1], (NUM_EXPERTS, D), jnp.float32) * scale, 'w1': jax.random.normal(ks[2], (NUM_EXPERTS, D, D), jnp.float32) * scale, 'b1': jnp.zeros((NUM_EXPERTS, D), jnp.float32), 'w2': jax.random.normal(ks[3], (NUM_EXPERTS, D, D), jnp.float32) * scale, 'b2': jnp.zeros((NUM_EXPERTS, D), jnp.float32)}
    _L1_ffn_all = _L1_ffn_setup()
    _L1_ffn_in = {k: v for k, v in _L1_ffn_all.items() if k in ('router_w', 'w1', 'b1', 'w2', 'b2', )}
    del _L1_ffn_all

    return {
        "x": x,
        "L0_conv_pe": _L0_conv_in["pe"],
        "L0_conv_ln_w": _L0_conv_in["ln_w"],
        "L0_conv_ln_b": _L0_conv_in["ln_b"],
        "L0_conv_in_proj": _L0_conv_in["in_proj"],
        "L0_conv_conv_w": _L0_conv_in["conv_w"],
        "L0_conv_conv_b": _L0_conv_in["conv_b"],
        "L0_conv_x_proj": _L0_conv_in["x_proj"],
        "L0_conv_dt_w": _L0_conv_in["dt_w"],
        "L0_conv_dt_b": _L0_conv_in["dt_b"],
        "L0_conv_A_log": _L0_conv_in["A_log"],
        "L0_conv_Dp": _L0_conv_in["Dp"],
        "L0_conv_out_proj": _L0_conv_in["out_proj"],
        "L1_attn_W": _L1_attn_in["W"],
        "L1_attn_a": _L1_attn_in["a"],
        "L1_ffn_router_w": _L1_ffn_in["router_w"],
        "L1_ffn_w1": _L1_ffn_in["w1"],
        "L1_ffn_b1": _L1_ffn_in["b1"],
        "L1_ffn_w2": _L1_ffn_in["w2"],
        "L1_ffn_b2": _L1_ffn_in["b2"],
    }

def reference(x, L0_conv_pe, L0_conv_ln_w, L0_conv_ln_b, L0_conv_in_proj, L0_conv_conv_w, L0_conv_conv_b, L0_conv_x_proj, L0_conv_dt_w, L0_conv_dt_b, L0_conv_A_log, L0_conv_Dp, L0_conv_out_proj, L1_attn_W, L1_attn_a, L1_ffn_router_w, L1_ffn_w1, L1_ffn_b1, L1_ffn_w2, L1_ffn_b2):
    import jax
    import jax.numpy as jnp
    def _L0_conv_ref(x, pe, ln_w, ln_b, in_proj, conv_w, conv_b, x_proj, dt_w, dt_b, A_log, Dp, out_proj):
        import jax, jax.numpy as jnp
        import numpy as np
        from jax import lax
        B, O, T, DM = (8, 12, 64, 256)
        NL = 2
        EXP = 2
        DI = DM * EXP
        DS = 16
        DCONV = 4
        DTR = DM // 16

        def _layernorm(x, w, b, eps=1e-05):
            m = jnp.mean(x, axis=-1, keepdims=True)
            v = jnp.mean(jnp.square(x - m), axis=-1, keepdims=True)
            return (x - m) * lax.rsqrt(v + eps) * w + b

        def _selective_scan(xc, delta, Bm, Cm, A, Dpar):

            def step(h, t):
                d_t, B_t, C_t, x_t = t
                dA = jnp.exp(d_t[..., None] * A)
                h = dA * h + (d_t * x_t)[..., None] * B_t[:, None, :]
                y = jnp.einsum('bds,bs->bd', h, C_t)
                return (h, y)
            h0 = jnp.zeros((xc.shape[0], DI, DS), xc.dtype)
            tm = lambda a: jnp.swapaxes(a, 0, 1)
            _, ys = lax.scan(step, h0, (tm(delta), tm(Bm), tm(Cm), tm(xc)))
            return jnp.swapaxes(ys, 0, 1) + xc * Dpar

        def _mamba_dir(x, ip, cw, cb, xp, dw, db, alog, dpar, op):
            xz = x @ ip
            xin, z = jnp.split(xz, 2, axis=-1)
            conv = lax.conv_general_dilated(jnp.swapaxes(xin, 1, 2), cw[:, None, :], (1,), [(DCONV - 1, 0)], feature_group_count=DI)
            xc = jax.nn.silu(jnp.swapaxes(conv, 1, 2) + cb)
            dbl = xc @ xp
            dt, Bm, Cm = (dbl[..., :DTR], dbl[..., DTR:DTR + DS], dbl[..., DTR + DS:])
            delta = jax.nn.softplus(dt @ dw + db)
            A = -jnp.exp(alog)
            y = _selective_scan(xc, delta, Bm, Cm, A, dpar)
            return y * jax.nn.silu(z) @ op

        def _bimamba(x, params, l, blk):
            fwd = _mamba_dir(x, *[p[l, blk, 0] for p in params])
            bwd = _mamba_dir(x[:, ::-1], *[p[l, blk, 1] for p in params])[:, ::-1]
            return fwd + bwd

        def _forward(x, pe, ln_w, ln_b, in_proj, conv_w, conv_b, x_proj, dt_w, dt_b, A_log, Dp, out_proj):
            batch, no, nf, f = x.shape
            x = x + pe[:nf]
            params = (in_proj, conv_w, conv_b, x_proj, dt_w, dt_b, A_log, Dp, out_proj)
            for l in range(NL):
                s1 = _layernorm(_bimamba(x.reshape(batch, -1, f), params, l, 0), ln_w, ln_b)
                y = jnp.transpose(x, (0, 2, 1, 3))
                s2 = _layernorm(_bimamba(y.reshape(batch, -1, f), params, l, 1), ln_w, ln_b)
                out = (s1 + s2) / 2
                x = out.reshape(batch, no, nf, f) + x
            return x
        return _forward(x, pe, ln_w, ln_b, in_proj, conv_w, conv_b, x_proj, dt_w, dt_b, A_log, Dp, out_proj)

    def _L1_attn_ref(inp, W, a):
        import jax, jax.numpy as jnp
        import numpy as np
        ALPHA = 0.01
        h = jnp.matmul(inp, W)
        F_out = W.shape[1]
        a1 = a[:F_out, 0]
        a2 = a[F_out:, 0]
        f1 = jnp.einsum('bnf,f->bn', h, a1)
        f2 = jnp.einsum('bnf,f->bn', h, a2)
        e = f1[:, :, None] + f2[:, None, :]
        e = jnp.where(e > 0, e, ALPHA * e)
        attention = jax.nn.softmax(e, axis=-1)
        h_prime = jnp.matmul(attention, h)
        return jax.nn.elu(h_prime)

    def _L1_ffn_ref(input_embeddings, router_w, w1, b1, w2, b2):
        import jax, jax.numpy as jnp
        import numpy as np
        NUM_EXPERTS = 8
        TOP_K = 2
        B, S, D = (8, 8192, 256)

        def _moe(tokens, router_w, w1, b1, w2, b2):
            N = tokens.shape[0]
            E = router_w.shape[0]
            logits = tokens.astype(jnp.float32) @ router_w.astype(jnp.float32).T
            probs = jax.nn.softmax(logits, axis=-1)
            rw, re = jax.lax.top_k(probs, TOP_K)
            if TOP_K > 1:
                rw = rw / jnp.maximum(rw.sum(-1, keepdims=True), 1e-12)
            rw = rw.astype(tokens.dtype)
            combine = jnp.zeros((N, E), tokens.dtype).at[jnp.arange(N)[:, None], re].set(rw)
            out = tokens
            for e in range(E):
                h = jax.nn.gelu(tokens @ w1[e] + b1[e], approximate=False)
                y = h @ w2[e] + b2[e]
                out = out + combine[:, e:e + 1] * y
            return out
        b, s, d = input_embeddings.shape
        tokens = input_embeddings.reshape(b * s, d)
        return _moe(tokens, router_w, w1, b1, w2, b2).reshape(b, s, d)

    def _gn(v, G=32, eps=1e-5):
        B_, H_, W_, C_ = v.shape
        g = v.reshape(B_, H_, W_, G, C_ // G)
        m = jnp.mean(g, axis=(1, 2, 4), keepdims=True)
        s = jnp.var(g, axis=(1, 2, 4), keepdims=True)
        return ((g - m) / jnp.sqrt(s + eps)).reshape(v.shape)

    def _ln_c(v, eps=1e-6):
        m = jnp.mean(v, axis=-1, keepdims=True)
        s = jnp.var(v, axis=-1, keepdims=True)
        return (v - m) / jnp.sqrt(s + eps)

    def _ln_t(v, eps=1e-5):
        m = jnp.mean(v, axis=-1, keepdims=True)
        s = jnp.var(v, axis=-1, keepdims=True)
        return (v - m) / jnp.sqrt(s + eps)

    def _to_tokens(v):
        B_, H_, W_, C_ = v.shape
        return v.reshape(B_, H_ * W_, C_)
    def _from_tokens(t, like):
        return t.reshape(like.shape)

    x = _L0_conv_ref(x, L0_conv_pe, L0_conv_ln_w, L0_conv_ln_b, L0_conv_in_proj, L0_conv_conv_w, L0_conv_conv_b, L0_conv_x_proj, L0_conv_dt_w, L0_conv_dt_b, L0_conv_A_log, L0_conv_Dp, L0_conv_out_proj)
    t = _to_tokens(x)
    t = t + _L1_attn_ref(_ln_t(t), L1_attn_W, L1_attn_a)
    t = t + _L1_ffn_ref(_ln_t(t), L1_ffn_router_w, L1_ffn_w1, L1_ffn_b1, L1_ffn_w2, L1_ffn_b2)
    x = _from_tokens(t, x)
    return x


_drawn_inputs = setup_inputs


def setup_inputs(seed=0):
    import zlib

    import numpy as np

    out = dict(_drawn_inputs(seed))
    spreads = {'L0_conv_ln_w': (1.0, 0.2),
     'L0_conv_ln_b': (0.0, 0.1),
     'L0_conv_conv_b': (0.0, 0.1),
     'L0_conv_Dp': (1.0, 0.2),
     'L1_ffn_b1': (0.0, 0.373),
     'L1_ffn_b2': (0.0, 0.1)}
    factors = {'L0_conv_x_proj': 8.0, 'L0_conv_dt_w': 8.0, 'L0_conv_dt_b': 8.0, 'L0_conv_A_log': 8.0}
    for name, (base, spread) in spreads.items():
        noise = np.random.default_rng([zlib.crc32(name.encode()), seed]).standard_normal(out[name].shape)
        drawn = base * np.exp(spread * noise) if base else spread * noise
        out[name] = jnp.asarray(drawn.astype(out[name].dtype))
    for name, factor in factors.items():
        out[name] = (out[name] * factor).astype(out[name].dtype)
    return out
```

```python
import concourse.bass as bass
from concourse import mybir
from contextlib import ExitStack

F32 = mybir.dt.float32
BF16 = mybir.dt.bfloat16
U32 = mybir.dt.uint32
ALU = mybir.AluOpType
ACT = mybir.ActivationFunctionType
AX = mybir.AxisListType
P = 128

NB, NO, NT, DM = 8, 12, 64, 256
SEQ = NO * NT
TOK = NB * SEQ
NL = 2
DI = 2 * DM
DS = 16
DCONV = 4
DTR = DM // 16
HALF = SEQ // 2
KC = DM // P
MC = DI // P
XPW = DTR + 2 * DS
NE = 8
CHUNKS = 2 * NB
STAGES = 4


class Sem:

    def __init__(self, sem, per):
        self.sem, self.per = sem, per

    def at(self, period, n):
        return (period + 1) * self.per + n


def wait_apart(eng, s, period, n, passed):
    eng.wait_ge(s.sem, s.at(period, n))
    eng.sem_inc(passed, 1)


def load_tokens(nc, x, pe, X, ident, eps5):
    TILES = TOK // P
    GROUP = 4
    with ExitStack() as ctx:
        raw = ctx.enter_context(nc.sbuf_tensor("raw_tokens", [P, GROUP, DM], F32))
        pos = ctx.enter_context(nc.sbuf_tensor("pos_tokens", [P, DM], F32))
        turned = [ctx.enter_context(nc.psum_tensor(f"turned{i}", [P, 512], F32)) for i in range(2)]
        sem = lambda n: ctx.enter_context(nc.semaphore(n))
        pos_loaded = sem("pos_loaded")
        raw_loaded = [sem(f"raw_loaded{i}") for i in range(GROUP)]
        pos_added = sem("pos_added")
        tile_turned = sem("tile_turned")
        tile_kept = sem("tile_kept")
        ident_zeroed = sem("ident_zeroed")
        ident_ready = sem("ident_ready")
        block = ctx.enter_context(nc.Block())
        xt = x.rearrange("b o t d -> (b o t) d").rearrange("(n p) d -> p n d", p=P)

        @block.sync
        def _(sp):
            for i in range(P // NT):
                sp.dma_start(pos[i * NT:(i + 1) * NT, :], pe).then_inc(pos_loaded, 16)
            with sp.Fori(0, TILES // GROUP) as g:
                for i in range(GROUP):
                    sp.wait_ge(tile_turned, g * GROUP + i + 1)
                    sp.dma_start(raw[:, i, :], xt[:, g * GROUP + i, :]).then_inc(raw_loaded[i], 16)

        @block.gpsimd
        def _(pool):
            nc.gpsimd.memset(ident[:, :], 0.0).then_inc(ident_zeroed, 1)
            nc.gpsimd.memset(eps5[:, :], 1e-5)
            pool.wait_ge(ident_zeroed, 1)
            nc.gpsimd.affine_select(out=ident[:, :], in_=ident[:, :], compare_op=ALU.not_equal, fill=1.0,
                                    base=0, pattern=[[-1, P]], channel_multiplier=1).then_inc(ident_ready, 1)

        @block.vector
        def _(dve):
            dve.wait_ge(pos_loaded, 16 * (P // NT))
            with dve.Fori(0, TILES // GROUP) as g:
                for i in range(GROUP):
                    dve.wait_ge(raw_loaded[i], g * 16 + 16)
                    nc.vector.tensor_tensor(raw[:, i, :], raw[:, i, :], pos[:, :], ALU.add).then_inc(pos_added, 1)

        @block.tensor
        def _(pe_):
            pe_.wait_ge(ident_ready, 1)
            pe_.sem_inc(tile_turned, GROUP)
            with pe_.Fori(0, TILES // GROUP) as g:
                for i in range(GROUP):
                    pe_.wait_ge(pos_added, g * GROUP + i + 1)
                    pe_.wait_ge(tile_kept, g * GROUP + i + 1)
                    for k in range(KC):
                        last = nc.tensor.transpose(turned[i % 2][:, k * P:(k + 1) * P],
                                                   raw[:, i, k * P:(k + 1) * P], ident[:, :])
                    last.then_inc(tile_turned, 1)

        @block.scalar
        def _(act):
            act.sem_inc(tile_kept, 2)
            xw = X[:, :, :].rearrange("p k (g n) -> p g k n", n=GROUP * P)
            with act.Fori(0, TILES // GROUP) as g:
                for i in range(GROUP):
                    act.wait_ge(tile_turned, g * GROUP + i + 1 + GROUP)
                    nc.scalar.copy(xw[:, g, :, i * P:(i + 1) * P],
                                   turned[i % 2][:, 0:KC * P].rearrange("p (k n) -> p k n", k=KC)
                                   ).then_inc(tile_kept, 1)


def mamba(nc, X, ident, eps5, w):
    with ExitStack() as ctx:
        def sb(name, shape, dt=F32):
            return ctx.enter_context(nc.sbuf_tensor(name, shape, dt))

        def sem(name, per):
            return Sem(ctx.enter_context(nc.semaphore(name)), per)

        w_in = sb("w_in", [P, KC, 2 * DI])
        w_out = sb("w_out", [P, MC, DM])
        w_bc = sb("w_bc", [P, MC, 6 * DS])
        w_dt = sb("w_dt", [P, MC, DTR])
        w_step = sb("w_step", [DTR, DI])
        taps = sb("taps", [P, MC, DCONV])
        conv_bias = sb("conv_bias", [P, MC])
        step_bias = sb("step_bias", [P, MC])
        skip = sb("skip", [P, MC])
        decay = sb("decay", [P, MC, DS])
        ln_w = sb("ln_w", [P, KC])
        ln_b = sb("ln_b", [P, KC])
        mean_w = sb("mean_w", [P, P])
        pick = sb("pick", [6 * DS, 2 * DS, P], BF16)

        xs = sb("xs", [P, KC, HALF])
        xin = sb("xin", [P, MC, DCONV - 1 + HALF])
        xc = sb("xc", [P, 2, MC, HALF])
        sz = sb("sz", [P, 2, MC, HALF])
        delta = sb("delta", [P, 2, MC, HALF])
        du = sb("du", [P, 2, MC, HALF])
        tmp = sb("tmp", [P, MC, HALF])
        dt_low = sb("dt_low", [DTR, HALF])
        bc_rest = sb("bc_rest", [6 * DS, HALF])
        bc_parts = sb("bc_parts", [6 * DS, 2, HALF], BF16)
        b_wide = sb("b_wide", [P, 2, HALF])
        dbx = sb("dbx", [P, 2, MC, HALF])
        hs = sb("hs", [P, 2, MC, HALF])
        hc = sb("hc", [P, 2, MC, HALF])
        carry = sb("carry", [P, DS, MC])
        yg = sb("yg", [P, MC, HALF])
        fo = sb("fo", [P, KC, HALF])
        fwd_in = sb("fwd_in", [P, KC, HALF])
        res_in = sb("res_in", [P, 2, KC, HALF])
        sq = sb("sq", [P, KC, HALF])
        rstd = sb("rstd", [P, HALF])

        fwd_dram = nc.dram_tensor("fwd_scratch", [P, CHUNKS, KC, HALF], F32, kind="Internal").ap()
        res_dram = nc.dram_tensor("res_scratch", [P, KC, TOK], F32, kind="Internal").ap()

        bank = lambda name: ctx.enter_context(nc.psum_tensor(name, [P, 512], F32))
        a_bank = [bank(f"a_bank{i}") for i in range(2)]
        y_all = ctx.enter_context(nc.psum_tensor("y_bank", [P, MC, 512], F32))
        c_bank = bank("c_bank")
        misc = bank("misc")

        ORDER = ([("in", m) for m in range(2 * MC)] + [("bc", 0), ("dt", 0)] + [("step", m) for m in range(MC)]
                 + [("b", s) for s in range(DS)] + [("out", k) for k in range(KC)] + [("mean", 0), ("var", 0)])
        USES = len(ORDER)
        USE = {what: n + 1 for n, what in enumerate(ORDER)}
        NW = 12

        weights_loaded = sem("weights_loaded", 16 * NW)
        decay_exp = sem("decay_exp", 1)
        decay_ready = sem("decay_ready", 1)
        misc_full = sem("misc_full", USES)
        misc_free = sem("misc_free", USES)
        x_picked = sem("x_picked", 1)
        halo_ready = sem("halo_ready", 1)
        conv_step = sem("conv_step", MC * DCONV)
        xpre_ready = sem("xpre_ready", 1)
        z_sig = sem("z_sig", 3)
        x_sig = sem("x_sig", 3)
        sz_ready = sem("sz_ready", 1)
        xc_ready = sem("xc_ready", 1)
        split_step = sem("split_step", 6)
        step_abs = sem("step_abs", 1)
        step_exp = sem("step_exp", 1)
        step_u = sem("step_u", 1)
        step_corr = sem("step_corr", 1)
        step_ln = sem("step_ln", 1)
        delta_step = sem("delta_step", 3)
        a_ready = sem("a_ready", DS * MC)
        scan_done = sem("scan_done", DS * MC)
        dbx_ready = sem("dbx_ready", DS)
        c_ready = sem("c_ready", DS)
        cmul_done = sem("cmul_done", DS)
        y_added = sem("y_added", DS)
        y_read = sem("y_read", MC)
        yg_ready = sem("yg_ready", 1)
        x_written = sem("x_written", 1)
        carry_saved = sem("carry_saved", DS)
        fwd_stored = sem("fwd_stored", 16)
        fwd_loaded = sem("fwd_loaded", 16)
        centred = sem("centred", 1)
        sq_ready = sem("sq_ready", 1)
        ln_var = sem("ln_var", 1)
        rstd_ready = sem("rstd_ready", 1)
        norm_step = sem("norm_step", 4)
        res_stored = sem("res_stored", 16)
        res_loaded = sem("res_loaded", 16)
        all_sems = [weights_loaded, decay_exp, decay_ready, misc_full, misc_free, x_picked, halo_ready, conv_step, xpre_ready,
                    z_sig, x_sig, sz_ready, xc_ready, split_step, step_abs, step_exp, step_u, step_corr, step_ln,
                    delta_step, a_ready, scan_done, dbx_ready, c_ready, cmul_done, y_added, y_read, yg_ready,
                    carry_saved, x_written, fwd_stored, fwd_loaded, centred, sq_ready, ln_var, rstd_ready, norm_step,
                    res_stored, res_loaded]
        ln_loaded = ctx.enter_context(nc.semaphore("ln_loaded"))
        ln_halved = ctx.enter_context(nc.semaphore("ln_halved"))
        halo_zeroed = ctx.enter_context(nc.semaphore("halo_zeroed"))
        passed = ctx.enter_context(nc.semaphore("waits_passed"))
        mean_w_set = ctx.enter_context(nc.semaphore("mean_w_set"))
        pick_zeroed = ctx.enter_context(nc.semaphore("pick_zeroed"))
        pick_set = ctx.enter_context(nc.semaphore("pick_set"))

        ctx.enter_context(nc.allow_non_contiguous_dma(reason="vectors of a few hundred values"))
        block = ctx.enter_context(nc.Block())

        def periods(l, st, b, half):
            blk = st // 2
            return (l * STAGES + st,
                    l * (STAGES * CHUNKS) + b * 2 + (st * CHUNKS + half),
                    l * (STAGES * NB) + b + st * NB,
                    l * (2 * CHUNKS) + b * 2 + (blk * CHUNKS + half),
                    l * CHUNKS + b * 2 + half)

        def half_of(t, b, nh):
            return t.rearrange("p k (b h n) -> p b h k n", b=NB, h=2)[:, b, nh]

        def pick_chunk(st, b, half):
            blk, back = divmod(st, 2)
            nh = 1 - half if back else half
            place = xs[:, :, ::-1] if back else xs[:, :, :]
            if blk == 0:
                return place, half_of(X[:, :, :], b, nh)
            return (place.rearrange("p k (t o) -> p k t o", o=NO),
                    X[:, :, :].rearrange("p k (b o h t) -> p b h k t o", b=NB, o=NO, h=2)[:, b, nh])

        def wide(ap):
            return ap.unsqueeze(1).broadcast_to([P, MC, HALF])

        def wait(eng, s, period, n):
            eng.wait_ge(s.sem, s.at(period, n))

        @block.sync
        def _(sp):
            for s in all_sems:
                sp.sem_inc(s.sem, s.per)
            sp.dma_start(ln_w[:, :], w["ln_w"].rearrange("(k p) -> p k", p=P)).then_inc(ln_loaded, 16)
            sp.dma_start(ln_b[:, :], w["ln_b"].rearrange("(k p) -> p k", p=P)).then_inc(ln_loaded, 16)

            def stage(l, st):
                blk, back = divmod(st, 2)
                sg, g0, _, _, _ = periods(l, st, 0, 0)
                wait_apart(sp, misc_free, g0, 0, passed)
                wait_apart(sp, scan_done, g0, 0, passed)
                at = lambda name: w[name][l, blk, back]
                loads = [
                    (w_in[:, :, :], at("in_proj").rearrange("(k p) n -> p k n", p=P)),
                    (w_out[:, :, :], at("out_proj").rearrange("(k p) n -> p k n", p=P)),
                    (w_dt[:, :, :], at("x_proj").rearrange("(k p) n -> p k n", p=P)[:, :, 0:DTR]),
                    (w_step[:, :], at("dt_w")),
                    (taps[:, :, :], at("conv_w").rearrange("(k p) n -> p k n", p=P)),
                    (conv_bias[:, :], at("conv_b").rearrange("(k p) -> p k", p=P)),
                    (step_bias[:, :], at("dt_b").rearrange("(k p) -> p k", p=P)),
                    (skip[:, :], at("Dp").rearrange("(k p) -> p k", p=P)),
                    (decay[:, :, :], at("A_log").rearrange("(k p) n -> p k n", p=P)),
                ] + [(w_bc[:, :, i * 2 * DS:(i + 1) * 2 * DS],
                      at("x_proj").rearrange("(k p) n -> p k n", p=P)[:, :, DTR:XPW]) for i in range(3)]
                assert len(loads) == NW
                for dst, src in loads:
                    sp.dma_start(dst, src).then_inc(weights_loaded.sem, 16)

                with sp.Fori(0, NB) as b:
                    for half in range(2):
                        _, g, _, gd, gb = periods(l, st, b, half)
                        nh = 1 - half if back else half
                        here = fwd_dram.rearrange("p (b h) k n -> p b h k n", h=2)[:, b, nh]
                        if not back:
                            wait_apart(sp, misc_free, g, USES, passed)
                            sp.dma_start(here, fo[:, :, :]).then_inc(fwd_stored.sem, 16)
                            continue
                        if half == 0:
                            wait_apart(sp, fwd_stored, l * (2 * CHUNKS) + (blk + 1) * CHUNKS, 0, passed)
                        wait_apart(sp, norm_step, gd, 0, passed)
                        sp.dma_start(fwd_in[:, :, :], here).then_inc(fwd_loaded.sem, 16)
                        if blk == 0:
                            wait_apart(sp, norm_step, gd, 4, passed)
                            sp.dma_start(half_of(res_dram, b, nh), fo[:, :, :]).then_inc(res_stored.sem, 16)
                        else:
                            if half == 0:
                                wait_apart(sp, res_stored, (l + 1) * CHUNKS, 0, passed)
                                wait_apart(sp, x_written, l * NB + b, 0, passed)
                            sp.dma_start(res_in[:, half], half_of(res_dram, b, nh)).then_inc(res_loaded.sem, 16)

            with sp.Fori(0, NL) as l:
                for st in range(STAGES):
                    stage(l, st)

        @block.gpsimd
        def _(pool):
            nc.gpsimd.memset(mean_w[:, :], 1.0 / DM).then_inc(mean_w_set, 1)
            nc.gpsimd.memset(pick[:, :, :], 0.0).then_inc(pick_zeroed, 1)
            for part in range(3):
                pool.wait_ge(pick_zeroed, part + 1)
                last = nc.gpsimd.affine_select(out=pick[:, :, :], in_=pick[:, :, :], compare_op=ALU.not_equal,
                                               fill=1.0, base=-2 * DS * part, pattern=[[-1, 2 * DS], [0, P]],
                                               channel_multiplier=1)
                last.then_inc(pick_zeroed if part < 2 else pick_set, 1)
            pool.wait_ge(ln_loaded, 32)
            nc.gpsimd.tensor_scalar(ln_w[:, :], ln_w[:, :], 0.5, 1.0, ALU.mult, ALU.mult).then_inc(ln_halved, 1)
            nc.gpsimd.tensor_scalar(ln_b[:, :], ln_b[:, :], 0.5, 1.0, ALU.mult, ALU.mult).then_inc(ln_halved, 1)

            def chunk(l, st, b, half):
                _, g, _, _, _ = periods(l, st, b, half)
                wait_apart(pool, misc_full, g, 0, passed)
                nc.gpsimd.tensor_copy(*pick_chunk(st, b, half)).then_inc(x_picked.sem, 1)
                wait(pool, z_sig, g, 3)
                nc.gpsimd.tensor_tensor(sz[:, half], sz[:, half], tmp[:, :, :], ALU.mult).then_inc(sz_ready.sem, 1)
                wait(pool, x_sig, g, 3)
                nc.gpsimd.tensor_tensor(xc[:, half], xc[:, half], tmp[:, :, :], ALU.mult).then_inc(xc_ready.sem, 1)
                wait(pool, step_ln, g, 1)
                nc.gpsimd.tensor_tensor(delta[:, half], delta[:, half], du[:, half], ALU.subtract
                                        ).then_inc(delta_step.sem, 1)
                wait(pool, delta_step, g, 1)
                nc.gpsimd.tensor_tensor(delta[:, half], delta[:, half], tmp[:, :, :], ALU.add
                                        ).then_inc(delta_step.sem, 1)
                wait(pool, delta_step, g, 2)
                wait(pool, xc_ready, g, 1)
                nc.gpsimd.tensor_tensor(du[:, half], delta[:, half], xc[:, half], ALU.mult).then_inc(delta_step.sem, 1)
                wait(pool, delta_step, g, 3)
                for s in range(DS):
                    wait(pool, misc_free, g, USE["b", s])
                    wait(pool, scan_done, g, MC * (s - 1))
                    nc.gpsimd.tensor_tensor(dbx[:, s % 2], du[:, half], wide(b_wide[:, s % 2, :]), ALU.mult
                                            ).then_inc(dbx_ready.sem, 1)

            with pool.Fori(0, NL) as l:
                for st in range(STAGES):
                    gd = periods(l, st, 0, 0)[3]
                    wait_apart(pool, norm_step, gd, 0, passed)
                    if st == 0:
                        wait_apart(pool, x_written, l * NB, 0, passed)
                    with pool.Fori(0, NB) as b:
                        for half in range(2):
                            chunk(l, st, b, half)

        @block.tensor
        def _(pe):
            pe.wait_ge(mean_w_set, 1)
            pe.wait_ge(pick_set, 1)

            def use(g, what):
                wait(pe, misc_free, g, USE[what] - 1)

            def chunk(l, st, b, half):
                back = st % 2
                _, g, _, _, _ = periods(l, st, b, half)
                wait(pe, x_picked, g, 1)
                for m in range(2 * MC):
                    use(g, ("in", m))
                    for k in range(KC):
                        last = nc.tensor.matmul(misc[:, 0:HALF], w_in[:, k, m * P:(m + 1) * P], xs[:, k, :],
                                                start=(k == 0), stop=(k == KC - 1))
                    last.then_inc(misc_full.sem, 1)
                wait(pe, xc_ready, g, 1)
                for what, weight, rows in ((("bc", 0), w_bc, 6 * DS), (("dt", 0), w_dt, DTR)):
                    use(g, what)
                    for k in range(MC):
                        last = nc.tensor.matmul(misc[0:rows, 0:HALF], weight[:, k, :], xc[:, half, k, :],
                                                start=(k == 0), stop=(k == MC - 1))
                    last.then_inc(misc_full.sem, 1)
                for m in range(MC):
                    use(g, ("step", m))
                    nc.tensor.matmul(misc[:, 0:HALF], w_step[:, m * P:(m + 1) * P], dt_low[:, :],
                                     start=True, stop=True).then_inc(misc_full.sem, 1)

                def add_states(s):
                    wait(pe, cmul_done, g, s + 1)
                    if s == 0:
                        wait(pe, y_read, g, 0)
                    for c in range(MC):
                        last = nc.tensor.matmul(y_all[:, c, 0:HALF], ident[:, :], hc[:, s % 2, c, :],
                                                start=(s == 0), stop=(s == DS - 1))
                    last.then_inc(y_added.sem, 1)

                wait(pe, split_step, g, 6)
                for s in range(DS):
                    use(g, ("b", s))
                    nc.tensor.matmul(misc[:, 0:HALF], pick[:, s, :], bc_parts[:, half, :],
                                     start=True, stop=True).then_inc(misc_full.sem, 1)
                    wait(pe, cmul_done, g, s)
                    nc.tensor.matmul(c_bank[:, 0:HALF], pick[:, DS + s, :], bc_parts[:, half, :],
                                     start=True, stop=True).then_inc(c_ready.sem, 1)
                    if s > 0:
                        add_states(s - 1)
                add_states(DS - 1)

                wait(pe, yg_ready, g, 1)
                for k in range(KC):
                    use(g, ("out", k))
                    for m in range(MC):
                        ys = yg[:, m, ::-1] if back else yg[:, m, :]
                        last = nc.tensor.matmul(misc[:, 0:HALF], w_out[:, m, k * P:(k + 1) * P], ys,
                                                start=(m == 0), stop=(m == MC - 1))
                    last.then_inc(misc_full.sem, 1 if back or k < KC - 1 else 3)
                if back:
                    for what, src in (("mean", fo), ("var", sq)):
                        use(g, (what, 0))
                        if what == "var":
                            wait(pe, sq_ready, periods(l, st, b, half)[3], 1)
                        for k in range(KC):
                            last = nc.tensor.matmul(misc[:, 0:HALF], mean_w[:, :], src[:, k, :],
                                                    start=(k == 0), stop=(k == KC - 1))
                        last.then_inc(misc_full.sem, 1)

            with pe.Fori(0, NL) as l:
                for st in range(STAGES):
                    sg = periods(l, st, 0, 0)[0]
                    wait_apart(pe, weights_loaded, sg, 16 * NW, passed)
                    with pe.Fori(0, NB) as b:
                        for half in range(2):
                            chunk(l, st, b, half)

        @block.scalar
        def _(act):
            nc.scalar.preload_act_table_set("natural_log_exp_and_others")

            def sigmoid(src, s, g):
                nc.scalar.activation(tmp[:, :, :], src, ACT.Exp, scale=-1.0).then_inc(s.sem, 1)
                wait(act, s, g, 1)
                nc.scalar.activation(tmp[:, :, :], tmp[:, :, :], ACT.Ln, bias=1.0).then_inc(s.sem, 1)
                wait(act, s, g, 2)
                nc.scalar.activation(tmp[:, :, :], tmp[:, :, :], ACT.Exp, scale=-1.0).then_inc(s.sem, 1)

            def chunk(l, st, b, half):
                back = st % 2
                _, g, _, gd, _ = periods(l, st, b, half)
                wait(act, halo_ready, g, 0)
                for m in range(MC):
                    wait(act, misc_full, g, USE["in", m])
                    nc.scalar.copy(xin[:, m, DCONV - 1:], misc[:, 0:HALF]).then_inc(misc_free.sem, 1)
                wait(act, misc_free, g, USE["in", 2 * MC - 1])
                wait(act, delta_step, g, 0)
                sigmoid(sz[:, half], z_sig, g)
                wait(act, xpre_ready, g, 1)
                wait(act, sz_ready, g, 1)
                sigmoid(xc[:, half], x_sig, g)
                wait(act, misc_full, g, USE["dt", 0])
                nc.scalar.copy(dt_low[:, :], misc[0:DTR, 0:HALF]).then_inc(misc_free.sem, 1)
                wait(act, xc_ready, g, 1)
                for m in range(MC):
                    wait(act, misc_full, g, USE["step", m])
                    pre = nc.scalar.activation(delta[:, half, m, :], misc[:, 0:HALF], ACT.Abs,
                                               bias=step_bias[:, m:m + 1])
                    if m == MC - 1:
                        pre.then_inc(step_abs.sem, 1)
                    nc.scalar.activation(tmp[:, m, :], misc[:, 0:HALF], ACT.Relu,
                                         bias=step_bias[:, m:m + 1]).then_inc(misc_free.sem, 1)
                wait(act, step_abs, g, 1)
                nc.scalar.activation(du[:, half], delta[:, half], ACT.Exp, scale=-1.0).then_inc(step_exp.sem, 1)
                wait(act, step_exp, g, 1)
                nc.scalar.activation(delta[:, half], du[:, half], ACT.Identity, bias=1.0).then_inc(step_u.sem, 1)
                wait(act, step_u, g, 1)
                wait(act, step_corr, g, 1)
                nc.scalar.activation(delta[:, half], delta[:, half], ACT.Ln).then_inc(step_ln.sem, 1)

                def widen_b(s):
                    wait(act, misc_full, g, USE["b", s])
                    wait(act, dbx_ready, g, s - 1)
                    nc.scalar.copy(b_wide[:, s % 2, :], misc[:, 0:HALF]).then_inc(misc_free.sem, 1)

                wait(act, delta_step, g, 2)
                widen_b(0)
                for s in range(DS):
                    for c in range(MC):
                        n = s * MC + c
                        wait(act, scan_done, g, n - 1)
                        nc.scalar.activation(a_bank[n % 2][:, 0:HALF], delta[:, half, c, :], ACT.Exp,
                                             scale=decay[:, c, s:s + 1]).then_inc(a_ready.sem, 1)
                        if c == 1 and s < DS - 1:
                            widen_b(s + 1)
                if not back:
                    wait(act, fwd_stored, gd, 0)
                    for k in range(KC):
                        wait(act, misc_full, g, USE["out", k])
                        nc.scalar.copy(fo[:, k, :], misc[:, 0:HALF]
                                       ).then_inc(misc_free.sem, 1 if k < KC - 1 else 3)
                else:
                    wait(act, misc_free, g, USE["mean", 0])
                    wait(act, centred, gd, 1)
                    nc.scalar.activation(sq[:, :, :], fo[:, :, :], ACT.Square).then_inc(sq_ready.sem, 1)
                    wait(act, misc_full, g, USE["var", 0])
                    nc.scalar.activation(rstd[:, :], misc[:, 0:HALF], ACT.Ln, bias=eps5[:, 0:1]
                                         ).then_inc(misc_free.sem, 1)
                    wait(act, misc_free, g, USE["var", 0])
                    nc.scalar.activation(rstd[:, :], rstd[:, :], ACT.Exp, scale=-0.5).then_inc(rstd_ready.sem, 1)

            with act.Fori(0, NL) as l:
                for st in range(STAGES):
                    sg, _, _, gd, _ = periods(l, st, 0, 0)
                    wait(act, weights_loaded, sg, 16 * NW)
                    wait(act, norm_step, gd, 0)
                    if st == 2:
                        wait(act, res_stored, (l + 1) * CHUNKS, 0)
                    nc.scalar.activation(decay[:, :, :], decay[:, :, :], ACT.Exp).then_inc(decay_exp.sem, 1)
                    wait(act, decay_ready, sg, 1)
                    with act.Fori(0, NB) as b:
                        for half in range(2):
                            chunk(l, st, b, half)

        @block.vector
        def _(dve):
            LOW = -44.0
            nc.vector.memset(xin[:, :, 0:DCONV - 1], 0.0).then_inc(halo_zeroed, 1)
            dve.wait_ge(halo_zeroed, 1)
            dve.wait_ge(ln_halved, 2)

            def chunk(l, st, b, half):
                blk, back = divmod(st, 2)
                _, g, gc, gd, gb = periods(l, st, b, half)
                for m in range(MC):
                    wait(dve, misc_full, g, USE["in", MC + m])
                    nc.vector.tensor_scalar(sz[:, half, m, :], misc[:, 0:HALF], LOW, None, ALU.max
                                            ).then_inc(misc_free.sem, 1)
                wait(dve, misc_free, g, USE["in", MC - 1])
                wait(dve, halo_ready, g, 0)
                for tap in range(DCONV):
                    for m in range(MC):
                        src = xin[:, m, tap:tap + HALF]
                        if tap == 0:
                            ins = nc.vector.tensor_scalar(xc[:, half, m, :], src, taps[:, m, 0:1],
                                                          conv_bias[:, m:m + 1], ALU.mult, ALU.add)
                        else:
                            wait(dve, conv_step, g, (tap - 1) * MC + m + 1)
                            ins = nc.vector.scalar_tensor_tensor(out=xc[:, half, m, :], in0=src,
                                                                 scalar=taps[:, m, tap:tap + 1],
                                                                 in1=xc[:, half, m, :], op0=ALU.mult, op1=ALU.add)
                        ins.then_inc(conv_step.sem, 1)
                wait(dve, conv_step, g, MC * DCONV)
                nc.vector.tensor_scalar(xc[:, half], xc[:, half], LOW, None, ALU.max).then_inc(xpre_ready.sem, 1)
                if half == 0:
                    nc.vector.tensor_copy(xin[:, :, 0:DCONV - 1], xin[:, :, HALF:HALF + DCONV - 1]
                                          ).then_inc(halo_ready.sem, 1)
                else:
                    nc.vector.memset(xin[:, :, 0:DCONV - 1], 0.0).then_inc(halo_ready.sem, 1)
                parts = bc_parts[:, half, :]
                wait(dve, misc_full, g, USE["bc", 0])
                nc.vector.tensor_copy(bc_rest[:, :], misc[0:6 * DS, 0:HALF]).then_inc(misc_free.sem, 1)
                wait(dve, misc_free, g, USE["bc", 0])
                nc.vector.tensor_copy(parts, bc_rest[:, :]).then_inc(split_step.sem, 1)
                wait(dve, split_step, g, 1)
                nc.vector.tensor_tensor(bc_rest[:, :], bc_rest[:, :], parts, ALU.subtract).then_inc(split_step.sem, 1)
                wait(dve, split_step, g, 2)
                for part in (1, 2):
                    rows = slice(part * 2 * DS, (part + 1) * 2 * DS)
                    nc.vector.tensor_copy(parts[rows], bc_rest[rows, :]).then_inc(split_step.sem, 1)
                wait(dve, split_step, g, 4)
                nc.vector.tensor_tensor(bc_rest[rows, :], bc_rest[rows, :], parts[rows], ALU.subtract
                                        ).then_inc(split_step.sem, 1)
                wait(dve, split_step, g, 5)
                nc.vector.tensor_copy(parts[rows], bc_rest[rows, :]).then_inc(split_step.sem, 1)
                wait(dve, step_u, g, 1)
                nc.vector.scalar_tensor_tensor(out=du[:, half], in0=delta[:, half], scalar=1.0, in1=du[:, half],
                                               op0=ALU.subtract, op1=ALU.subtract).then_inc(step_corr.sem, 1)

                def times_c(s):
                    wait(dve, c_ready, g, s + 1)
                    wait(dve, scan_done, g, MC * (s + 1))
                    wait(dve, y_added, g, s - 1)
                    nc.vector.tensor_tensor(hc[:, s % 2], hs[:, s % 2], wide(c_bank[:, 0:HALF]), ALU.mult
                                            ).then_inc(cmul_done.sem, 1)
                    if half == 0:
                        nc.vector.tensor_copy(carry[:, s, :], hs[:, s % 2, :, HALF - 1]
                                              ).then_inc(carry_saved.sem, 1)

                for s in range(DS):
                    wait(dve, dbx_ready, g, s + 1)
                    if half == 1 and s == 0:
                        wait(dve, carry_saved, gc, DS)
                    wait(dve, cmul_done, g, s - 1)
                    for c in range(MC):
                        n = s * MC + c
                        wait(dve, a_ready, g, n + 1)
                        nc.vector.tensor_tensor_scan(hs[:, s % 2, c, :], a_bank[n % 2][:, 0:HALF],
                                                     dbx[:, s % 2, c, :], 0.0 if half == 0 else carry[:, s, c:c + 1],
                                                     ALU.mult, ALU.add).then_inc(scan_done.sem, 1)
                        if c == 0 and s > 0:
                            times_c(s - 1)
                times_c(DS - 1)

                wait(dve, y_added, g, DS)
                wait(dve, misc_full, g, 0)
                for m in range(MC):
                    nc.vector.scalar_tensor_tensor(out=yg[:, m, :], in0=xc[:, half, m, :], scalar=skip[:, m:m + 1],
                                                   in1=y_all[:, m, 0:HALF], op0=ALU.mult, op1=ALU.add
                                                   ).then_inc(y_read.sem, 1)
                wait(dve, y_read, g, MC)
                wait(dve, sz_ready, g, 1)
                nc.vector.tensor_tensor(yg[:, :, :], yg[:, :, :], sz[:, half], ALU.mult).then_inc(yg_ready.sem, 1)
                if not back:
                    return
                wait(dve, fwd_loaded, gd, 16)
                if blk == 0:
                    wait(dve, res_stored, gb, 0)
                wait(dve, fwd_stored, l * (2 * CHUNKS) + (blk + 1) * CHUNKS, 0)
                for k in range(KC):
                    wait(dve, misc_full, g, USE["out", k])
                    nc.vector.tensor_tensor(fo[:, k, :], misc[:, 0:HALF], fwd_in[:, k, :], ALU.add
                                            ).then_inc(misc_free.sem, 1)
                wait(dve, misc_full, g, USE["mean", 0])
                for k in range(KC):
                    nc.vector.tensor_tensor(fo[:, k, :], fo[:, k, :], misc[:, 0:HALF], ALU.subtract
                                            ).then_inc(centred.sem if k == 0 else misc_free.sem, 1)
                wait(dve, rstd_ready, gd, 1)
                wait(dve, misc_free, g, USE["mean", 0])
                wait(dve, sq_ready, gd, 1)
                nc.vector.tensor_tensor(fo[:, :, :], fo[:, :, :],
                                        rstd[:, :].unsqueeze(1).broadcast_to([P, KC, HALF]), ALU.mult
                                        ).then_inc(norm_step.sem, 1)
                wait(dve, norm_step, gd, 1)
                for k in range(KC):
                    nc.vector.tensor_scalar(fo[:, k, :], fo[:, k, :], ln_w[:, k:k + 1], ln_b[:, k:k + 1],
                                            ALU.mult, ALU.add).then_inc(norm_step.sem, 1)
                wait(dve, norm_step, gd, 3)
                nh = 1 - half
                if blk == 0:
                    nc.vector.tensor_tensor(fo[:, :, :], fo[:, :, :], half_of(X[:, :, :], b, nh), ALU.add
                                            ).then_inc(norm_step.sem, 1)
                    return
                wait(dve, res_loaded, gb, 16)
                to = res_in[:, 0] if half == 0 else half_of(X[:, :, :], b, nh)
                nc.vector.tensor_tensor(to, fo[:, :, :], res_in[:, half], ALU.add).then_inc(norm_step.sem, 1)
                if half == 1:
                    wait(dve, norm_step, gd, 0)
                    nc.vector.tensor_copy(half_of(X[:, :, :], b, half), res_in[:, 0]).then_inc(x_written.sem, 1)

            with dve.Fori(0, NL) as l:
                for st in range(STAGES):
                    sg = periods(l, st, 0, 0)[0]
                    wait(dve, weights_loaded, sg, 16 * NW)
                    wait(dve, decay_exp, sg, 1)
                    nc.vector.tensor_scalar(decay[:, :, :], decay[:, :, :], -1.0, None, ALU.mult
                                            ).then_inc(decay_ready.sem, 1)
                    with dve.Fori(0, NB) as b:
                        for half in range(2):
                            chunk(l, st, b, half)


def attention(nc, X, ident, eps5, w):
    KT = SEQ // P
    with ExitStack() as ctx:
        def sb(name, shape, dt=F32):
            return ctx.enter_context(nc.sbuf_tensor(name, shape, dt))

        def sem(name, per=1):
            return Sem(ctx.enter_context(nc.semaphore(name)), per)

        mean_w = sb("attn_mean_w", [P, P])
        ones = sb("ones", [P, P])
        w_h = sb("w_h", [P, KC, DM + 1])
        w_t = sb("w_t", [P, KC, DM])
        a_cols = sb("a_cols", [P, 2 * KC])
        wa = sb("wa", [P, 2, KC, P])
        z = sb("z", [P, KC, 2, HALF])
        sq = sb("attn_sq", [P, KC, 2, HALF])
        rstd = sb("attn_rstd", [P, 2, HALF])
        h_sb = sb("h_sb", [P, KT, DM + 1])
        f2_max = sb("f2_max", [P, 1])
        row_max = sb("row_max", [P, 2, HALF])
        score = sb("score", [P, 2, 2, HALF])
        prob = sb("prob", [P, 2, 2, HALF])
        rden = sb("rden", [P, 2, HALF])
        hp = sb("hp", [P, KC, 2, HALF])
        neg = sb("neg", [P, KC, 2, HALF])
        bank4 = ctx.enter_context(nc.psum_tensor("out_banks", [P, KC, 2, 512], F32))
        f1_bank = ctx.enter_context(nc.psum_tensor("f1_bank", [P, 2, 512], F32))
        den_bank = ctx.enter_context(nc.psum_tensor("den_bank", [P, 2, 512], F32))
        f1, den, outp = f1_bank[:, :, 0:HALF], den_bank[:, :, 0:HALF], bank4[:, :, :, 0:HALF]
        h_bank = [bank4[:, 0, 0, 0:DM + 1], bank4[:, 0, 1, 0:DM + 1]]

        loaded = ctx.enter_context(nc.semaphore("attn_loaded"))
        consts_set = ctx.enter_context(nc.semaphore("consts_set"))
        w_turned = ctx.enter_context(nc.semaphore("w_turned"))
        w_t_kept = ctx.enter_context(nc.semaphore("w_t_kept"))
        wa_made = ctx.enter_context(nc.semaphore("wa_made"))
        wa_kept = ctx.enter_context(nc.semaphore("wa_kept"))
        mean_made = sem("mean_made")
        centred = sem("attn_centred", 2)
        squared = sem("squared")
        var_made = sem("var_made")
        rstd_step = sem("rstd_step", 2)
        z_ready = sem("z_ready")
        h_made = sem("h_made", KT)
        h_kept = sem("h_kept", KT)
        f_made = sem("f_made")
        max_step = sem("max_step", 3)
        score_step = sem("score_step", 3 * KT)
        prob_ready = sem("prob_ready", KT)
        prob_used = sem("prob_used", KT)
        rden_ready = sem("rden_ready")
        hp_step = sem("hp_step", 3)
        neg_exp = sem("neg_exp")
        x_added = sem("x_added", 2)
        sems = [mean_made, centred, squared, var_made, rstd_step, z_ready, h_made, h_kept, f_made, max_step,
                score_step, prob_ready, prob_used, rden_ready, hp_step, neg_exp, x_added]
        ctx.enter_context(nc.allow_non_contiguous_dma(reason="vectors of a few hundred values"))
        block = ctx.enter_context(nc.Block())

        def wait(eng, s, b, n):
            eng.wait_ge(s.sem, s.at(b, n))

        def tokens(b):
            return X[:, :, :].rearrange("p k (b h n) -> p b k h n", b=NB, h=2)[:, b]

        def each_block(ap):
            return ap.unsqueeze(1).broadcast_to([P, KC, 2, HALF])

        @block.sync
        def _(sp):
            for s in sems:
                sp.sem_inc(s.sem, s.per)
            sp.dma_start(w_h[:, :, 0:DM], w["W"].rearrange("(k p) n -> p k n", p=P)).then_inc(loaded, 16)
            sp.dma_start(a_cols[:, :], w["a"].rearrange("(c p) n -> p (c n)", p=P)).then_inc(loaded, 16)
            sp.wait_ge(loaded, 32)

        @block.gpsimd
        def _(pool):
            nc.gpsimd.memset(mean_w[:, :], 1.0 / DM).then_inc(consts_set, 1)
            nc.gpsimd.memset(ones[:, :], 1.0).then_inc(consts_set, 1)

        @block.tensor
        def _(pe):
            pe.wait_ge(consts_set, 2)
            pe.wait_ge(loaded, 32)
            for k in range(KC):
                for o in range(KC):
                    last = nc.tensor.transpose(den_bank[:, o, k * P:(k + 1) * P], w_h[:, k, o * P:(o + 1) * P],
                                               ident[:, :])
            last.then_inc(w_turned, 1)
            pe.wait_ge(w_t_kept, 1)
            for v in range(2):
                for k in range(KC):
                    for o in range(KC):
                        last = nc.tensor.matmul(f1_bank[:, v, k * P:(k + 1) * P], w_t[:, o, k * P:(k + 1) * P],
                                                a_cols[:, v * KC + o:v * KC + o + 1].broadcast_to([P, P]),
                                                start=(o == 0), stop=(o == KC - 1))
            last.then_inc(wa_made, 1)
            pe.wait_ge(wa_kept, 2)

            with pe.Fori(0, NB) as b:
                t = tokens(b)

                def over_features(dst, weight, src):
                    for h in range(2):
                        for k in range(KC):
                            last = nc.tensor.matmul(dst[:, h, 0:HALF], weight(k), src[:, k, h],
                                                    start=(k == 0), stop=(k == KC - 1))
                    return last

                wait(pe, rden_ready, b, 0)
                over_features(den_bank, lambda k: mean_w[:, :], t).then_inc(mean_made.sem, 1)
                wait(pe, squared, b, 1)
                wait(pe, centred, b, 2)
                over_features(den_bank, lambda k: mean_w[:, :], sq).then_inc(var_made.sem, 1)
                wait(pe, z_ready, b, 1)
                wait(pe, hp_step, b, 0)
                for j in range(KT):
                    if j >= 2:
                        wait(pe, h_kept, b, j - 1)
                    zj = z[:, :, :, :].rearrange("p k h n -> p k (h n)")
                    for k in range(KC):
                        last = nc.tensor.matmul(h_bank[j % 2], zj[:, k, j * P:(j + 1) * P], w_h[:, k, :],
                                                start=(k == 0), stop=(k == KC - 1))
                    last.then_inc(h_made.sem, 1)
                wait(pe, rstd_step, b, 2)
                wait(pe, score_step, b, 0)
                over_features(f1_bank, lambda k: wa[:, 0, k, :], z)
                over_features(den_bank, lambda k: wa[:, 1, k, :], z).then_inc(f_made.sem, 1)
                wait(pe, h_kept, b, KT)
                wait(pe, max_step, b, 1)
                for j in range(KT):
                    wait(pe, prob_ready, b, j + 1)
                    for h in range(2):
                        ph = prob[:, j % 2, h]
                        nc.tensor.matmul(den_bank[:, h, 0:HALF], ones[:, :], ph, start=(j == 0), stop=(j == KT - 1))
                        for k in range(KC):
                            last = nc.tensor.matmul(bank4[:, k, h, 0:HALF], h_sb[:, j, k * P:(k + 1) * P], ph,
                                                    start=(j == 0), stop=(j == KT - 1))
                    last.then_inc(prob_used.sem, 1)

        @block.scalar
        def _(act):
            nc.scalar.preload_act_table_set("natural_log_exp_and_others")
            act.wait_ge(w_turned, 1)
            nc.scalar.copy(w_t[:, :, :], den_bank[:, :, 0:DM]).then_inc(w_t_kept, 1)
            act.wait_ge(wa_made, 1)
            nc.scalar.copy(wa[:, :, :, :], f1_bank[:, :, 0:KC * P].rearrange("p v (k n) -> p v k n", k=KC)
                           ).then_inc(wa_kept, 1)
            act.wait_ge(wa_kept, 1)
            nc.scalar.copy(w_h[:, :, DM], wa[:, 1, :, 0]).then_inc(wa_kept, 1)
            with act.Fori(0, NB) as b:
                wait(act, centred, b, 2)
                nc.scalar.activation(sq[:, :, :, :], z[:, :, :, :], ACT.Square).then_inc(squared.sem, 1)
                wait(act, var_made, b, 1)
                nc.scalar.activation(rstd[:, :, :], den, ACT.Ln, bias=eps5[:, 0:1]).then_inc(rstd_step.sem, 1)
                wait(act, rstd_step, b, 1)
                nc.scalar.activation(rstd[:, :, :], rstd[:, :, :], ACT.Exp, scale=-0.5).then_inc(rstd_step.sem, 1)
                wait(act, prob_used, b, 0)
                for j in range(KT):
                    wait(act, h_made, b, j + 1)
                    nc.scalar.copy(h_sb[:, j, :], h_bank[j % 2]).then_inc(h_kept.sem, 1)
                for j in range(KT):
                    wait(act, score_step, b, 3 * j + 3)
                    wait(act, prob_used, b, j - 1)
                    nc.scalar.activation(prob[:, j % 2], score[:, j % 2], ACT.Exp).then_inc(prob_ready.sem, 1)
                wait(act, hp_step, b, 2)
                nc.scalar.activation(neg[:, :, :, :], neg[:, :, :, :], ACT.Exp).then_inc(neg_exp.sem, 1)

        @block.vector
        def _(dve):
            with dve.Fori(0, NB) as b:
                t = tokens(b)
                wait(dve, mean_made, b, 1)
                for h in range(2):
                    nc.vector.tensor_tensor(z[:, :, h], t[:, :, h],
                                            den_bank[:, h, 0:HALF].unsqueeze(1).broadcast_to([P, KC, HALF]),
                                            ALU.subtract).then_inc(centred.sem, 1)
                wait(dve, rstd_step, b, 2)
                wait(dve, squared, b, 1)
                nc.vector.tensor_tensor(z[:, :, :, :], z[:, :, :, :], each_block(rstd[:, :, :]), ALU.mult
                                        ).then_inc(z_ready.sem, 1)
                wait(dve, f_made, b, 1)
                nc.vector.tensor_reduce(f2_max[:, :], den, AX.XY, ALU.max).then_inc(max_step.sem, 1)
                wait(dve, max_step, b, 1)
                nc.vector.tensor_scalar(row_max[:, :, :], f1, f2_max[:, 0:1], None, ALU.add).then_inc(max_step.sem, 1)
                wait(dve, max_step, b, 2)
                nc.vector.scalar_tensor_tensor(out=row_max[:, :, :], in0=row_max[:, :, :], scalar=0.01,
                                               in1=row_max[:, :, :], op0=ALU.mult, op1=ALU.max
                                               ).then_inc(max_step.sem, 1)
                wait(dve, max_step, b, 3)
                wait(dve, h_kept, b, KT)
                for j in range(KT):
                    sc = score[:, j % 2]
                    wait(dve, prob_ready, b, j - 1)
                    nc.vector.tensor_scalar(sc, f1, h_sb[:, j, DM:DM + 1], None, ALU.add).then_inc(score_step.sem, 1)
                    wait(dve, score_step, b, 3 * j + 1)
                    nc.vector.scalar_tensor_tensor(out=sc, in0=sc, scalar=0.01, in1=sc, op0=ALU.mult, op1=ALU.max
                                                   ).then_inc(score_step.sem, 1)
                    wait(dve, score_step, b, 3 * j + 2)
                    nc.vector.tensor_tensor(sc, sc, row_max[:, :, :], ALU.subtract).then_inc(score_step.sem, 1)
                wait(dve, prob_used, b, KT)
                nc.vector.reciprocal(rden[:, :, :], den).then_inc(rden_ready.sem, 1)
                wait(dve, rden_ready, b, 1)
                nc.vector.tensor_tensor(hp[:, :, :, :], outp, each_block(rden[:, :, :]), ALU.mult
                                        ).then_inc(hp_step.sem, 1)
                wait(dve, hp_step, b, 1)
                nc.vector.tensor_scalar(neg[:, :, :, :], hp[:, :, :, :], 0.0, None, ALU.min).then_inc(hp_step.sem, 1)
                nc.vector.scalar_tensor_tensor(out=hp[:, :, :, :], in0=hp[:, :, :, :], scalar=0.0, in1=t,
                                               op0=ALU.max, op1=ALU.add).then_inc(hp_step.sem, 1)
                wait(dve, neg_exp, b, 1)
                wait(dve, hp_step, b, 3)
                nc.vector.tensor_scalar(neg[:, :, :, :], neg[:, :, :, :], -1.0, None, ALU.add
                                        ).then_inc(x_added.sem, 1)
                wait(dve, x_added, b, 1)
                nc.vector.tensor_tensor(t, hp[:, :, :, :], neg[:, :, :, :], ALU.add).then_inc(x_added.sem, 1)


def experts(nc, X, ident, eps5, w, out):
    TILES = HALF // P
    with ExitStack() as ctx:
        def sb(name, shape, dt=F32):
            return ctx.enter_context(nc.sbuf_tensor(name, shape, dt))

        def sem(name, per=1):
            return Sem(ctx.enter_context(nc.semaphore(name)), per)

        mean_w = sb("moe_mean_w", [P, P])
        router = sb("router", [NE, DM])
        router_t = sb("router_t", [P, KC, NE])
        w1 = sb("w1", [P, NE, KC, DM])
        w2 = sb("w2", [P, NE, KC, DM])
        b1 = sb("b1", [P, NE, KC])
        b2 = sb("b2", [NE, DM])
        number = sb("number", [P, NE])
        held = sb("held", [P, KC, HALF])
        n = sb("n", [P, KC, HALF])
        sq = sb("moe_sq", [P, KC, HALF])
        rstd = sb("moe_rstd", [P, HALF])
        logit = sb("logit", [P, TILES, NE])
        best = sb("best", [P, TILES, 8])
        best_at = sb("best_at", [P, TILES, 8], U32)
        at_f = sb("at_f", [P, TILES, 2])
        top = sb("top", [P, TILES, 2])
        total = sb("total", [P, TILES])
        weight = sb("weight", [P, TILES, NE])
        other = sb("other", [P, TILES, NE])
        weight_t = sb("weight_t", [NE, HALF])
        hg = sb("hg", [P, 2, KC, HALF])
        acc = sb("acc", [P, TILES, DM])
        h_bank = ctx.enter_context(nc.psum_tensor("h_bank", [P, 2, KC, 512], F32))
        y_bank = ctx.enter_context(nc.psum_tensor("y_out", [P, 2 * 512], F32))
        stat = ctx.enter_context(nc.psum_tensor("stat", [P, 512], F32))
        small = ctx.enter_context(nc.psum_tensor("small", [P, 512], F32))
        y_tile = [y_bank[:, i * DM:(i + 1) * DM] for i in range(TILES)]
        y_all = y_bank[:, 0:TILES * DM].rearrange("p (t n) -> p t n", t=TILES)

        loaded = ctx.enter_context(nc.semaphore("moe_loaded"))
        consts_set = ctx.enter_context(nc.semaphore("moe_consts_set"))
        router_turned = ctx.enter_context(nc.semaphore("router_turned"))
        router_kept = ctx.enter_context(nc.semaphore("router_kept"))
        passed = ctx.enter_context(nc.semaphore("moe_waits_passed"))
        x_held = sem("x_held")
        mean_made = sem("moe_mean_made")
        centred = sem("moe_centred")
        squared = sem("moe_squared")
        var_made = sem("moe_var_made")
        rstd_step = sem("moe_rstd_step", 2)
        n_ready = sem("n_ready")
        logits_made = sem("logits_made")
        route_step = sem("route_step", 13)
        top_exp = sem("top_exp")
        total_step = sem("total_step", 2)
        weight_ready = sem("weight_ready")
        weight_turned = sem("weight_turned")
        weight_t_kept = sem("weight_t_kept")
        x_turned = sem("x_turned")
        acc_step = sem("acc_step", 2 + TILES * NE)
        bias_made = sem("bias_made")
        h_made = sem("moe_h_made", NE)
        h_done = sem("moe_h_done", KC * NE)
        y_made = sem("y_made", NE)
        stored = sem("stored", 16)
        sems = [x_held, mean_made, centred, squared, var_made, rstd_step, n_ready, logits_made, route_step, top_exp, total_step,
                weight_ready, weight_turned, weight_t_kept, x_turned, acc_step, bias_made, h_made, h_done,
                y_made, stored]
        ctx.enter_context(nc.allow_non_contiguous_dma(reason="biases of a few thousand values"))
        block = ctx.enter_context(nc.Block())

        def wait(eng, s, g, k):
            eng.wait_ge(s.sem, s.at(g, k))

        def tokens(g):
            return X[:, :, :].rearrange("p k (g n) -> p g k n", n=HALF)[:, g]

        @block.sync
        def _(sp):
            for s in sems:
                sp.sem_inc(s.sem, s.per)
            sp.dma_start(router[:, :], w["router_w"]).then_inc(loaded, 16)
            sp.dma_start(b1[:, :, :], w["b1"].rearrange("e (k p) -> p e k", p=P)).then_inc(loaded, 16)
            sp.dma_start(b2[:, :], w["b2"]).then_inc(loaded, 16)
            sp.dma_start(w1[:, :, :, :], w["w1"].rearrange("e (k p) n -> p e k n", p=P)).then_inc(loaded, 16)
            sp.dma_start(w2[:, :, :, :], w["w2"].rearrange("e (k p) n -> p e k n", p=P)).then_inc(loaded, 16)
            rows = out.rearrange("b o t d -> (b o t) d").rearrange("(g i p) d -> g p i d", p=P, i=TILES)
            with sp.Fori(0, CHUNKS) as g:
                wait_apart(sp, acc_step, g, 2 + TILES * NE, passed)
                sp.dma_start(rows[g], acc[:, :, :]).then_inc(stored.sem, 16)
            sp.wait_ge(stored.sem, stored.at(CHUNKS, 0))

        @block.gpsimd
        def _(pool):
            nc.gpsimd.memset(mean_w[:, :], 1.0 / DM).then_inc(consts_set, 1)
            nc.gpsimd.iota(number[:, :], pattern=[[1, NE]], base=0, channel_multiplier=0,
                           allow_small_or_imprecise_dtypes=True).then_inc(consts_set, 1)
            with pool.Fori(0, CHUNKS) as g:
                wait(pool, x_turned, g, 0)
                wait(pool, n_ready, g, 1)
                nc.gpsimd.tensor_tensor(held[:, :, :], tokens(g), n[:, :, :], ALU.add).then_inc(x_held.sem, 1)

        @block.tensor
        def _(pe):
            pe.wait_ge(consts_set, 2)
            pe.wait_ge(loaded, 16 * 5)
            for k in range(KC):
                last = nc.tensor.transpose(small[:, k * NE:(k + 1) * NE], router[:, k * P:(k + 1) * P],
                                           ident[0:NE, 0:NE])
            last.then_inc(router_turned, 1)
            pe.wait_ge(router_kept, 1)
            with pe.Fori(0, CHUNKS) as g:
                t = tokens(g)
                wait(pe, rstd_step, g, 0)
                for k in range(KC):
                    last = nc.tensor.matmul(stat[:, 0:HALF], mean_w[:, :], t[:, k], start=(k == 0), stop=(k == KC - 1))
                last.then_inc(mean_made.sem, 1)
                wait(pe, squared, g, 1)
                for k in range(KC):
                    last = nc.tensor.matmul(stat[:, 0:HALF], mean_w[:, :], sq[:, k, :],
                                            start=(k == 0), stop=(k == KC - 1))
                last.then_inc(var_made.sem, 1)
                wait(pe, n_ready, g, 1)
                wait(pe, weight_t_kept, g, 0)
                for i in range(TILES):
                    for k in range(KC):
                        last = nc.tensor.matmul(small[:, i * NE:(i + 1) * NE], n[:, k, i * P:(i + 1) * P],
                                                router_t[:, k, :], start=(k == 0), stop=(k == KC - 1))
                last.then_inc(logits_made.sem, 1)

                def hidden(e):
                    wait(pe, h_done, g, KC * (e - 1))
                    for m in range(KC):
                        for k in range(KC):
                            last = nc.tensor.matmul(h_bank[:, e % 2, m, 0:HALF], w1[:, e, k, m * P:(m + 1) * P],
                                                    n[:, k, :], start=(k == 0), stop=(k == KC - 1))
                    last.then_inc(h_made.sem, 1)

                hidden(0)
                wait(pe, acc_step, g, 0)
                wait(pe, x_held, g, 1)
                for i in range(TILES):
                    for k in range(KC):
                        last = nc.tensor.transpose(y_tile[i][:, k * P:(k + 1) * P], held[:, k, i * P:(i + 1) * P],
                                                   ident[:, :])
                last.then_inc(x_turned.sem, 1)
                wait(pe, weight_ready, g, 1)
                for i in range(TILES):
                    last = nc.tensor.transpose(small[0:NE, i * P:(i + 1) * P], weight[:, i, :], ident[:, :])
                last.then_inc(weight_turned.sem, 1)
                hidden(1)
                wait(pe, weight_t_kept, g, 1)
                wait(pe, acc_step, g, 1)
                for i in range(TILES):
                    last = nc.tensor.matmul(y_tile[i], weight_t[:, i * P:(i + 1) * P], b2[:, :], start=True, stop=True)
                last.then_inc(bias_made.sem, 1)
                for e in range(NE):
                    wait(pe, h_done, g, KC * (e + 1))
                    wait(pe, acc_step, g, 2 + TILES * e)
                    for i in range(TILES):
                        for k in range(KC):
                            last = nc.tensor.matmul(y_tile[i], hg[:, e % 2, k, i * P:(i + 1) * P], w2[:, e, k, :],
                                                    start=(k == 0), stop=(k == KC - 1))
                    last.then_inc(y_made.sem, 1)
                    if e + 2 < NE:
                        hidden(e + 2)

        @block.scalar
        def _(act):
            act.wait_ge(router_turned, 1)
            nc.scalar.copy(router_t[:, :, :], small[:, 0:KC * NE].rearrange("p (k e) -> p k e", k=KC)
                           ).then_inc(router_kept, 1)
            with act.Fori(0, CHUNKS) as g:
                wait(act, centred, g, 1)
                nc.scalar.activation(sq[:, :, :], n[:, :, :], ACT.Square).then_inc(squared.sem, 1)
                wait(act, var_made, g, 1)
                nc.scalar.activation(rstd[:, :], stat[:, 0:HALF], ACT.Ln, bias=eps5[:, 0:1]).then_inc(rstd_step.sem, 1)
                wait(act, rstd_step, g, 1)
                nc.scalar.activation(rstd[:, :], rstd[:, :], ACT.Exp, scale=-0.5).then_inc(rstd_step.sem, 1)
                wait(act, route_step, g, 7)
                nc.scalar.activation(logit[:, :, :], logit[:, :, :], ACT.Exp).then_inc(top_exp.sem, 1)
                for e in range(NE):
                    wait(act, h_made, g, e + 1)
                    wait(act, y_made, g, e - 1)
                    for m in range(KC):
                        nc.scalar.activation(hg[:, e % 2, m, :], h_bank[:, e % 2, m, 0:HALF], ACT.Gelu,
                                             bias=b1[:, e, m:m + 1]).then_inc(h_done.sem, 1)

        @block.vector
        def _(dve):
            dve.wait_ge(consts_set, 2)
            with dve.Fori(0, CHUNKS) as g:
                t = tokens(g)
                wait(dve, h_made, g, 0)
                wait(dve, x_held, g, 0)
                wait(dve, mean_made, g, 1)
                nc.vector.tensor_tensor(n[:, :, :], t, stat[:, 0:HALF].unsqueeze(1).broadcast_to([P, KC, HALF]),
                                        ALU.subtract).then_inc(centred.sem, 1)
                wait(dve, rstd_step, g, 2)
                wait(dve, squared, g, 1)
                nc.vector.tensor_tensor(n[:, :, :], n[:, :, :], rstd[:, :].unsqueeze(1).broadcast_to([P, KC, HALF]),
                                        ALU.mult).then_inc(n_ready.sem, 1)
                wait(dve, logits_made, g, 1)
                nc.vector.tensor_copy(logit[:, :, :], small[:, 0:TILES * NE].rearrange("p (i e) -> p i e", i=TILES)
                                      ).then_inc(route_step.sem, 1)
                wait_apart(dve, route_step, g, 1, passed)
                for i in range(TILES):
                    last = nc.vector.max(best[:, i, :], logit[:, i, :])
                last.then_inc(route_step.sem, 1)
                wait_apart(dve, route_step, g, 2, passed)
                for i in range(TILES):
                    last = nc.vector.max_index(best_at[:, i, :], best[:, i, :], logit[:, i, :])
                last.then_inc(route_step.sem, 1)
                wait(dve, route_step, g, 3)
                nc.vector.tensor_copy(at_f[:, :, :], best_at[:, :, 0:2]).then_inc(route_step.sem, 1)
                nc.vector.tensor_tensor(logit[:, :, :], logit[:, :, :], best[:, :, 0:1].broadcast_to([P, TILES, NE]),
                                        ALU.subtract).then_inc(route_step.sem, 3)
                wait(dve, top_exp, g, 1)
                nc.vector.tensor_reduce(total[:, :], logit[:, :, :], AX.X, ALU.add).then_inc(route_step.sem, 1)
                wait(dve, route_step, g, 8)
                nc.vector.reciprocal(total[:, :], total[:, :]).then_inc(route_step.sem, 1)
                wait(dve, route_step, g, 9)
                nc.vector.tensor_tensor(logit[:, :, :], logit[:, :, :],
                                        total[:, :].unsqueeze(2).broadcast_to([P, TILES, NE]), ALU.mult
                                        ).then_inc(route_step.sem, 1)
                wait(dve, route_step, g, 10)
                for i in range(TILES):
                    for r, dst in ((0, weight), (1, other)):
                        last = nc.vector.scalar_tensor_tensor(out=dst[:, i, :], in0=number[:, :],
                                                              scalar=at_f[:, i, r:r + 1], in1=logit[:, i, :],
                                                              op0=ALU.is_equal, op1=ALU.mult)
                last.then_inc(route_step.sem, 1)
                wait(dve, route_step, g, 11)
                wait(dve, weight_turned, g, 0)
                nc.vector.tensor_tensor(other[:, :, :], weight[:, :, :], other[:, :, :], ALU.add
                                        ).then_inc(route_step.sem, 1)
                wait(dve, route_step, g, 12)
                nc.vector.tensor_reduce(total[:, :], other[:, :, :], AX.X, ALU.add).then_inc(route_step.sem, 1)
                wait(dve, route_step, g, 13)
                nc.vector.tensor_scalar(total[:, :], total[:, :], 1e-12, None, ALU.max).then_inc(total_step.sem, 1)
                wait(dve, total_step, g, 1)
                nc.vector.reciprocal(total[:, :], total[:, :]).then_inc(total_step.sem, 1)
                wait(dve, total_step, g, 2)
                nc.vector.tensor_tensor(weight[:, :, :], other[:, :, :],
                                        total[:, :].unsqueeze(2).broadcast_to([P, TILES, NE]), ALU.mult
                                        ).then_inc(weight_ready.sem, 1)
                wait(dve, stored, g, 0)
                wait(dve, x_turned, g, 1)
                nc.vector.tensor_copy(acc[:, :, :], y_all).then_inc(acc_step.sem, 1)
                wait(dve, weight_turned, g, 1)
                nc.vector.tensor_copy(weight_t[:, :], small[0:NE, 0:HALF]).then_inc(weight_t_kept.sem, 1)
                wait(dve, bias_made, g, 1)
                wait(dve, acc_step, g, 1)
                nc.vector.tensor_tensor(acc[:, :, :], acc[:, :, :], y_all, ALU.add).then_inc(acc_step.sem, 1)
                wait(dve, weight_ready, g, 1)
                for e in range(NE):
                    wait(dve, y_made, g, e + 1)
                    wait(dve, acc_step, g, 2 + TILES * e)
                    for i in range(TILES):
                        nc.vector.scalar_tensor_tensor(out=acc[:, i, :], in0=y_tile[i], scalar=weight[:, i, e:e + 1],
                                                       in1=acc[:, i, :], op0=ALU.mult, op1=ALU.add
                                                       ).then_inc(acc_step.sem, 1)


def conv_attn_hybrid(nc, x, pe, ln_w, ln_b, in_proj, conv_w, conv_b, x_proj, dt_w, dt_b, A_log, Dp, out_proj,
                     W, a, router_w, w1, b1, w2, b2, out):
    with ExitStack() as ctx:
        X = ctx.enter_context(nc.sbuf_tensor("X", [P, KC, TOK], F32))
        ident = ctx.enter_context(nc.sbuf_tensor("ident", [P, P], F32))
        eps5 = ctx.enter_context(nc.sbuf_tensor("eps5", [P, 1], F32))
        load_tokens(nc, x, pe, X, ident, eps5)
        mamba(nc, X, ident, eps5, dict(ln_w=ln_w, ln_b=ln_b, in_proj=in_proj, conv_w=conv_w, conv_b=conv_b,
                                       x_proj=x_proj, dt_w=dt_w, dt_b=dt_b, A_log=A_log, Dp=Dp, out_proj=out_proj))
        attention(nc, X, ident, eps5, dict(W=W, a=a))
        experts(nc, X, ident, eps5, dict(router_w=router_w, w1=w1, b1=b1, w2=w2, b2=b2), out)


_INS = ["x"] + ["L0_conv_" + n for n in ("pe", "ln_w", "ln_b", "in_proj", "conv_w", "conv_b", "x_proj", "dt_w",
                                         "dt_b", "A_log", "Dp", "out_proj")] + \
    ["L1_attn_W", "L1_attn_a", "L1_ffn_router_w", "L1_ffn_w1", "L1_ffn_b1", "L1_ffn_w2", "L1_ffn_b2"]


def kernel(**inputs):
    import numpy as _np
    import concourse.bacc as _bacc
    from concourse import mybir as _mybir
    from concourse.bass_utils import run_bass_kernel_spmd as _run

    nc = _bacc.Bacc("TRN2", target_bir_lowering=False, num_devices=1)
    arrays, args = {}, []
    for name in _INS:
        arr = _np.ascontiguousarray(inputs[name])
        arrays[f"in_{name}"] = arr
        args.append(nc.dram_tensor(f"in_{name}", arr.shape, _mybir.dt.from_np(arr.dtype), kind="ExternalInput").ap())
    out = nc.dram_tensor("out_tokens", (NB, NO, NT, DM), _mybir.dt.float32, kind="ExternalOutput").ap()
    conv_attn_hybrid(nc, *args, out)
    r = _run(nc, [arrays], core_ids=[0])
    return r.results[0]["out_tokens"]
```

```python
import concourse.bass as bass
from concourse import mybir
from contextlib import ExitStack

F32 = mybir.dt.float32
BF16 = mybir.dt.bfloat16
U32 = mybir.dt.uint32
ALU = mybir.AluOpType
ACT = mybir.ActivationFunctionType
AX = mybir.AxisListType
P = 128

NB, NO, NT, DM = 8, 12, 64, 256
SEQ = NO * NT
TOK = NB * SEQ
NL = 2
DI = 2 * DM
DS = 16
DCONV = 4
DTR = DM // 16
HALF = SEQ // 2
KC = DM // P
MC = DI // P
XPW = DTR + 2 * DS
NE = 8
CHUNKS = 2 * NB
STAGES = 4


PE_IN = {1: (0, 1), 2: (2, 3), 11: (4, 5), 12: (6, 7)}
PE_OUT, PE_MEAN, SQUARE, PE_VAR, NORM = 3, 4, 5, 6, 6
ACT_X, X_GATE = (3, 4, 5), 5
PE_BC, DT_LOW, SPLIT = 7, 8, 8
PE_STEP = {9: (0, 1), 10: (2, 3)}
STEP_EXP, STEP_U, STEP_CORR, STEP_REST, STEP_LN = 11, 12, 12, 12, 13
DELTA, DU = 13, 14
ACT_Z, Z_GATE = (13, 14, 15), 15


class Sem:

    def __init__(self, sem, per, ahead=2):
        self.sem, self.per, self.ahead = sem, per, ahead

    def at(self, period, n):
        return (period + self.ahead) * self.per + n

    def start(self, eng):
        eng.sem_inc(self.sem, self.ahead * self.per)


def wait_apart(eng, s, period, n, passed):
    eng.wait_ge(s.sem, s.at(period, n))
    eng.sem_inc(passed, 1)


def load_tokens(nc, x, pe, X, ident, eps5):
    TILES = TOK // P
    GROUP = 4
    with ExitStack() as ctx:
        raw = ctx.enter_context(nc.sbuf_tensor("raw_tokens", [P, GROUP, DM], F32))
        pos = ctx.enter_context(nc.sbuf_tensor("pos_tokens", [P, DM], F32))
        turned = [ctx.enter_context(nc.psum_tensor(f"turned{i}", [P, 512], F32)) for i in range(2)]
        sem = lambda n: ctx.enter_context(nc.semaphore(n))
        pos_loaded = sem("pos_loaded")
        raw_loaded = [sem(f"raw_loaded{i}") for i in range(GROUP)]
        pos_added = sem("pos_added")
        tile_turned = sem("tile_turned")
        tile_kept = sem("tile_kept")
        ident_zeroed = sem("ident_zeroed")
        ident_ready = sem("ident_ready")
        block = ctx.enter_context(nc.Block())
        xt = x.rearrange("b o t d -> (b o t) d").rearrange("(n p) d -> p n d", p=P)

        @block.sync
        def _(sp):
            for i in range(P // NT):
                sp.dma_start(pos[i * NT:(i + 1) * NT, :], pe).then_inc(pos_loaded, 16)
            with sp.Fori(0, TILES // GROUP) as g:
                for i in range(GROUP):
                    sp.wait_ge(tile_turned, g * GROUP + i + 1)
                    sp.dma_start(raw[:, i, :], xt[:, g * GROUP + i, :]).then_inc(raw_loaded[i], 16)

        @block.gpsimd
        def _(pool):
            nc.gpsimd.memset(ident[:, :], 0.0).then_inc(ident_zeroed, 1)
            nc.gpsimd.memset(eps5[:, :], 1e-5)
            pool.wait_ge(ident_zeroed, 1)
            nc.gpsimd.affine_select(out=ident[:, :], in_=ident[:, :], compare_op=ALU.not_equal, fill=1.0,
                                    base=0, pattern=[[-1, P]], channel_multiplier=1).then_inc(ident_ready, 1)

        @block.vector
        def _(dve):
            dve.wait_ge(pos_loaded, 16 * (P // NT))
            with dve.Fori(0, TILES // GROUP) as g:
                for i in range(GROUP):
                    dve.wait_ge(raw_loaded[i], g * 16 + 16)
                    nc.vector.tensor_tensor(raw[:, i, :], raw[:, i, :], pos[:, :], ALU.add).then_inc(pos_added, 1)

        @block.tensor
        def _(pe_):
            pe_.wait_ge(ident_ready, 1)
            pe_.sem_inc(tile_turned, GROUP)
            with pe_.Fori(0, TILES // GROUP) as g:
                for i in range(GROUP):
                    pe_.wait_ge(pos_added, g * GROUP + i + 1)
                    pe_.wait_ge(tile_kept, g * GROUP + i + 1)
                    for k in range(KC):
                        last = nc.tensor.transpose(turned[i % 2][:, k * P:(k + 1) * P],
                                                   raw[:, i, k * P:(k + 1) * P], ident[:, :])
                    last.then_inc(tile_turned, 1)

        @block.scalar
        def _(act):
            act.sem_inc(tile_kept, 2)
            xw = X[:, :, :].rearrange("p k (g n) -> p g k n", n=GROUP * P)
            with act.Fori(0, TILES // GROUP) as g:
                for i in range(GROUP):
                    act.wait_ge(tile_turned, g * GROUP + i + 1 + GROUP)
                    nc.scalar.copy(xw[:, g, :, i * P:(i + 1) * P],
                                   turned[i % 2][:, 0:KC * P].rearrange("p (k n) -> p k n", k=KC)
                                   ).then_inc(tile_kept, 1)


def mamba(nc, X, ident, eps5, w):
    with ExitStack() as ctx:
        def sb(name, shape, dt=F32):
            return ctx.enter_context(nc.sbuf_tensor(name, shape, dt))

        def sem(name, per, ahead=2):
            s = Sem(ctx.enter_context(nc.semaphore(name)), per, ahead)
            all_sems.append(s)
            return s

        all_sems = []

        w_in = sb("w_in", [P, 2, KC, 2 * DI])
        w_out = sb("w_out", [P, 2, MC, DM])
        w_bc = sb("w_bc", [P, 2, MC, 6 * DS])
        w_dt = sb("w_dt", [P, 2, MC, DTR])
        w_step = sb("w_step", [DTR, 2, DI])
        taps = sb("taps", [P, 2, MC, DCONV])
        conv_bias = sb("conv_bias", [P, 2, MC])
        step_bias = sb("step_bias", [P, 2, MC])
        skip = sb("skip", [P, 2, MC])
        decay = sb("decay", [P, 2, MC, DS])
        ln_w = sb("ln_w", [P, KC])
        ln_b = sb("ln_b", [P, KC])
        mean_w = sb("mean_w", [P, P])
        pick = sb("pick", [6 * DS, 2 * DS], BF16)

        xs = sb("xs", [P, KC, HALF])
        xin = sb("xin", [P, MC, DCONV - 1 + HALF])
        xc = sb("xc", [P, 2, MC, HALF])
        sz = sb("sz", [P, 2, MC, HALF])
        delta = sb("delta", [P, 2, MC, HALF])
        du = sb("du", [P, 2, MC, HALF])
        tmp = sb("tmp", [P, MC, HALF])
        dt_low = sb("dt_low", [DTR, HALF])
        bc_rest = sb("bc_rest", [6 * DS, HALF])
        bc_parts = sb("bc_parts", [6 * DS, 2, HALF], BF16)
        b_wide = sb("b_wide", [P, 2, HALF])
        dbx = sb("dbx", [P, 2, MC, HALF])
        hs = sb("hs", [P, 2, MC, HALF])
        hc = sb("hc", [P, 2, MC, HALF])
        carry = sb("carry", [P, DS, MC])
        yg = sb("yg", [P, MC, HALF])
        fo = sb("fo", [P, KC, HALF])
        fwd_in = sb("fwd_in", [P, KC, HALF])
        res_in = sb("res_in", [P, 2, KC, HALF])
        rstd = sb("rstd", [P, HALF])
        sq = fwd_in

        fwd_dram = nc.dram_tensor("fwd_scratch", [P, CHUNKS, KC, HALF], F32, kind="Internal").ap()
        res_dram = nc.dram_tensor("res_scratch", [P, KC, TOK], F32, kind="Internal").ap()

        bank = lambda name: ctx.enter_context(nc.psum_tensor(name, [P, 512], F32))
        a_bank = [bank(f"a_bank{i}") for i in range(2)]
        y_bank = ctx.enter_context(nc.psum_tensor("y_bank", [P, MC * HALF], F32))
        b_bank = bank("b_bank")
        c_bank = bank("c_bank")
        misc = bank("misc")

        PREP = ([("in", m) for m in range(MC)] + [("bc", 0), ("dt", 0)] + [("step", m) for m in range(MC)]
                + [("in", m) for m in range(MC, 2 * MC)])
        CLOSE = [("out", k) for k in range(KC)] + [("mean", 0), ("var", 0)]
        USE = {what: n + 1 for order in (PREP, CLOSE) for n, what in enumerate(order)}
        NW = 12

        weights_loaded = sem("weights_loaded", 16 * NW)
        decay_step = sem("decay_step", 2)
        prep_full = sem("prep_full", len(PREP))
        prep_free = sem("prep_free", len(PREP))
        close_full = sem("close_full", len(CLOSE))
        close_free = sem("close_free", len(CLOSE))
        x_picked = sem("x_picked", 1)
        last_tap = sem("last_tap", MC)
        conv_step = sem("conv_step", MC * (DCONV - 1))
        xpre_ready = sem("xpre_ready", 1)
        halo_ready = sem("halo_ready", 1)
        z_sig = sem("z_sig", 3)
        x_sig = sem("x_sig", 3)
        sz_ready = sem("sz_ready", 1)
        xc_ready = sem("xc_ready", 1)
        split_step = sem("split_step", 6)
        step_abs = sem("step_abs", 1)
        step_exp = sem("step_exp", 1)
        step_u = sem("step_u", 1)
        step_corr = sem("step_corr", 1)
        step_rest = sem("step_rest", 1)
        step_ln = sem("step_ln", 1)
        delta_ready = sem("delta_ready", 1)
        du_ready = sem("du_ready", 1)
        a_ready = sem("a_ready", DS * MC)
        scan_done = sem("scan_done", DS * MC)
        b_made = sem("b_made", DS)
        b_copied = sem("b_copied", DS)
        dbx_ready = sem("dbx_ready", DS)
        c_ready = sem("c_ready", DS)
        cmul_done = sem("cmul_done", DS)
        y_added = sem("y_added", DS)
        y_read = sem("y_read", MC)
        yg_ready = sem("yg_ready", 1)
        carry_saved = sem("carry_saved", DS)
        x_written = sem("x_written", 1, ahead=NB + 1)
        fwd_stored = sem("fwd_stored", 16)
        fwd_loaded = sem("fwd_loaded", 16)
        centred = sem("centred", 1)
        sq_ready = sem("sq_ready", 1)
        rstd_ready = sem("rstd_ready", 1)
        norm_step = sem("norm_step", 4)
        res_stored = sem("res_stored", 16)
        res_loaded = sem("res_loaded", 16)
        plain = lambda name: ctx.enter_context(nc.semaphore(name))
        ln_loaded = plain("ln_loaded")
        ln_halved = plain("ln_halved")
        halo_zeroed = plain("halo_zeroed")
        passed = plain("waits_passed")
        mean_w_set = plain("mean_w_set")
        pick_zeroed = plain("pick_zeroed")
        pick_set = plain("pick_set")

        ctx.enter_context(nc.allow_non_contiguous_dma(reason="vectors of a few hundred values"))
        block = ctx.enter_context(nc.Block())

        class Chunk:

            def __init__(self, l, st, b, half):
                self.st, self.b, self.half = st, b, half
                self.blk, self.back = divmod(st, 2)
                self.nh = 1 - half if self.back else half
                self.g = l * (STAGES * CHUNKS) + b * 2 + (st * CHUNKS + half)
                self.batch = l * (STAGES * NB) + b + st * NB
                self.stage = l * STAGES + st
                self.dir = l * (2 * CHUNKS) + b * 2 + (self.blk * CHUNKS + half)
                self.dir_start = l * (2 * CHUNKS) + self.blk * CHUNKS
                self.layer = l * CHUNKS + b * 2 + half
                self.layer_start = l * CHUNKS
                self.layer_batch = l * NB + b

        def rounds(eng, start, round_, end):
            start(Chunk(0, 0, 0, 0))
            with eng.Fori(0, NL) as l:
                for st in range(STAGES):
                    round_(Chunk(l, st, 0, 0), Chunk(l, st, 0, 1), Chunk(l, st - 1, NB - 1, 1) if st else None)
                    with eng.Fori(0, NB - 1) as b:
                        round_(Chunk(l, st, b, 1), Chunk(l, st, b + 1, 0), Chunk(l, st, b, 0))
                        round_(Chunk(l, st, b + 1, 0), Chunk(l, st, b + 1, 1), Chunk(l, st, b, 1))
                    after = Chunk(l, st + 1, 0, 0) if st < STAGES - 1 else Chunk(l + 1, 0, 0, 0)
                    round_(Chunk(l, st, NB - 1, 1), after, Chunk(l, st, NB - 1, 0))
                end(Chunk(l, STAGES - 1, NB - 1, 1))

        def half_of(t, b, nh):
            return t.rearrange("p k (b h n) -> p b h k n", b=NB, h=2)[:, b, nh]

        def pick_chunk(ch):
            place = xs[:, :, ::-1] if ch.back else xs[:, :, :]
            if ch.blk == 0:
                return place, half_of(X[:, :, :], ch.b, ch.nh)
            return (place.rearrange("p k (t o) -> p k t o", o=NO),
                    X[:, :, :].rearrange("p k (b o h t) -> p b h k t o", b=NB, o=NO, h=2)[:, ch.b, ch.nh])

        def wide(ap, blocks=MC):
            return ap.unsqueeze(1).broadcast_to([P, blocks, HALF])

        def wait(eng, s, period, n):
            eng.wait_ge(s.sem, s.at(period, n))

        @block.sync
        def _(sp):
            for s in all_sems:
                s.start(sp)
            sp.dma_start(ln_w[:, :], w["ln_w"].rearrange("(k p) -> p k", p=P)).then_inc(ln_loaded, 16)
            sp.dma_start(ln_b[:, :], w["ln_b"].rearrange("(k p) -> p k", p=P)).then_inc(ln_loaded, 16)

            def load_weights(l, st):
                blk, back = divmod(st, 2)
                at = lambda name: w[name][l, blk, back]
                x_proj = at("x_proj").rearrange("(k p) n -> p k n", p=P)
                loads = [
                    (w_in[:, back], at("in_proj").rearrange("(k p) n -> p k n", p=P)),
                    (taps[:, back], at("conv_w").rearrange("(k p) n -> p k n", p=P)),
                    (conv_bias[:, back], at("conv_b").rearrange("(k p) -> p k", p=P)),
                    (w_dt[:, back], x_proj[:, :, 0:DTR]),
                    (w_step[:, back], at("dt_w")),
                    (step_bias[:, back], at("dt_b").rearrange("(k p) -> p k", p=P)),
                    (decay[:, back], at("A_log").rearrange("(k p) n -> p k n", p=P)),
                    (skip[:, back], at("Dp").rearrange("(k p) -> p k", p=P)),
                    (w_out[:, back], at("out_proj").rearrange("(k p) n -> p k n", p=P)),
                ] + [(w_bc[:, back, :, i * 2 * DS:(i + 1) * 2 * DS], x_proj[:, :, DTR:XPW]) for i in range(3)]
                assert len(loads) == NW
                for dst, src in loads:
                    sp.dma_start(dst, src).then_inc(weights_loaded.sem, 16)

            def results(ch):
                here = fwd_dram.rearrange("p (b h) k n -> p b h k n", h=2)[:, ch.b, ch.nh]
                if not ch.back:
                    wait_apart(sp, close_free, ch.g, len(CLOSE), passed)
                    sp.dma_start(here, fo[:, :, :]).then_inc(fwd_stored.sem, 16)
                    return
                wait_apart(sp, fwd_stored, ch.dir_start + CHUNKS, 0, passed)
                wait_apart(sp, norm_step, ch.dir, 0, passed)
                sp.dma_start(fwd_in[:, :, :], here).then_inc(fwd_loaded.sem, 16)
                if ch.blk == 0:
                    wait_apart(sp, norm_step, ch.dir, 4, passed)
                    sp.dma_start(half_of(res_dram, ch.b, ch.nh), fo[:, :, :]).then_inc(res_stored.sem, 16)
                else:
                    wait_apart(sp, res_stored, ch.layer_start + CHUNKS, 0, passed)
                    wait_apart(sp, x_written, ch.layer_batch, 0, passed)
                    sp.dma_start(res_in[:, ch.half], half_of(res_dram, ch.b, ch.nh)).then_inc(res_loaded.sem, 16)

            load_weights(0, 0)
            with sp.Fori(0, NL) as l:
                for st in range(STAGES):
                    wait_apart(sp, close_free, Chunk(l, st, 0, 0).g, 0, passed)
                    wait_apart(sp, weights_loaded, l * STAGES + st, 16 * NW, passed)
                    load_weights(l, st + 1) if st < STAGES - 1 else load_weights(NL - 1, 0)
                    with sp.Fori(0, NB) as b:
                        for half in range(2):
                            results(Chunk(l, st, b, half))
            sp.wait_ge(weights_loaded.sem, weights_loaded.at(NL * STAGES, 16 * NW))

        @block.gpsimd
        def _(pool):
            nc.gpsimd.memset(mean_w[:, :], 1.0 / DM).then_inc(mean_w_set, 1)
            nc.gpsimd.memset(pick[:, :], 0.0).then_inc(pick_zeroed, 1)
            for part in range(3):
                pool.wait_ge(pick_zeroed, part + 1)
                last = nc.gpsimd.affine_select(out=pick[:, :], in_=pick[:, :], compare_op=ALU.not_equal,
                                               fill=1.0, base=-2 * DS * part, pattern=[[-1, 2 * DS]],
                                               channel_multiplier=1)
                last.then_inc(pick_zeroed if part < 2 else pick_set, 1)
            pool.wait_ge(ln_loaded, 32)
            nc.gpsimd.tensor_scalar(ln_w[:, :], ln_w[:, :], 0.5, 1.0, ALU.mult, ALU.mult).then_inc(ln_halved, 1)
            nc.gpsimd.tensor_scalar(ln_b[:, :], ln_b[:, :], 0.5, 1.0, ALU.mult, ALU.mult).then_inc(ln_halved, 1)

            def prepare(s, ch):
                g, half = ch.g, ch.half
                if s == 0:
                    wait_apart(pool, prep_full, g, 0, passed)
                    if ch.st == 0:
                        wait_apart(pool, x_written, ch.layer_batch - NB, 1, passed)
                    nc.gpsimd.tensor_copy(*pick_chunk(ch)).then_inc(x_picked.sem, 1)
                if s == X_GATE:
                    wait(pool, x_sig, g, 3)
                    nc.gpsimd.tensor_tensor(xc[:, half], xc[:, half], tmp[:, :, :], ALU.mult).then_inc(xc_ready.sem, 1)
                if s == STEP_REST:
                    wait(pool, step_corr, g, 1)
                    wait(pool, prep_free, g, USE["step", MC - 1])
                    nc.gpsimd.tensor_tensor(tmp[:, :, :], tmp[:, :, :], du[:, half], ALU.subtract
                                            ).then_inc(step_rest.sem, 1)
                if s == DELTA:
                    wait(pool, step_ln, g, 1)
                    wait(pool, step_rest, g, 1)
                    nc.gpsimd.tensor_tensor(delta[:, half], delta[:, half], tmp[:, :, :], ALU.add
                                            ).then_inc(delta_ready.sem, 1)
                if s == DU:
                    wait(pool, delta_ready, g, 1)
                    wait(pool, xc_ready, g, 1)
                    nc.gpsimd.tensor_tensor(du[:, half], delta[:, half], xc[:, half], ALU.mult).then_inc(du_ready.sem, 1)
                if s == Z_GATE:
                    wait(pool, z_sig, g, 3)
                    nc.gpsimd.tensor_tensor(sz[:, half], sz[:, half], yg[:, :, :], ALU.mult).then_inc(sz_ready.sem, 1)

            def start(ch):
                for s in range(DS):
                    prepare(s, ch)

            def round_(cur, nxt, prv):
                g = cur.g
                wait(pool, du_ready, g, 1)
                for s in range(DS):
                    wait(pool, b_copied, g, s + 1)
                    wait(pool, scan_done, g, MC * (s - 1))
                    nc.gpsimd.tensor_tensor(dbx[:, s % 2], du[:, cur.half], wide(b_wide[:, s % 2, :]), ALU.mult
                                            ).then_inc(dbx_ready.sem, 1)
                    prepare(s, nxt)

            rounds(pool, start, round_, lambda ch: None)

        @block.tensor
        def _(pe):
            pe.wait_ge(mean_w_set, 1)
            pe.wait_ge(pick_set, 1)

            def widen_b(ch, s):
                wait(pe, split_step, ch.g, 6)
                wait(pe, b_copied, ch.g, s)
                nc.tensor.matmul(b_bank[:, 0:HALF], pick[:, s:s + 1].broadcast_to([6 * DS, P]), bc_parts[:, ch.half, :],
                                 start=True, stop=True).then_inc(b_made.sem, 1)

            def widen_c(ch, s):
                wait(pe, cmul_done, ch.g, s)
                nc.tensor.matmul(c_bank[:, 0:HALF], pick[:, DS + s:DS + s + 1].broadcast_to([6 * DS, P]), bc_parts[:, ch.half, :],
                                 start=True, stop=True).then_inc(c_ready.sem, 1)

            def add_state(ch, s):
                wait(pe, cmul_done, ch.g, s + 1)
                if s == 0:
                    wait(pe, y_read, ch.g, 0)
                flat = hc[:, s % 2].rearrange("p m n -> p (m n)")
                for c in range(0, MC * HALF, 512):
                    last = nc.tensor.matmul(y_bank[:, c:c + 512], ident[:, :], flat[:, c:c + 512],
                                            start=(s == 0), stop=(s == DS - 1))
                last.then_inc(y_added.sem, 1)

            def prepare(s, ch, closed):
                g, back = ch.g, ch.back
                for m in PE_IN.get(s, ()):
                    if m == 0:
                        wait(pe, weights_loaded, ch.stage, 16 * NW)
                        wait(pe, x_picked, g, 1)
                        wait(pe, close_free, g - 1, 0) if closed is None else wait(pe, close_free, closed.g, 0)
                    wait(pe, prep_free, g, USE["in", m] - 1)
                    for k in range(KC):
                        last = nc.tensor.matmul(misc[:, 0:HALF], w_in[:, back, k, m * P:(m + 1) * P], xs[:, k, :],
                                                start=(k == 0), stop=(k == KC - 1))
                    last.then_inc(prep_full.sem, 1)
                if s == PE_BC:
                    wait(pe, xc_ready, g, 1)
                    if closed is not None:
                        wait(pe, close_free, closed.g, len(CLOSE))
                    for what, weight, rows in ((("bc", 0), w_bc, 6 * DS), (("dt", 0), w_dt, DTR)):
                        wait(pe, prep_free, g, USE[what] - 1)
                        for k in range(MC):
                            last = nc.tensor.matmul(misc[0:rows, 0:HALF], weight[:, back, k, :], xc[:, ch.half, k, :],
                                                    start=(k == 0), stop=(k == MC - 1))
                        last.then_inc(prep_full.sem, 1)
                for m in PE_STEP.get(s, ()):
                    wait(pe, prep_free, g, USE["step", m] - 1)
                    nc.tensor.matmul(misc[:, 0:HALF], w_step[:, back, m * P:(m + 1) * P], dt_low[:, :],
                                     start=True, stop=True).then_inc(prep_full.sem, 1)

            def close(s, ch, prepared_uses):
                back = ch.back
                if s == PE_OUT:
                    wait(pe, yg_ready, ch.g, 1)
                    wait(pe, prep_free, ch.g + 2, prepared_uses)
                    for k in range(KC):
                        wait(pe, close_free, ch.g, USE["out", k] - 1)
                        for m in range(MC):
                            ys = yg[:, m, ::-1] if back else yg[:, m, :]
                            last = nc.tensor.matmul(misc[:, 0:HALF], w_out[:, back, m, k * P:(k + 1) * P], ys,
                                                    start=(m == 0), stop=(m == MC - 1))
                        last.then_inc(close_full.sem, 1 if back or k < KC - 1 else 1 + len(CLOSE) - KC)
                for step, what, src in ((PE_MEAN, "mean", fo), (PE_VAR, "var", sq)):
                    if back and s == step:
                        wait(pe, close_free, ch.g, USE[what, 0] - 1)
                        if what == "var":
                            wait(pe, sq_ready, ch.dir, 1)
                        for k in range(KC):
                            last = nc.tensor.matmul(misc[:, 0:HALF], mean_w[:, :], src[:, k, :],
                                                    start=(k == 0), stop=(k == KC - 1))
                        last.then_inc(close_full.sem, 1)

            def start(ch):
                for s in range(DS):
                    prepare(s, ch, None)
                for s in range(2):
                    widen_b(ch, s)

            def round_(cur, nxt, prv):
                for s in range(DS):
                    widen_b(cur, s + 2) if s + 2 < DS else widen_b(nxt, s + 2 - DS)
                    if prv is not None:
                        close(s, prv, MC)
                    prepare(s, nxt, prv)
                    widen_c(cur, s)
                    if s > 0:
                        add_state(cur, s - 1)
                    elif prv is not None:
                        add_state(prv, DS - 1)

            def end(ch):
                add_state(ch, DS - 1)
                for s in range(DS):
                    close(s, ch, 0)

            rounds(pe, start, round_, end)

        @block.scalar
        def _(act):
            nc.scalar.preload_act_table_set("natural_log_exp_and_others")

            def sigmoid(part, dst, src, s, g):
                if part == 0:
                    nc.scalar.activation(dst, src, ACT.Exp, scale=-1.0).then_inc(s.sem, 1)
                else:
                    wait(act, s, g, part)
                    if part == 1:
                        nc.scalar.activation(dst, dst, ACT.Ln, bias=1.0).then_inc(s.sem, 1)
                    else:
                        nc.scalar.activation(dst, dst, ACT.Exp, scale=-1.0).then_inc(s.sem, 1)

            def copy_b(ch, s):
                wait(act, b_made, ch.g, s + 1)
                wait(act, dbx_ready, ch.g, s - 1)
                nc.scalar.copy(b_wide[:, s % 2, :], b_bank[:, 0:HALF]).then_inc(b_copied.sem, 1)

            def prepare(s, ch):
                g, half, back = ch.g, ch.half, ch.back
                for m in PE_IN.get(s, ()):
                    if m >= MC:
                        continue
                    if m == 0:
                        wait(act, halo_ready, g, 0)
                        wait(act, weights_loaded, ch.stage, 16 * NW)
                    if m == 0:
                        wait(act, y_read, g - 1, 0)
                    wait(act, prep_full, g, USE["in", m])
                    nc.scalar.activation(xc[:, half, m, :], misc[:, 0:HALF], ACT.Identity,
                                         bias=conv_bias[:, back, m:m + 1], scale=taps[:, back, m, DCONV - 1:DCONV]
                                         ).then_inc(last_tap.sem, 1)
                    nc.scalar.copy(xin[:, m, DCONV - 1:], misc[:, 0:HALF]).then_inc(prep_free.sem, 1)
                for part in range(3):
                    if s == ACT_X[part]:
                        if part == 0:
                            wait(act, xpre_ready, g, 1)
                            wait(act, delta_ready, g, 0)
                        sigmoid(part, tmp[:, :, :], xc[:, half], x_sig, g)
                    if s == ACT_Z[part]:
                        if part == 0:
                            wait(act, prep_free, g, USE["in", 2 * MC - 1])
                            wait(act, close_full, g - 1, 0)
                        sigmoid(part, yg[:, :, :], sz[:, half], z_sig, g)
                if s == DT_LOW:
                    wait(act, prep_full, g, USE["dt", 0])
                    nc.scalar.copy(dt_low[:, :], misc[0:DTR, 0:HALF]).then_inc(prep_free.sem, 1)
                for m in PE_STEP.get(s, ()):
                    if m == 0:
                        wait(act, xc_ready, g, 1)
                    wait(act, prep_full, g, USE["step", m])
                    pre = nc.scalar.activation(delta[:, half, m, :], misc[:, 0:HALF], ACT.Abs,
                                               bias=step_bias[:, back, m:m + 1])
                    if m == MC - 1:
                        pre.then_inc(step_abs.sem, 1)
                    nc.scalar.activation(tmp[:, m, :], misc[:, 0:HALF], ACT.Relu,
                                         bias=step_bias[:, back, m:m + 1]).then_inc(prep_free.sem, 1)
                if s == STEP_EXP:
                    wait(act, step_abs, g, 1)
                    nc.scalar.activation(du[:, half], delta[:, half], ACT.Exp, scale=-1.0).then_inc(step_exp.sem, 1)
                if s == STEP_U:
                    wait(act, step_exp, g, 1)
                    nc.scalar.activation(delta[:, half], du[:, half], ACT.Identity, bias=1.0).then_inc(step_u.sem, 1)
                if s == STEP_LN:
                    wait(act, step_u, g, 1)
                    wait(act, step_corr, g, 1)
                    nc.scalar.activation(delta[:, half], delta[:, half], ACT.Ln).then_inc(step_ln.sem, 1)

            def make_decay(ch):
                wait(act, weights_loaded, ch.stage, 16 * NW)
                nc.scalar.activation(decay[:, ch.back], decay[:, ch.back], ACT.Exp).then_inc(decay_step.sem, 1)
                wait(act, decay_step, ch.stage, 1)
                nc.scalar.mul(decay[:, ch.back], decay[:, ch.back], -1.0).then_inc(decay_step.sem, 1)

            def close(s, ch):
                if not ch.back and s == PE_OUT:
                    wait(act, fwd_stored, ch.dir, 0)
                    wait(act, norm_step, ch.dir_start, 0)
                    if ch.st == 2:
                        wait(act, res_stored, ch.layer_start + CHUNKS, 0)
                    for k in range(KC):
                        wait(act, close_full, ch.g, USE["out", k])
                        nc.scalar.copy(fo[:, k, :], misc[:, 0:HALF]
                                       ).then_inc(close_free.sem, 1 if k < KC - 1 else 1 + len(CLOSE) - KC)
                if ch.back and s == SQUARE:
                    wait(act, close_free, ch.g, USE["mean", 0])
                    wait(act, centred, ch.dir, 1)
                    nc.scalar.activation(sq[:, :, :], fo[:, :, :], ACT.Square).then_inc(sq_ready.sem, 1)
                if ch.back and s == PE_VAR:
                    wait(act, close_full, ch.g, USE["var", 0])
                    nc.scalar.activation(rstd[:, :], misc[:, 0:HALF], ACT.Ln, bias=eps5[:, 0:1]
                                         ).then_inc(close_free.sem, 1)
                    wait(act, close_free, ch.g, USE["var", 0])
                    nc.scalar.activation(rstd[:, :], rstd[:, :], ACT.Exp, scale=-0.5).then_inc(rstd_ready.sem, 1)

            def start(ch):
                make_decay(ch)
                for s in range(DS):
                    prepare(s, ch)
                for s in range(2):
                    copy_b(ch, s)

            def round_(cur, nxt, prv):
                g = cur.g
                wait(act, delta_ready, g, 1)
                wait(act, decay_step, cur.stage, 2)
                for s in range(DS):
                    for c in range(MC):
                        n = s * MC + c
                        wait(act, scan_done, g, n - 1)
                        nc.scalar.activation(a_bank[n % 2][:, 0:HALF], delta[:, cur.half, c, :], ACT.Exp,
                                             scale=decay[:, cur.back, c, s:s + 1]).then_inc(a_ready.sem, 1)
                        if c == 2:
                            if s == 0 and nxt.st != cur.st:
                                make_decay(nxt)
                            prepare(s, nxt)
                            if prv is not None:
                                close(s, prv)
                        if c == 3:
                            copy_b(cur, s + 2) if s + 2 < DS else copy_b(nxt, s + 2 - DS)

            def end(ch):
                for s in range(DS):
                    close(s, ch)

            rounds(act, start, round_, end)

        @block.vector
        def _(dve):
            LOW = -44.0
            nc.vector.memset(xin[:, :, 0:DCONV - 1], 0.0).then_inc(halo_zeroed, 1)
            dve.wait_ge(halo_zeroed, 1)
            dve.wait_ge(ln_halved, 2)

            def prepare(s, ch):
                g, half, back = ch.g, ch.half, ch.back
                for m in PE_IN.get(s, ()):
                    if m < MC:
                        if m == 0:
                            wait(dve, halo_ready, g, 0)
                            wait(dve, weights_loaded, ch.stage, 16 * NW)
                        wait(dve, prep_free, g, USE["in", m])
                        wait(dve, last_tap, g, m + 1)
                        continue
                    wait(dve, prep_full, g, USE["in", m])
                    nc.vector.tensor_scalar(sz[:, half, m - MC, :], misc[:, 0:HALF], LOW, None, ALU.max
                                            ).then_inc(prep_free.sem, 1)
                xparts = [m for m in PE_IN.get(s, ()) if m < MC]
                for tap in range(DCONV - 1):
                    for m in xparts:
                        if tap > 0:
                            wait(dve, conv_step, g, xparts[0] * (DCONV - 1) + (tap - 1) * len(xparts) + m - xparts[0] + 1)
                        nc.vector.scalar_tensor_tensor(out=xc[:, half, m, :], in0=xin[:, m, tap:tap + HALF],
                                                       scalar=taps[:, back, m, tap:tap + 1], in1=xc[:, half, m, :],
                                                       op0=ALU.mult, op1=ALU.add).then_inc(conv_step.sem, 1)
                if MC - 1 in xparts:
                    wait(dve, conv_step, g, MC * (DCONV - 1))
                    nc.vector.tensor_scalar(xc[:, half], xc[:, half], LOW, None, ALU.max).then_inc(xpre_ready.sem, 1)
                    if half == 0:
                        nc.vector.tensor_copy(xin[:, :, 0:DCONV - 1], xin[:, :, HALF:HALF + DCONV - 1]
                                              ).then_inc(halo_ready.sem, 1)
                    else:
                        nc.vector.memset(xin[:, :, 0:DCONV - 1], 0.0).then_inc(halo_ready.sem, 1)
                if s == PE_BC:
                    wait(dve, prep_full, g, USE["bc", 0])
                    nc.vector.tensor_copy(bc_rest[:, :], misc[0:6 * DS, 0:HALF]).then_inc(prep_free.sem, 1)
                if s == SPLIT:
                    parts = bc_parts[:, half, :]
                    wait(dve, prep_free, g, USE["bc", 0])
                    nc.vector.tensor_copy(parts, bc_rest[:, :]).then_inc(split_step.sem, 1)
                    wait(dve, split_step, g, 1)
                    nc.vector.tensor_tensor(bc_rest[:, :], bc_rest[:, :], parts, ALU.subtract
                                            ).then_inc(split_step.sem, 1)
                    wait(dve, split_step, g, 2)
                    for part in (1, 2):
                        rows = slice(part * 2 * DS, (part + 1) * 2 * DS)
                        nc.vector.tensor_copy(parts[rows], bc_rest[rows, :]).then_inc(split_step.sem, 1)
                    wait(dve, split_step, g, 4)
                    nc.vector.tensor_tensor(bc_rest[rows, :], bc_rest[rows, :], parts[rows], ALU.subtract
                                            ).then_inc(split_step.sem, 1)
                    wait(dve, split_step, g, 5)
                    nc.vector.tensor_copy(parts[rows], bc_rest[rows, :]).then_inc(split_step.sem, 1)
                if s == STEP_CORR:
                    wait(dve, step_u, g, 1)
                    nc.vector.scalar_tensor_tensor(out=du[:, half], in0=delta[:, half], scalar=1.0, in1=du[:, half],
                                                   op0=ALU.subtract, op1=ALU.subtract).then_inc(step_corr.sem, 1)

            def times_c(ch, s):
                wait(dve, c_ready, ch.g, s + 1)
                wait(dve, scan_done, ch.g, MC * (s + 1))
                wait(dve, y_added, ch.g, s - 1)
                nc.vector.tensor_tensor(hc[:, s % 2], hs[:, s % 2], wide(c_bank[:, 0:HALF]), ALU.mult
                                        ).then_inc(cmul_done.sem, 1)
                if ch.half == 0:
                    nc.vector.tensor_copy(carry[:, s, :], hs[:, s % 2, :, HALF - 1]).then_inc(carry_saved.sem, 1)

            def gate(ch):
                wait(dve, y_added, ch.g, DS)
                wait(dve, close_full, ch.g, 0)
                wait(dve, sz_ready, ch.g + 1, 1)
                for m in range(MC):
                    nc.vector.scalar_tensor_tensor(out=yg[:, m, :], in0=xc[:, ch.half, m, :],
                                                   scalar=skip[:, ch.back, m:m + 1],
                                                   in1=y_bank[:, m * HALF:(m + 1) * HALF], op0=ALU.mult, op1=ALU.add
                                                   ).then_inc(y_read.sem, 1)
                wait(dve, y_read, ch.g, MC)
                nc.vector.tensor_tensor(yg[:, :, :], yg[:, :, :], sz[:, ch.half], ALU.mult).then_inc(yg_ready.sem, 1)

            def close(s, ch):
                if not ch.back:
                    return
                if s == PE_OUT:
                    wait(dve, fwd_loaded, ch.dir, 16)
                    wait(dve, fwd_stored, ch.dir_start + CHUNKS, 0)
                    if ch.blk == 0:
                        wait(dve, res_stored, ch.layer, 0)
                    for k in range(KC):
                        wait(dve, close_full, ch.g, USE["out", k])
                        nc.vector.tensor_tensor(fo[:, k, :], misc[:, 0:HALF], fwd_in[:, k, :], ALU.add
                                                ).then_inc(close_free.sem, 1)
                if s == PE_MEAN:
                    wait(dve, close_full, ch.g, USE["mean", 0])
                    for k in range(KC):
                        nc.vector.tensor_tensor(fo[:, k, :], fo[:, k, :], misc[:, 0:HALF], ALU.subtract
                                                ).then_inc(centred.sem if k == 0 else close_free.sem, 1)
                if s == NORM:
                    wait(dve, rstd_ready, ch.dir, 1)
                    wait(dve, close_free, ch.g, USE["mean", 0])
                    wait(dve, sq_ready, ch.dir, 1)
                    nc.vector.tensor_tensor(fo[:, :, :], fo[:, :, :], wide(rstd[:, :], KC), ALU.mult
                                            ).then_inc(norm_step.sem, 1)
                    wait(dve, norm_step, ch.dir, 1)
                    for k in range(KC):
                        nc.vector.tensor_scalar(fo[:, k, :], fo[:, k, :], ln_w[:, k:k + 1], ln_b[:, k:k + 1],
                                                ALU.mult, ALU.add).then_inc(norm_step.sem, 1)
                    wait(dve, norm_step, ch.dir, 3)
                    if ch.blk == 0:
                        nc.vector.tensor_tensor(fo[:, :, :], fo[:, :, :], half_of(X[:, :, :], ch.b, ch.nh), ALU.add
                                                ).then_inc(norm_step.sem, 1)
                        return
                    wait(dve, res_loaded, ch.layer, 16)
                    to = res_in[:, 0] if ch.half == 0 else half_of(X[:, :, :], ch.b, ch.nh)
                    nc.vector.tensor_tensor(to, fo[:, :, :], res_in[:, ch.half], ALU.add).then_inc(norm_step.sem, 1)
                    if ch.half == 1:
                        wait(dve, norm_step, ch.dir, 4)
                        nc.vector.tensor_copy(half_of(X[:, :, :], ch.b, ch.half), res_in[:, 0]
                                              ).then_inc(x_written.sem, 1)

            def start(ch):
                for s in range(DS):
                    prepare(s, ch)

            def round_(cur, nxt, prv):
                g = cur.g
                for s in range(DS):
                    wait(dve, dbx_ready, g, s + 1)
                    if cur.half == 1:
                        wait(dve, carry_saved, cur.batch, s + 1)
                    wait(dve, cmul_done, g, s - 1)
                    for c in range(MC):
                        n = s * MC + c
                        wait(dve, a_ready, g, n + 1)
                        nc.vector.tensor_tensor_scan(hs[:, s % 2, c, :], a_bank[n % 2][:, 0:HALF],
                                                     dbx[:, s % 2, c, :],
                                                     0.0 if cur.half == 0 else carry[:, s, c:c + 1],
                                                     ALU.mult, ALU.add).then_inc(scan_done.sem, 1)
                        if c == 0 and s > 0:
                            times_c(cur, s - 1)
                        elif c == 0 and prv is not None:
                            times_c(prv, DS - 1)
                    if s == 0 and prv is not None:
                        gate(prv)
                    prepare(s, nxt)
                    if prv is not None:
                        close(s, prv)

            def end(ch):
                times_c(ch, DS - 1)
                gate(ch)
                for s in range(DS):
                    close(s, ch)

            rounds(dve, start, round_, end)


def attention(nc, X, ident, eps5, w):
    KT = SEQ // P
    with ExitStack() as ctx:
        def sb(name, shape, dt=F32):
            return ctx.enter_context(nc.sbuf_tensor(name, shape, dt))

        def sem(name, per=1):
            return Sem(ctx.enter_context(nc.semaphore(name)), per)

        mean_w = sb("attn_mean_w", [P, P])
        ones = sb("ones", [P, P])
        w_h = sb("w_h", [P, KC, DM + 1])
        w_t = sb("w_t", [P, KC, DM])
        a_cols = sb("a_cols", [P, 2 * KC])
        wa = sb("wa", [P, 2, KC, P])
        z = sb("z", [P, KC, 2, HALF])
        sq = sb("attn_sq", [P, KC, 2, HALF])
        rstd = sb("attn_rstd", [P, 2, HALF])
        h_sb = sb("h_sb", [P, KT, DM + 1])
        f2_max = sb("f2_max", [P, 1])
        row_max = sb("row_max", [P, 2, HALF])
        score = sb("score", [P, 2, 2, HALF])
        prob = sb("prob", [P, 2, 2, HALF])
        rden = sb("rden", [P, 2, HALF])
        hp = sb("hp", [P, KC, 2, HALF])
        neg = sb("neg", [P, KC, 2, HALF])
        bank4 = ctx.enter_context(nc.psum_tensor("out_banks", [P, KC, 2, 512], F32))
        f1_bank = ctx.enter_context(nc.psum_tensor("f1_bank", [P, 2, 512], F32))
        den_bank = ctx.enter_context(nc.psum_tensor("den_bank", [P, 2, 512], F32))
        f1, den, outp = f1_bank[:, :, 0:HALF], den_bank[:, :, 0:HALF], bank4[:, :, :, 0:HALF]
        h_bank = [bank4[:, 0, 0, 0:DM + 1], bank4[:, 0, 1, 0:DM + 1]]

        loaded = ctx.enter_context(nc.semaphore("attn_loaded"))
        consts_set = ctx.enter_context(nc.semaphore("consts_set"))
        w_turned = ctx.enter_context(nc.semaphore("w_turned"))
        w_t_kept = ctx.enter_context(nc.semaphore("w_t_kept"))
        wa_made = ctx.enter_context(nc.semaphore("wa_made"))
        wa_kept = ctx.enter_context(nc.semaphore("wa_kept"))
        mean_made = sem("mean_made")
        centred = sem("attn_centred", 2)
        squared = sem("squared")
        var_made = sem("var_made")
        rstd_step = sem("rstd_step", 2)
        z_ready = sem("z_ready")
        h_made = sem("h_made", KT)
        h_kept = sem("h_kept", KT)
        f_made = sem("f_made")
        max_step = sem("max_step", 3)
        score_step = sem("score_step", 3 * KT)
        prob_ready = sem("prob_ready", KT)
        prob_used = sem("prob_used", KT)
        rden_ready = sem("rden_ready")
        hp_step = sem("hp_step", 3)
        neg_exp = sem("neg_exp")
        x_added = sem("x_added", 2)
        sems = [mean_made, centred, squared, var_made, rstd_step, z_ready, h_made, h_kept, f_made, max_step,
                score_step, prob_ready, prob_used, rden_ready, hp_step, neg_exp, x_added]
        ctx.enter_context(nc.allow_non_contiguous_dma(reason="vectors of a few hundred values"))
        block = ctx.enter_context(nc.Block())

        def wait(eng, s, b, n):
            eng.wait_ge(s.sem, s.at(b, n))

        def tokens(b):
            return X[:, :, :].rearrange("p k (b h n) -> p b k h n", b=NB, h=2)[:, b]

        def each_block(ap):
            return ap.unsqueeze(1).broadcast_to([P, KC, 2, HALF])

        @block.sync
        def _(sp):
            for s in sems:
                s.start(sp)
            sp.dma_start(w_h[:, :, 0:DM], w["W"].rearrange("(k p) n -> p k n", p=P)).then_inc(loaded, 16)
            sp.dma_start(a_cols[:, :], w["a"].rearrange("(c p) n -> p (c n)", p=P)).then_inc(loaded, 16)
            sp.wait_ge(loaded, 32)

        @block.gpsimd
        def _(pool):
            nc.gpsimd.memset(mean_w[:, :], 1.0 / DM).then_inc(consts_set, 1)
            nc.gpsimd.memset(ones[:, :], 1.0).then_inc(consts_set, 1)

        @block.tensor
        def _(pe):
            pe.wait_ge(consts_set, 2)
            pe.wait_ge(loaded, 32)
            for k in range(KC):
                for o in range(KC):
                    last = nc.tensor.transpose(den_bank[:, o, k * P:(k + 1) * P], w_h[:, k, o * P:(o + 1) * P],
                                               ident[:, :])
            last.then_inc(w_turned, 1)
            pe.wait_ge(w_t_kept, 1)
            for v in range(2):
                for k in range(KC):
                    for o in range(KC):
                        last = nc.tensor.matmul(f1_bank[:, v, k * P:(k + 1) * P], w_t[:, o, k * P:(k + 1) * P],
                                                a_cols[:, v * KC + o:v * KC + o + 1].broadcast_to([P, P]),
                                                start=(o == 0), stop=(o == KC - 1))
            last.then_inc(wa_made, 1)
            pe.wait_ge(wa_kept, 2)

            with pe.Fori(0, NB) as b:
                t = tokens(b)

                def over_features(dst, weight, src):
                    for h in range(2):
                        for k in range(KC):
                            last = nc.tensor.matmul(dst[:, h, 0:HALF], weight(k), src[:, k, h],
                                                    start=(k == 0), stop=(k == KC - 1))
                    return last

                wait(pe, rden_ready, b, 0)
                over_features(den_bank, lambda k: mean_w[:, :], t).then_inc(mean_made.sem, 1)
                wait(pe, squared, b, 1)
                wait(pe, centred, b, 2)
                over_features(den_bank, lambda k: mean_w[:, :], sq).then_inc(var_made.sem, 1)
                wait(pe, z_ready, b, 1)
                wait(pe, hp_step, b, 0)
                for j in range(KT):
                    if j >= 2:
                        wait(pe, h_kept, b, j - 1)
                    zj = z[:, :, :, :].rearrange("p k h n -> p k (h n)")
                    for k in range(KC):
                        last = nc.tensor.matmul(h_bank[j % 2], zj[:, k, j * P:(j + 1) * P], w_h[:, k, :],
                                                start=(k == 0), stop=(k == KC - 1))
                    last.then_inc(h_made.sem, 1)
                wait(pe, rstd_step, b, 2)
                wait(pe, score_step, b, 0)
                over_features(f1_bank, lambda k: wa[:, 0, k, :], z)
                over_features(den_bank, lambda k: wa[:, 1, k, :], z).then_inc(f_made.sem, 1)
                wait(pe, h_kept, b, KT)
                wait(pe, max_step, b, 1)
                for j in range(KT):
                    wait(pe, prob_ready, b, j + 1)
                    for h in range(2):
                        ph = prob[:, j % 2, h]
                        nc.tensor.matmul(den_bank[:, h, 0:HALF], ones[:, :], ph, start=(j == 0), stop=(j == KT - 1))
                        for k in range(KC):
                            last = nc.tensor.matmul(bank4[:, k, h, 0:HALF], h_sb[:, j, k * P:(k + 1) * P], ph,
                                                    start=(j == 0), stop=(j == KT - 1))
                    last.then_inc(prob_used.sem, 1)

        @block.scalar
        def _(act):
            nc.scalar.preload_act_table_set("natural_log_exp_and_others")
            act.wait_ge(w_turned, 1)
            nc.scalar.copy(w_t[:, :, :], den_bank[:, :, 0:DM]).then_inc(w_t_kept, 1)
            act.wait_ge(wa_made, 1)
            nc.scalar.copy(wa[:, :, :, :], f1_bank[:, :, 0:KC * P].rearrange("p v (k n) -> p v k n", k=KC)
                           ).then_inc(wa_kept, 1)
            act.wait_ge(wa_kept, 1)
            nc.scalar.copy(w_h[:, :, DM], wa[:, 1, :, 0]).then_inc(wa_kept, 1)
            with act.Fori(0, NB) as b:
                wait(act, centred, b, 2)
                nc.scalar.activation(sq[:, :, :, :], z[:, :, :, :], ACT.Square).then_inc(squared.sem, 1)
                wait(act, var_made, b, 1)
                nc.scalar.activation(rstd[:, :, :], den, ACT.Ln, bias=eps5[:, 0:1]).then_inc(rstd_step.sem, 1)
                wait(act, rstd_step, b, 1)
                nc.scalar.activation(rstd[:, :, :], rstd[:, :, :], ACT.Exp, scale=-0.5).then_inc(rstd_step.sem, 1)
                wait(act, prob_used, b, 0)
                for j in range(KT):
                    wait(act, h_made, b, j + 1)
                    nc.scalar.copy(h_sb[:, j, :], h_bank[j % 2]).then_inc(h_kept.sem, 1)
                for j in range(KT):
                    wait(act, score_step, b, 3 * j + 3)
                    wait(act, prob_used, b, j - 1)
                    nc.scalar.activation(prob[:, j % 2], score[:, j % 2], ACT.Exp).then_inc(prob_ready.sem, 1)
                wait(act, hp_step, b, 2)
                nc.scalar.activation(neg[:, :, :, :], neg[:, :, :, :], ACT.Exp).then_inc(neg_exp.sem, 1)

        @block.vector
        def _(dve):
            with dve.Fori(0, NB) as b:
                t = tokens(b)
                wait(dve, mean_made, b, 1)
                for h in range(2):
                    nc.vector.tensor_tensor(z[:, :, h], t[:, :, h],
                                            den_bank[:, h, 0:HALF].unsqueeze(1).broadcast_to([P, KC, HALF]),
                                            ALU.subtract).then_inc(centred.sem, 1)
                wait(dve, rstd_step, b, 2)
                wait(dve, squared, b, 1)
                nc.vector.tensor_tensor(z[:, :, :, :], z[:, :, :, :], each_block(rstd[:, :, :]), ALU.mult
                                        ).then_inc(z_ready.sem, 1)
                wait(dve, f_made, b, 1)
                nc.vector.tensor_reduce(f2_max[:, :], den, AX.XY, ALU.max).then_inc(max_step.sem, 1)
                wait(dve, max_step, b, 1)
                nc.vector.tensor_scalar(row_max[:, :, :], f1, f2_max[:, 0:1], None, ALU.add).then_inc(max_step.sem, 1)
                wait(dve, max_step, b, 2)
                nc.vector.scalar_tensor_tensor(out=row_max[:, :, :], in0=row_max[:, :, :], scalar=0.01,
                                               in1=row_max[:, :, :], op0=ALU.mult, op1=ALU.max
                                               ).then_inc(max_step.sem, 1)
                wait(dve, max_step, b, 3)
                wait(dve, h_kept, b, KT)
                for j in range(KT):
                    sc = score[:, j % 2]
                    wait(dve, prob_ready, b, j - 1)
                    nc.vector.tensor_scalar(sc, f1, h_sb[:, j, DM:DM + 1], None, ALU.add).then_inc(score_step.sem, 1)
                    wait(dve, score_step, b, 3 * j + 1)
                    nc.vector.scalar_tensor_tensor(out=sc, in0=sc, scalar=0.01, in1=sc, op0=ALU.mult, op1=ALU.max
                                                   ).then_inc(score_step.sem, 1)
                    wait(dve, score_step, b, 3 * j + 2)
                    nc.vector.tensor_tensor(sc, sc, row_max[:, :, :], ALU.subtract).then_inc(score_step.sem, 1)
                wait(dve, prob_used, b, KT)
                nc.vector.reciprocal(rden[:, :, :], den).then_inc(rden_ready.sem, 1)
                wait(dve, rden_ready, b, 1)
                nc.vector.tensor_tensor(hp[:, :, :, :], outp, each_block(rden[:, :, :]), ALU.mult
                                        ).then_inc(hp_step.sem, 1)
                wait(dve, hp_step, b, 1)
                nc.vector.tensor_scalar(neg[:, :, :, :], hp[:, :, :, :], 0.0, None, ALU.min).then_inc(hp_step.sem, 1)
                nc.vector.scalar_tensor_tensor(out=hp[:, :, :, :], in0=hp[:, :, :, :], scalar=0.0, in1=t,
                                               op0=ALU.max, op1=ALU.add).then_inc(hp_step.sem, 1)
                wait(dve, neg_exp, b, 1)
                wait(dve, hp_step, b, 3)
                nc.vector.tensor_scalar(neg[:, :, :, :], neg[:, :, :, :], -1.0, None, ALU.add
                                        ).then_inc(x_added.sem, 1)
                wait(dve, x_added, b, 1)
                nc.vector.tensor_tensor(t, hp[:, :, :, :], neg[:, :, :, :], ALU.add).then_inc(x_added.sem, 1)


def experts(nc, X, ident, eps5, w, out):
    TILES = HALF // P
    with ExitStack() as ctx:
        def sb(name, shape, dt=F32):
            return ctx.enter_context(nc.sbuf_tensor(name, shape, dt))

        def sem(name, per=1):
            return Sem(ctx.enter_context(nc.semaphore(name)), per)

        mean_w = sb("moe_mean_w", [P, P])
        router = sb("router", [NE, DM])
        router_t = sb("router_t", [P, KC, NE])
        w1 = sb("w1", [P, NE, KC, DM])
        w2 = sb("w2", [P, NE, KC, DM])
        b1 = sb("b1", [P, NE, KC])
        b2 = sb("b2", [NE, DM])
        number = sb("number", [P, NE])
        held = sb("held", [P, KC, HALF])
        n = sb("n", [P, KC, HALF])
        sq = sb("moe_sq", [P, KC, HALF])
        rstd = sb("moe_rstd", [P, HALF])
        logit = sb("logit", [P, TILES, NE])
        best = sb("best", [P, TILES, 8])
        best_at = sb("best_at", [P, TILES, 8], U32)
        at_f = sb("at_f", [P, TILES, 2])
        top = sb("top", [P, TILES, 2])
        total = sb("total", [P, TILES])
        weight = sb("weight", [P, TILES, NE])
        other = sb("other", [P, TILES, NE])
        weight_t = sb("weight_t", [NE, HALF])
        hg = sb("hg", [P, 2, KC, HALF])
        acc = sb("acc", [P, TILES, DM])
        h_bank = ctx.enter_context(nc.psum_tensor("h_bank", [P, 2, KC, 512], F32))
        y_bank = ctx.enter_context(nc.psum_tensor("y_out", [P, 2 * 512], F32))
        stat = ctx.enter_context(nc.psum_tensor("stat", [P, 512], F32))
        small = ctx.enter_context(nc.psum_tensor("small", [P, 512], F32))
        y_tile = [y_bank[:, i * DM:(i + 1) * DM] for i in range(TILES)]
        y_all = y_bank[:, 0:TILES * DM].rearrange("p (t n) -> p t n", t=TILES)

        loaded = ctx.enter_context(nc.semaphore("moe_loaded"))
        consts_set = ctx.enter_context(nc.semaphore("moe_consts_set"))
        router_turned = ctx.enter_context(nc.semaphore("router_turned"))
        router_kept = ctx.enter_context(nc.semaphore("router_kept"))
        passed = ctx.enter_context(nc.semaphore("moe_waits_passed"))
        x_held = sem("x_held")
        mean_made = sem("moe_mean_made")
        centred = sem("moe_centred")
        squared = sem("moe_squared")
        var_made = sem("moe_var_made")
        rstd_step = sem("moe_rstd_step", 2)
        n_ready = sem("n_ready")
        logits_made = sem("logits_made")
        route_step = sem("route_step", 13)
        top_exp = sem("top_exp")
        total_step = sem("total_step", 2)
        weight_ready = sem("weight_ready")
        weight_turned = sem("weight_turned")
        weight_t_kept = sem("weight_t_kept")
        x_turned = sem("x_turned")
        acc_step = sem("acc_step", 2 + TILES * NE)
        bias_made = sem("bias_made")
        h_made = sem("moe_h_made", NE)
        h_done = sem("moe_h_done", KC * NE)
        y_made = sem("y_made", NE)
        stored = sem("stored", 16)
        sems = [x_held, mean_made, centred, squared, var_made, rstd_step, n_ready, logits_made, route_step, top_exp, total_step,
                weight_ready, weight_turned, weight_t_kept, x_turned, acc_step, bias_made, h_made, h_done,
                y_made, stored]
        ctx.enter_context(nc.allow_non_contiguous_dma(reason="biases of a few thousand values"))
        block = ctx.enter_context(nc.Block())

        def wait(eng, s, g, k):
            eng.wait_ge(s.sem, s.at(g, k))

        def tokens(g):
            return X[:, :, :].rearrange("p k (g n) -> p g k n", n=HALF)[:, g]

        @block.sync
        def _(sp):
            for s in sems:
                s.start(sp)
            sp.dma_start(router[:, :], w["router_w"]).then_inc(loaded, 16)
            sp.dma_start(b1[:, :, :], w["b1"].rearrange("e (k p) -> p e k", p=P)).then_inc(loaded, 16)
            sp.dma_start(b2[:, :], w["b2"]).then_inc(loaded, 16)
            sp.dma_start(w1[:, :, :, :], w["w1"].rearrange("e (k p) n -> p e k n", p=P)).then_inc(loaded, 16)
            sp.dma_start(w2[:, :, :, :], w["w2"].rearrange("e (k p) n -> p e k n", p=P)).then_inc(loaded, 16)
            rows = out.rearrange("b o t d -> (b o t) d").rearrange("(g i p) d -> g p i d", p=P, i=TILES)
            with sp.Fori(0, CHUNKS) as g:
                wait_apart(sp, acc_step, g, 2 + TILES * NE, passed)
                sp.dma_start(rows[g], acc[:, :, :]).then_inc(stored.sem, 16)
            sp.wait_ge(stored.sem, stored.at(CHUNKS, 0))

        @block.gpsimd
        def _(pool):
            nc.gpsimd.memset(mean_w[:, :], 1.0 / DM).then_inc(consts_set, 1)
            nc.gpsimd.iota(number[:, :], pattern=[[1, NE]], base=0, channel_multiplier=0,
                           allow_small_or_imprecise_dtypes=True).then_inc(consts_set, 1)
            with pool.Fori(0, CHUNKS) as g:
                wait(pool, x_turned, g, 0)
                wait(pool, n_ready, g, 1)
                nc.gpsimd.tensor_tensor(held[:, :, :], tokens(g), n[:, :, :], ALU.add).then_inc(x_held.sem, 1)

        @block.tensor
        def _(pe):
            pe.wait_ge(consts_set, 2)
            pe.wait_ge(loaded, 16 * 5)
            for k in range(KC):
                last = nc.tensor.transpose(small[:, k * NE:(k + 1) * NE], router[:, k * P:(k + 1) * P],
                                           ident[0:NE, 0:NE])
            last.then_inc(router_turned, 1)
            pe.wait_ge(router_kept, 1)
            with pe.Fori(0, CHUNKS) as g:
                t = tokens(g)
                wait(pe, rstd_step, g, 0)
                for k in range(KC):
                    last = nc.tensor.matmul(stat[:, 0:HALF], mean_w[:, :], t[:, k], start=(k == 0), stop=(k == KC - 1))
                last.then_inc(mean_made.sem, 1)
                wait(pe, squared, g, 1)
                for k in range(KC):
                    last = nc.tensor.matmul(stat[:, 0:HALF], mean_w[:, :], sq[:, k, :],
                                            start=(k == 0), stop=(k == KC - 1))
                last.then_inc(var_made.sem, 1)
                wait(pe, n_ready, g, 1)
                wait(pe, weight_t_kept, g, 0)
                for i in range(TILES):
                    for k in range(KC):
                        last = nc.tensor.matmul(small[:, i * NE:(i + 1) * NE], n[:, k, i * P:(i + 1) * P],
                                                router_t[:, k, :], start=(k == 0), stop=(k == KC - 1))
                last.then_inc(logits_made.sem, 1)

                def hidden(e):
                    wait(pe, h_done, g, KC * (e - 1))
                    for m in range(KC):
                        for k in range(KC):
                            last = nc.tensor.matmul(h_bank[:, e % 2, m, 0:HALF], w1[:, e, k, m * P:(m + 1) * P],
                                                    n[:, k, :], start=(k == 0), stop=(k == KC - 1))
                    last.then_inc(h_made.sem, 1)

                hidden(0)
                wait(pe, acc_step, g, 0)
                wait(pe, x_held, g, 1)
                for i in range(TILES):
                    for k in range(KC):
                        last = nc.tensor.transpose(y_tile[i][:, k * P:(k + 1) * P], held[:, k, i * P:(i + 1) * P],
                                                   ident[:, :])
                last.then_inc(x_turned.sem, 1)
                wait(pe, weight_ready, g, 1)
                for i in range(TILES):
                    last = nc.tensor.transpose(small[0:NE, i * P:(i + 1) * P], weight[:, i, :], ident[:, :])
                last.then_inc(weight_turned.sem, 1)
                hidden(1)
                wait(pe, weight_t_kept, g, 1)
                wait(pe, acc_step, g, 1)
                for i in range(TILES):
                    last = nc.tensor.matmul(y_tile[i], weight_t[:, i * P:(i + 1) * P], b2[:, :], start=True, stop=True)
                last.then_inc(bias_made.sem, 1)
                for e in range(NE):
                    wait(pe, h_done, g, KC * (e + 1))
                    wait(pe, acc_step, g, 2 + TILES * e)
                    for i in range(TILES):
                        for k in range(KC):
                            last = nc.tensor.matmul(y_tile[i], hg[:, e % 2, k, i * P:(i + 1) * P], w2[:, e, k, :],
                                                    start=(k == 0), stop=(k == KC - 1))
                    last.then_inc(y_made.sem, 1)
                    if e + 2 < NE:
                        hidden(e + 2)

        @block.scalar
        def _(act):
            act.wait_ge(router_turned, 1)
            nc.scalar.copy(router_t[:, :, :], small[:, 0:KC * NE].rearrange("p (k e) -> p k e", k=KC)
                           ).then_inc(router_kept, 1)
            with act.Fori(0, CHUNKS) as g:
                wait(act, centred, g, 1)
                nc.scalar.activation(sq[:, :, :], n[:, :, :], ACT.Square).then_inc(squared.sem, 1)
                wait(act, var_made, g, 1)
                nc.scalar.activation(rstd[:, :], stat[:, 0:HALF], ACT.Ln, bias=eps5[:, 0:1]).then_inc(rstd_step.sem, 1)
                wait(act, rstd_step, g, 1)
                nc.scalar.activation(rstd[:, :], rstd[:, :], ACT.Exp, scale=-0.5).then_inc(rstd_step.sem, 1)
                wait(act, route_step, g, 7)
                nc.scalar.activation(logit[:, :, :], logit[:, :, :], ACT.Exp).then_inc(top_exp.sem, 1)
                for e in range(NE):
                    wait(act, h_made, g, e + 1)
                    wait(act, y_made, g, e - 1)
                    for m in range(KC):
                        nc.scalar.activation(hg[:, e % 2, m, :], h_bank[:, e % 2, m, 0:HALF], ACT.Gelu,
                                             bias=b1[:, e, m:m + 1]).then_inc(h_done.sem, 1)

        @block.vector
        def _(dve):
            dve.wait_ge(consts_set, 2)
            with dve.Fori(0, CHUNKS) as g:
                t = tokens(g)
                wait(dve, h_made, g, 0)
                wait(dve, x_held, g, 0)
                wait(dve, mean_made, g, 1)
                nc.vector.tensor_tensor(n[:, :, :], t, stat[:, 0:HALF].unsqueeze(1).broadcast_to([P, KC, HALF]),
                                        ALU.subtract).then_inc(centred.sem, 1)
                wait(dve, rstd_step, g, 2)
                wait(dve, squared, g, 1)
                nc.vector.tensor_tensor(n[:, :, :], n[:, :, :], rstd[:, :].unsqueeze(1).broadcast_to([P, KC, HALF]),
                                        ALU.mult).then_inc(n_ready.sem, 1)
                wait(dve, logits_made, g, 1)
                nc.vector.tensor_copy(logit[:, :, :], small[:, 0:TILES * NE].rearrange("p (i e) -> p i e", i=TILES)
                                      ).then_inc(route_step.sem, 1)
                wait_apart(dve, route_step, g, 1, passed)
                for i in range(TILES):
                    last = nc.vector.max(best[:, i, :], logit[:, i, :])
                last.then_inc(route_step.sem, 1)
                wait_apart(dve, route_step, g, 2, passed)
                for i in range(TILES):
                    last = nc.vector.max_index(best_at[:, i, :], best[:, i, :], logit[:, i, :])
                last.then_inc(route_step.sem, 1)
                wait(dve, route_step, g, 3)
                nc.vector.tensor_copy(at_f[:, :, :], best_at[:, :, 0:2]).then_inc(route_step.sem, 1)
                nc.vector.tensor_tensor(logit[:, :, :], logit[:, :, :], best[:, :, 0:1].broadcast_to([P, TILES, NE]),
                                        ALU.subtract).then_inc(route_step.sem, 3)
                wait(dve, top_exp, g, 1)
                nc.vector.tensor_reduce(total[:, :], logit[:, :, :], AX.X, ALU.add).then_inc(route_step.sem, 1)
                wait(dve, route_step, g, 8)
                nc.vector.reciprocal(total[:, :], total[:, :]).then_inc(route_step.sem, 1)
                wait(dve, route_step, g, 9)
                nc.vector.tensor_tensor(logit[:, :, :], logit[:, :, :],
                                        total[:, :].unsqueeze(2).broadcast_to([P, TILES, NE]), ALU.mult
                                        ).then_inc(route_step.sem, 1)
                wait(dve, route_step, g, 10)
                for i in range(TILES):
                    for r, dst in ((0, weight), (1, other)):
                        last = nc.vector.scalar_tensor_tensor(out=dst[:, i, :], in0=number[:, :],
                                                              scalar=at_f[:, i, r:r + 1], in1=logit[:, i, :],
                                                              op0=ALU.is_equal, op1=ALU.mult)
                last.then_inc(route_step.sem, 1)
                wait(dve, route_step, g, 11)
                wait(dve, weight_turned, g, 0)
                nc.vector.tensor_tensor(other[:, :, :], weight[:, :, :], other[:, :, :], ALU.add
                                        ).then_inc(route_step.sem, 1)
                wait(dve, route_step, g, 12)
                nc.vector.tensor_reduce(total[:, :], other[:, :, :], AX.X, ALU.add).then_inc(route_step.sem, 1)
                wait(dve, route_step, g, 13)
                nc.vector.tensor_scalar(total[:, :], total[:, :], 1e-12, None, ALU.max).then_inc(total_step.sem, 1)
                wait(dve, total_step, g, 1)
                nc.vector.reciprocal(total[:, :], total[:, :]).then_inc(total_step.sem, 1)
                wait(dve, total_step, g, 2)
                nc.vector.tensor_tensor(weight[:, :, :], other[:, :, :],
                                        total[:, :].unsqueeze(2).broadcast_to([P, TILES, NE]), ALU.mult
                                        ).then_inc(weight_ready.sem, 1)
                wait(dve, stored, g, 0)
                wait(dve, x_turned, g, 1)
                nc.vector.tensor_copy(acc[:, :, :], y_all).then_inc(acc_step.sem, 1)
                wait(dve, weight_turned, g, 1)
                nc.vector.tensor_copy(weight_t[:, :], small[0:NE, 0:HALF]).then_inc(weight_t_kept.sem, 1)
                wait(dve, bias_made, g, 1)
                wait(dve, acc_step, g, 1)
                nc.vector.tensor_tensor(acc[:, :, :], acc[:, :, :], y_all, ALU.add).then_inc(acc_step.sem, 1)
                wait(dve, weight_ready, g, 1)
                for e in range(NE):
                    wait(dve, y_made, g, e + 1)
                    wait(dve, acc_step, g, 2 + TILES * e)
                    for i in range(TILES):
                        nc.vector.scalar_tensor_tensor(out=acc[:, i, :], in0=y_tile[i], scalar=weight[:, i, e:e + 1],
                                                       in1=acc[:, i, :], op0=ALU.mult, op1=ALU.add
                                                       ).then_inc(acc_step.sem, 1)


def conv_attn_hybrid(nc, x, pe, ln_w, ln_b, in_proj, conv_w, conv_b, x_proj, dt_w, dt_b, A_log, Dp, out_proj,
                     W, a, router_w, w1, b1, w2, b2, out):
    with ExitStack() as ctx:
        X = ctx.enter_context(nc.sbuf_tensor("X", [P, KC, TOK], F32))
        ident = ctx.enter_context(nc.sbuf_tensor("ident", [P, P], F32))
        eps5 = ctx.enter_context(nc.sbuf_tensor("eps5", [P, 1], F32))
        load_tokens(nc, x, pe, X, ident, eps5)
        mamba(nc, X, ident, eps5, dict(ln_w=ln_w, ln_b=ln_b, in_proj=in_proj, conv_w=conv_w, conv_b=conv_b,
                                       x_proj=x_proj, dt_w=dt_w, dt_b=dt_b, A_log=A_log, Dp=Dp, out_proj=out_proj))
        attention(nc, X, ident, eps5, dict(W=W, a=a))
        experts(nc, X, ident, eps5, dict(router_w=router_w, w1=w1, b1=b1, w2=w2, b2=b2), out)


_INS = ["x"] + ["L0_conv_" + n for n in ("pe", "ln_w", "ln_b", "in_proj", "conv_w", "conv_b", "x_proj", "dt_w",
                                         "dt_b", "A_log", "Dp", "out_proj")] + \
    ["L1_attn_W", "L1_attn_a", "L1_ffn_router_w", "L1_ffn_w1", "L1_ffn_b1", "L1_ffn_w2", "L1_ffn_b2"]


def kernel(**inputs):
    import numpy as _np
    import concourse.bacc as _bacc
    from concourse import mybir as _mybir
    from concourse.bass_utils import run_bass_kernel_spmd as _run

    nc = _bacc.Bacc("TRN2", target_bir_lowering=False, num_devices=1)
    arrays, args = {}, []
    for name in _INS:
        arr = _np.ascontiguousarray(inputs[name])
        arrays[f"in_{name}"] = arr
        args.append(nc.dram_tensor(f"in_{name}", arr.shape, _mybir.dt.from_np(arr.dtype), kind="ExternalInput").ap())
    out = nc.dram_tensor("out_tokens", (NB, NO, NT, DM), _mybir.dt.float32, kind="ExternalOutput").ap()
    conv_attn_hybrid(nc, *args, out)
    r = _run(nc, [arrays], core_ids=[0])
    return r.results[0]["out_tokens"]
```

```python
import concourse.bass as bass
from concourse import mybir
from contextlib import ExitStack

F32 = mybir.dt.float32
BF16 = mybir.dt.bfloat16
U32 = mybir.dt.uint32
ALU = mybir.AluOpType
ACT = mybir.ActivationFunctionType
AX = mybir.AxisListType
P = 128

NB, NO, NT, DM = 8, 12, 64, 256
SEQ = NO * NT
TOK = NB * SEQ
NL = 2
DI = 2 * DM
DS = 16
DCONV = 4
DTR = DM // 16
HALF = SEQ // 2
KC = DM // P
MC = DI // P
XPW = DTR + 2 * DS
NE = 8
CHUNKS = 2 * NB
STAGES = 4


PE_X = {0: (0, 1), 1: (2, 3)}
READ_X = {1: (0, 1), 2: (2, 3)}
CLAMP_X, ACT_X, X_GATE = 3, (4, 5, 5), 7
PE_Z = {13: (0, 1), 14: (2, 3)}
READ_Z = {14: (0, 1), 15: (2, 3)}
ACT_Z, Z_GATE = (0, 1, 2), 4
GATE = 2
PE_LOW, READ_LOW, SPLIT, ROUND_REST = 6, 7, (9, 11), (10, 12)
PE_STEP = {7: (0, 1), 8: (2, 3)}
READ_STEP = {8: (0, 1), 9: (2, 3)}
STEP_EXP, STEP_U, STEP_CORR, STEP_REST, STEP_LN = 10, 11, 12, 12, 13
DELTA, DU = 15, 15
PE_OUT, READ_OUT = {2: 0, 3: 1}, {3: 0, 4: 1}
PE_MEAN, CENTRE, SQUARE, PE_VAR, RSTD, NORM = 5, 6, 7, 7, 8, 13


class Sem:

    def __init__(self, sem, per, ahead=2):
        self.sem, self.per, self.ahead = sem, per, ahead

    def at(self, period, n):
        return (period + self.ahead) * self.per + n

    def start(self, eng):
        eng.sem_inc(self.sem, self.ahead * self.per)


def wait_apart(eng, s, period, n, passed):
    eng.wait_ge(s.sem, s.at(period, n))
    eng.sem_inc(passed, 1)


def load_tokens(nc, x, pe, X, ident, eps5):
    TILES = TOK // P
    GROUP = 4
    with ExitStack() as ctx:
        raw = ctx.enter_context(nc.sbuf_tensor("raw_tokens", [P, GROUP, DM], F32))
        pos = ctx.enter_context(nc.sbuf_tensor("pos_tokens", [P, DM], F32))
        turned = [ctx.enter_context(nc.psum_tensor(f"turned{i}", [P, 512], F32)) for i in range(2)]
        sem = lambda n: ctx.enter_context(nc.semaphore(n))
        pos_loaded = sem("pos_loaded")
        raw_loaded = [sem(f"raw_loaded{i}") for i in range(GROUP)]
        pos_added = sem("pos_added")
        tile_turned = sem("tile_turned")
        tile_kept = sem("tile_kept")
        ident_zeroed = sem("ident_zeroed")
        ident_ready = sem("ident_ready")
        block = ctx.enter_context(nc.Block())
        xt = x.rearrange("b o t d -> (b o t) d").rearrange("(n p) d -> p n d", p=P)

        @block.sync
        def _(sp):
            for i in range(P // NT):
                sp.dma_start(pos[i * NT:(i + 1) * NT, :], pe).then_inc(pos_loaded, 16)
            with sp.Fori(0, TILES // GROUP) as g:
                for i in range(GROUP):
                    sp.wait_ge(tile_turned, g * GROUP + i + 1)
                    sp.dma_start(raw[:, i, :], xt[:, g * GROUP + i, :]).then_inc(raw_loaded[i], 16)

        @block.gpsimd
        def _(pool):
            nc.gpsimd.memset(ident[:, :], 0.0).then_inc(ident_zeroed, 1)
            nc.gpsimd.memset(eps5[:, :], 1e-5)
            pool.wait_ge(ident_zeroed, 1)
            nc.gpsimd.affine_select(out=ident[:, :], in_=ident[:, :], compare_op=ALU.not_equal, fill=1.0,
                                    base=0, pattern=[[-1, P]], channel_multiplier=1).then_inc(ident_ready, 1)

        @block.vector
        def _(dve):
            dve.wait_ge(pos_loaded, 16 * (P // NT))
            with dve.Fori(0, TILES // GROUP) as g:
                for i in range(GROUP):
                    dve.wait_ge(raw_loaded[i], g * 16 + 16)
                    nc.vector.tensor_tensor(raw[:, i, :], raw[:, i, :], pos[:, :], ALU.add).then_inc(pos_added, 1)

        @block.tensor
        def _(pe_):
            pe_.wait_ge(ident_ready, 1)
            pe_.sem_inc(tile_turned, GROUP)
            with pe_.Fori(0, TILES // GROUP) as g:
                for i in range(GROUP):
                    pe_.wait_ge(pos_added, g * GROUP + i + 1)
                    pe_.wait_ge(tile_kept, g * GROUP + i + 1)
                    for k in range(KC):
                        last = nc.tensor.transpose(turned[i % 2][:, k * P:(k + 1) * P],
                                                   raw[:, i, k * P:(k + 1) * P], ident[:, :])
                    last.then_inc(tile_turned, 1)

        @block.scalar
        def _(act):
            act.sem_inc(tile_kept, 2)
            xw = X[:, :, :].rearrange("p k (g n) -> p g k n", n=GROUP * P)
            with act.Fori(0, TILES // GROUP) as g:
                for i in range(GROUP):
                    act.wait_ge(tile_turned, g * GROUP + i + 1 + GROUP)
                    nc.scalar.copy(xw[:, g, :, i * P:(i + 1) * P],
                                   turned[i % 2][:, 0:KC * P].rearrange("p (k n) -> p k n", k=KC)
                                   ).then_inc(tile_kept, 1)


def mamba(nc, X, ident, eps5, w):
    with ExitStack() as ctx:
        def sb(name, shape, dt=F32):
            return ctx.enter_context(nc.sbuf_tensor(name, shape, dt))

        def sem(name, per, ahead=2):
            s = Sem(ctx.enter_context(nc.semaphore(name)), per, ahead)
            all_sems.append(s)
            return s

        all_sems = []

        w_in = sb("w_in", [P, 2, KC, 2 * DI])
        w_out = sb("w_out", [P, 2, MC, DM])
        w_low = sb("w_low", [P, 2, MC, 6 * DS + DTR])
        w_step = sb("w_step", [6 * DS + DTR, 2, DI])[6 * DS:]
        taps = sb("taps", [P, 2, MC, DCONV])
        conv_bias = sb("conv_bias", [P, 2, MC])
        step_bias = sb("step_bias", [P, 2, MC])
        skip = sb("skip", [P, 2, MC])
        decay = sb("decay", [P, 2, MC, DS])
        ln_w = sb("ln_w", [P, KC])
        ln_b = sb("ln_b", [P, KC])
        mean_w = sb("mean_w", [P, P])
        pick = sb("pick", [6 * DS, 2 * DS], BF16)

        a = sb("a", [P, MC, HALF])
        xin = sb("xin", [P, MC, DCONV - 1 + HALF])
        xc = sb("xc", [P, 2, MC, HALF])
        sz = sb("sz", [P, 2, MC, HALF])
        delta = sb("delta", [P, 2, MC, HALF])
        du = sb("du", [P, 2, MC, HALF])
        tmp = sb("tmp", [P, MC, HALF])
        low = sb("low", [6 * DS + DTR, HALF])
        bc_rest, dt_low = low[0:6 * DS], low[6 * DS:]
        bc_parts = sb("bc_parts", [6 * DS, 2, HALF], BF16)
        b_wide = sb("b_wide", [P, 2, HALF])
        dbx = sb("dbx", [P, 3, MC, HALF])
        hs = sb("hs", [P, 2, MC, HALF])
        hc = sb("hc", [P, 2, MC, HALF])
        carry = sb("carry", [P, DS, MC])
        fo = sb("fo", [P, KC, HALF])
        fwd_in = sb("fwd_in", [P, KC, HALF])
        res_in = sb("res_in", [P, 2, KC, HALF])
        sq = fwd_in
        rstd = fwd_in[:, 0, :]

        fwd_dram = nc.dram_tensor("fwd_scratch", [P, CHUNKS, KC, HALF], F32, kind="Internal").ap()
        res_dram = nc.dram_tensor("res_scratch", [P, KC, TOK], F32, kind="Internal").ap()

        bank = lambda name: ctx.enter_context(nc.psum_tensor(name, [P, 512], F32))
        y_bank = ctx.enter_context(nc.psum_tensor("y_bank", [P, MC * HALF], F32))
        b_bank = bank("b_bank")
        c_bank = bank("c_bank")
        prep_bank = [bank(f"prep_bank{i}") for i in range(2)]
        close_bank = bank("close_bank")

        CLOSE = [("out", k) for k in range(KC)] + [("mean", 0), ("var", 0)]
        USE = {what: n + 1 for n, what in enumerate(CLOSE)}
        NW = 12

        weights_loaded = sem("weights_loaded", 16 * NW)
        decay_step = sem("decay_step", 2)
        x_made = sem("x_made", MC)
        x_read = sem("x_read", MC)
        z_made = sem("z_made", MC)
        z_read = sem("z_read", MC)
        low_made = sem("low_made", 1)
        dt_read = sem("dt_read", 1)
        step_made = sem("step_made", MC)
        step_read = sem("step_read", MC)
        close_full = sem("close_full", len(CLOSE))
        close_free = sem("close_free", len(CLOSE))
        last_tap = sem("last_tap", MC)
        conv_step = sem("conv_step", MC * (DCONV - 1))
        xpre_ready = sem("xpre_ready", 1)
        halo_ready = sem("halo_ready", 1)
        z_sig = sem("z_sig", 3)
        x_sig = sem("x_sig", 3)
        sz_ready = sem("sz_ready", 1)
        xc_ready = sem("xc_ready", 1)
        split_step = sem("split_step", 6)
        step_abs = sem("step_abs", 1)
        step_exp = sem("step_exp", 1)
        step_u = sem("step_u", 1)
        step_corr = sem("step_corr", 1)
        step_rest = sem("step_rest", 1)
        step_ln = sem("step_ln", 1)
        delta_ready = sem("delta_ready", 1)
        du_ready = sem("du_ready", 1)
        a_ready = sem("a_ready", DS * MC)
        scan_done = sem("scan_done", DS * MC)
        b_made = sem("b_made", DS)
        b_copied = sem("b_copied", DS)
        dbx_ready = sem("dbx_ready", DS)
        c_ready = sem("c_ready", DS)
        cmul_done = sem("cmul_done", DS)
        y_added = sem("y_added", DS)
        y_read = sem("y_read", MC)
        yg_ready = sem("yg_ready", 1)
        carry_saved = sem("carry_saved", DS)
        x_written = sem("x_written", 1, ahead=NB + 1)
        fwd_stored = sem("fwd_stored", 16)
        fwd_loaded = sem("fwd_loaded", 16)
        centred = sem("centred", 1)
        sq_ready = sem("sq_ready", 1)
        rstd_ready = sem("rstd_ready", 1)
        norm_step = sem("norm_step", 4)
        res_stored = sem("res_stored", 16)
        res_loaded = sem("res_loaded", 16)
        plain = lambda name: ctx.enter_context(nc.semaphore(name))
        ln_loaded = plain("ln_loaded")
        ln_halved = plain("ln_halved")
        halo_zeroed = plain("halo_zeroed")
        passed = plain("waits_passed")
        mean_w_set = plain("mean_w_set")
        pick_zeroed = plain("pick_zeroed")
        pick_set = plain("pick_set")

        ctx.enter_context(nc.allow_non_contiguous_dma(reason="vectors of a few hundred values"))
        block = ctx.enter_context(nc.Block())

        LOW = -44.0

        class Chunk:

            def __init__(self, l, st, b, half):
                self.st, self.b, self.half = st, b, half
                self.blk, self.back = divmod(st, 2)
                self.nh = 1 - half if self.back else half
                self.g = l * (STAGES * CHUNKS) + b * 2 + (st * CHUNKS + half)
                self.batch = l * (STAGES * NB) + b + st * NB
                self.stage = l * STAGES + st
                self.dir = l * (2 * CHUNKS) + b * 2 + (self.blk * CHUNKS + half)
                self.dir_start = l * (2 * CHUNKS) + self.blk * CHUNKS
                self.layer = l * CHUNKS + b * 2 + half
                self.layer_start = l * CHUNKS
                self.layer_batch = l * NB + b

        def rounds(eng, start, round_, end):
            start(Chunk(0, 0, 0, 0))
            with eng.Fori(0, NL) as l:
                for st in range(STAGES):
                    round_(Chunk(l, st, 0, 0), Chunk(l, st, 0, 1), Chunk(l, st - 1, NB - 1, 1) if st else None)
                    with eng.Fori(0, NB - 1) as b:
                        round_(Chunk(l, st, b, 1), Chunk(l, st, b + 1, 0), Chunk(l, st, b, 0))
                        round_(Chunk(l, st, b + 1, 0), Chunk(l, st, b + 1, 1), Chunk(l, st, b, 1))
                    after = Chunk(l, st + 1, 0, 0) if st < STAGES - 1 else Chunk(l + 1, 0, 0, 0)
                    round_(Chunk(l, st, NB - 1, 1), after, Chunk(l, st, NB - 1, 0))
                end(Chunk(l, STAGES - 1, NB - 1, 1))

        def half_of(t, b, nh):
            return t.rearrange("p k (b h n) -> p b h k n", b=NB, h=2)[:, b, nh]

        def tokens(ch, k):
            if ch.blk == 0:
                return half_of(X[:, :, :], ch.b, ch.nh)[:, k]
            return X[:, :, :].rearrange("p k (b o h t) -> p b h k t o", b=NB, o=NO, h=2)[:, ch.b, ch.nh, k]

        def projected(ch, m):
            src = prep_bank[m % 2][:, 0:HALF]
            return src[:, ::-1] if ch.back else src

        def dbx_buffer(ch, s):
            return dbx[:, (s + ch.half) % 3]

        def wide(ap, blocks=MC):
            return ap.unsqueeze(1).broadcast_to([P, blocks, HALF])

        def wait(eng, s, period, n):
            eng.wait_ge(s.sem, s.at(period, n))

        @block.sync
        def _(sp):
            for s in all_sems:
                s.start(sp)
            sp.dma_start(ln_w[:, :], w["ln_w"].rearrange("(k p) -> p k", p=P)).then_inc(ln_loaded, 16)
            sp.dma_start(ln_b[:, :], w["ln_b"].rearrange("(k p) -> p k", p=P)).then_inc(ln_loaded, 16)

            def load_weights(l, st):
                blk, back = divmod(st, 2)
                at = lambda name: w[name][l, blk, back]
                x_proj = at("x_proj").rearrange("(k p) n -> p k n", p=P)
                loads = [
                    (w_in[:, back], at("in_proj").rearrange("(k p) n -> p k n", p=P)),
                    (taps[:, back], at("conv_w").rearrange("(k p) n -> p k n", p=P)),
                    (conv_bias[:, back], at("conv_b").rearrange("(k p) -> p k", p=P)),
                    (w_low[:, back, :, 6 * DS:], x_proj[:, :, 0:DTR]),
                    (w_step[:, back], at("dt_w")),
                    (step_bias[:, back], at("dt_b").rearrange("(k p) -> p k", p=P)),
                    (decay[:, back], at("A_log").rearrange("(k p) n -> p k n", p=P)),
                    (skip[:, back], at("Dp").rearrange("(k p) -> p k", p=P)),
                    (w_out[:, back], at("out_proj").rearrange("(k p) n -> p k n", p=P)),
                ] + [(w_low[:, back, :, i * 2 * DS:(i + 1) * 2 * DS], x_proj[:, :, DTR:XPW]) for i in range(3)]
                assert len(loads) == NW
                for dst, src in loads:
                    sp.dma_start(dst, src).then_inc(weights_loaded.sem, 16)

            def results(ch):
                here = fwd_dram.rearrange("p (b h) k n -> p b h k n", h=2)[:, ch.b, ch.nh]
                if not ch.back:
                    wait_apart(sp, close_free, ch.g, len(CLOSE), passed)
                    sp.dma_start(here, fo[:, :, :]).then_inc(fwd_stored.sem, 16)
                    return
                wait_apart(sp, fwd_stored, ch.dir_start + CHUNKS, 0, passed)
                wait_apart(sp, norm_step, ch.dir, 0, passed)
                sp.dma_start(fwd_in[:, :, :], here).then_inc(fwd_loaded.sem, 16)
                if ch.blk == 0:
                    wait_apart(sp, norm_step, ch.dir, 4, passed)
                    sp.dma_start(half_of(res_dram, ch.b, ch.nh), fo[:, :, :]).then_inc(res_stored.sem, 16)
                else:
                    wait_apart(sp, res_stored, ch.layer_start + CHUNKS, 0, passed)
                    wait_apart(sp, x_written, ch.layer_batch, 0, passed)
                    sp.dma_start(res_in[:, ch.half], half_of(res_dram, ch.b, ch.nh)).then_inc(res_loaded.sem, 16)

            load_weights(0, 0)
            with sp.Fori(0, NL) as l:
                for st in range(STAGES):
                    wait_apart(sp, close_free, Chunk(l, st, 0, 0).g, 0, passed)
                    wait_apart(sp, weights_loaded, l * STAGES + st, 16 * NW, passed)
                    load_weights(l, st + 1) if st < STAGES - 1 else load_weights(NL - 1, 0)
                    with sp.Fori(0, NB) as b:
                        for half in range(2):
                            results(Chunk(l, st, b, half))
            sp.wait_ge(weights_loaded.sem, weights_loaded.at(NL * STAGES, 16 * NW))

        @block.gpsimd
        def _(pool):
            nc.gpsimd.memset(mean_w[:, :], 1.0 / DM).then_inc(mean_w_set, 1)
            nc.gpsimd.memset(pick[:, :], 0.0).then_inc(pick_zeroed, 1)
            for part in range(3):
                pool.wait_ge(pick_zeroed, part + 1)
                last = nc.gpsimd.affine_select(out=pick[:, :], in_=pick[:, :], compare_op=ALU.not_equal,
                                               fill=1.0, base=-2 * DS * part, pattern=[[-1, 2 * DS]],
                                               channel_multiplier=1)
                last.then_inc(pick_zeroed if part < 2 else pick_set, 1)
            pool.wait_ge(ln_loaded, 32)
            nc.gpsimd.tensor_scalar(ln_w[:, :], ln_w[:, :], 0.5, 1.0, ALU.mult, ALU.mult).then_inc(ln_halved, 1)
            nc.gpsimd.tensor_scalar(ln_b[:, :], ln_b[:, :], 0.5, 1.0, ALU.mult, ALU.mult).then_inc(ln_halved, 1)

            def prepare(s, ch):
                g, half = ch.g, ch.half
                if s == X_GATE:
                    wait(pool, x_sig, g, 3)
                    nc.gpsimd.tensor_tensor(xc[:, half], xc[:, half], tmp[:, :, :], ALU.mult).then_inc(xc_ready.sem, 1)
                for n in range(2):
                    if s == SPLIT[n]:
                        wait(pool, split_step, g, (1, 4)[n])
                        nc.gpsimd.tensor_tensor(bc_rest[:, :], bc_rest[:, :], bc_parts[:, half, :], ALU.subtract
                                                ).then_inc(split_step.sem, 1)
                if s == DELTA:
                    wait(pool, step_ln, g, 1)
                    wait(pool, step_rest, g, 1)
                    nc.gpsimd.tensor_tensor(delta[:, half], delta[:, half], tmp[:, :, :], ALU.add
                                            ).then_inc(delta_ready.sem, 1)
                if s == DU:
                    wait(pool, delta_ready, g, 1)
                    wait(pool, xc_ready, g, 1)
                    nc.gpsimd.tensor_tensor(du[:, half], delta[:, half], xc[:, half], ALU.mult).then_inc(du_ready.sem, 1)

            def gate(s, ch):
                if s == Z_GATE:
                    wait(pool, z_sig, ch.g, 3)
                    nc.gpsimd.tensor_tensor(sz[:, ch.half], sz[:, ch.half], du[:, 1 - ch.half], ALU.mult
                                            ).then_inc(sz_ready.sem, 1)

            def close(s, ch):
                if s == GATE:
                    wait(pool, y_read, ch.g, MC)
                    wait(pool, sz_ready, ch.g, 1)
                    nc.gpsimd.tensor_tensor(sz[:, ch.half], xc[:, ch.half], sz[:, ch.half], ALU.mult
                                            ).then_inc(yg_ready.sem, 1)

            def start(ch):
                for s in range(DS):
                    prepare(s, ch)

            def round_(cur, nxt, prv):
                g = cur.g
                wait(pool, du_ready, g, 1)
                for s in range(DS):
                    wait(pool, b_copied, g, s + 1)
                    states = s - 2 + (cur.half == 0 and s < 2)
                    wait(pool, scan_done, g, MC * states)
                    nc.gpsimd.tensor_tensor(dbx_buffer(cur, s), du[:, cur.half], wide(b_wide[:, s % 2, :]), ALU.mult
                                            ).then_inc(dbx_ready.sem, 1)
                    prepare(s, nxt)
                    gate(s, cur)
                    if prv is not None:
                        close(s, prv)

            rounds(pool, start, round_, lambda ch: close(GATE, ch))

        @block.tensor
        def _(pe):
            pe.wait_ge(mean_w_set, 1)
            pe.wait_ge(pick_set, 1)

            def widen_b(ch, s):
                wait(pe, split_step, ch.g, 6)
                wait(pe, b_copied, ch.g, s)
                nc.tensor.matmul(b_bank[:, 0:HALF], pick[:, s:s + 1].broadcast_to([6 * DS, P]), bc_parts[:, ch.half, :],
                                 start=True, stop=True).then_inc(b_made.sem, 1)

            def widen_c(ch, s):
                wait(pe, cmul_done, ch.g, s)
                nc.tensor.matmul(c_bank[:, 0:HALF], pick[:, DS + s:DS + s + 1].broadcast_to([6 * DS, P]), bc_parts[:, ch.half, :],
                                 start=True, stop=True).then_inc(c_ready.sem, 1)

            def add_state(ch, s):
                wait(pe, cmul_done, ch.g, s + 1)
                if s == 0:
                    wait(pe, y_read, ch.g, 0)
                flat = hc[:, s % 2].rearrange("p m n -> p (m n)")
                for c in range(0, MC * HALF, 512):
                    last = nc.tensor.matmul(y_bank[:, c:c + 512], ident[:, :], flat[:, c:c + 512],
                                            start=(s == 0), stop=(s == DS - 1))
                last.then_inc(y_added.sem, 1)

            def project(bank, m, ch, made):
                for k in range(KC):
                    rhs = tokens(ch, k)
                    dst = prep_bank[bank][:, 0:HALF]
                    if ch.blk == 1:
                        dst = dst.rearrange("p (t o) -> p t o", o=NO)
                    last = nc.tensor.matmul(dst, w_in[:, ch.back, k, m * P:(m + 1) * P], rhs,
                                            start=(k == 0), stop=(k == KC - 1))
                last.then_inc(made.sem, 1)

            def prepare(s, ch):
                g, back = ch.g, ch.back
                for m in PE_X.get(s, ()):
                    if m == 0:
                        wait(pe, weights_loaded, ch.stage, 16 * NW)
                        if ch.st == 0:
                            wait(pe, x_written, ch.layer_batch - NB, 1)
                    if m < 2:
                        wait(pe, z_read, g, 0)
                    else:
                        wait(pe, x_read, g, m - 1)
                    project(m % 2, m, ch, x_made)
                for m in PE_Z.get(s, ()):
                    if m < 2:
                        wait(pe, step_read, g, MC)
                    else:
                        wait(pe, z_read, g, m - 1)
                    project(m % 2, MC + m, ch, z_made)
                if s == PE_LOW:
                    wait(pe, xc_ready, g, 1)
                    wait(pe, x_read, g, MC)
                    for k in range(MC):
                        last = nc.tensor.matmul(prep_bank[0][0:6 * DS + DTR, 0:HALF], w_low[:, back, k, :],
                                                xc[:, ch.half, k, :], start=(k == 0), stop=(k == MC - 1))
                    last.then_inc(low_made.sem, 1)
                for m in PE_STEP.get(s, ()):
                    if m == 0:
                        wait(pe, dt_read, g, 1)
                    elif m == 1:
                        wait(pe, split_step, g, 1)
                    else:
                        wait(pe, step_read, g, m - 1)
                    nc.tensor.matmul(prep_bank[(m + 1) % 2][:, 0:HALF], w_step[:, back, m * P:(m + 1) * P],
                                     dt_low[:, :], start=True, stop=True).then_inc(step_made.sem, 1)

            def close(s, ch):
                back = ch.back
                if s in PE_OUT:
                    k = PE_OUT[s]
                    wait(pe, yg_ready, ch.g, 1)
                    wait(pe, close_free, ch.g, USE["out", k] - 1)
                    for m in range(MC):
                        ys = sz[:, ch.half, m, ::-1] if back else sz[:, ch.half, m, :]
                        last = nc.tensor.matmul(close_bank[:, 0:HALF], w_out[:, back, m, k * P:(k + 1) * P], ys,
                                                start=(m == 0), stop=(m == MC - 1))
                    last.then_inc(close_full.sem, 1 if back or k < KC - 1 else 1 + len(CLOSE) - KC)
                for step, what, src in ((PE_MEAN, "mean", fo), (PE_VAR, "var", sq)):
                    if back and s == step:
                        wait(pe, close_free, ch.g, USE[what, 0] - 1)
                        if what == "var":
                            wait(pe, sq_ready, ch.dir, 1)
                        for k in range(KC):
                            last = nc.tensor.matmul(close_bank[:, 0:HALF], mean_w[:, :], src[:, k, :],
                                                    start=(k == 0), stop=(k == KC - 1))
                        last.then_inc(close_full.sem, 1)

            def start(ch):
                for s in range(DS):
                    prepare(s, ch)
                for s in range(3):
                    widen_b(ch, s)

            def round_(cur, nxt, prv):
                for s in range(DS):
                    widen_b(cur, s + 3) if s + 3 < DS else widen_b(nxt, s + 3 - DS)
                    widen_c(cur, s)
                    if s > 0:
                        add_state(cur, s - 1)
                    elif prv is not None:
                        add_state(prv, DS - 1)
                    prepare(s, nxt)
                    if prv is not None:
                        close(s, prv)

            def end(ch):
                add_state(ch, DS - 1)
                for s in range(DS):
                    close(s, ch)

            rounds(pe, start, round_, end)

        @block.scalar
        def _(act):
            nc.scalar.preload_act_table_set("natural_log_exp_and_others")
            act.wait_ge(ln_halved, 2)

            def sigmoid(part, dst, src, s, g):
                if part == 0:
                    nc.scalar.activation(dst, src, ACT.Exp, scale=-1.0).then_inc(s.sem, 1)
                else:
                    wait(act, s, g, part)
                    if part == 1:
                        nc.scalar.activation(dst, dst, ACT.Ln, bias=1.0).then_inc(s.sem, 1)
                    else:
                        nc.scalar.activation(dst, dst, ACT.Exp, scale=-1.0).then_inc(s.sem, 1)

            def copy_b(ch, s):
                wait(act, b_made, ch.g, s + 1)
                wait(act, dbx_ready, ch.g, s - 1)
                nc.scalar.copy(b_wide[:, s % 2, :], b_bank[:, 0:HALF]).then_inc(b_copied.sem, 1)

            def prepare(s, ch):
                g, half, back = ch.g, ch.half, ch.back
                for m in READ_X.get(s, ()):
                    if m == 0:
                        wait(act, halo_ready, g, 0)
                        wait(act, weights_loaded, ch.stage, 16 * NW)
                        wait(act, yg_ready, g - 1, 0)
                    wait(act, x_made, g, m + 1)
                    nc.scalar.activation(xc[:, half, m, :], projected(ch, m), ACT.Identity,
                                         bias=conv_bias[:, back, m:m + 1], scale=taps[:, back, m, DCONV - 1:DCONV]
                                         ).then_inc(last_tap.sem, 1)
                    nc.scalar.copy(xin[:, m, DCONV - 1:], projected(ch, m)).then_inc(x_read.sem, 1)
                for part in range(3):
                    if s == ACT_X[part]:
                        if part == 0:
                            wait(act, xpre_ready, g, 1)
                            wait(act, delta_ready, g, 0)
                        sigmoid(part, tmp[:, :, :], xc[:, half], x_sig, g)
                if s == READ_LOW:
                    wait(act, low_made, g, 1)
                    nc.scalar.copy(dt_low[:, :], prep_bank[0][6 * DS:6 * DS + DTR, 0:HALF]).then_inc(dt_read.sem, 1)
                    wait(act, split_step, g, 0)
                    wait(act, c_ready, g - 1, 0)
                    nc.scalar.copy(bc_rest[:, :], prep_bank[0][0:6 * DS, 0:HALF])
                    nc.scalar.copy(bc_parts[:, half, :], prep_bank[0][0:6 * DS, 0:HALF]).then_inc(split_step.sem, 1)
                for n in range(2):
                    if s == ROUND_REST[n]:
                        wait(act, split_step, g, (2, 5)[n])
                        for part in range(n + 1, 3):
                            rows = slice(part * 2 * DS, (part + 1) * 2 * DS)
                            nc.scalar.copy(bc_parts[rows, half, :], bc_rest[rows, :]).then_inc(split_step.sem, 1)
                for m in READ_STEP.get(s, ()):
                    src = prep_bank[(m + 1) % 2][:, 0:HALF]
                    if m == 0:
                        wait(act, xc_ready, g, 1)
                    wait(act, step_made, g, m + 1)
                    pre = nc.scalar.activation(delta[:, half, m, :], src, ACT.Abs, bias=step_bias[:, back, m:m + 1])
                    if m == MC - 1:
                        pre.then_inc(step_abs.sem, 1)
                    nc.scalar.activation(tmp[:, m, :], src, ACT.Relu, bias=step_bias[:, back, m:m + 1]
                                         ).then_inc(step_read.sem, 1)
                if s == STEP_EXP:
                    wait(act, sz_ready, g, 0)
                    wait(act, step_abs, g, 1)
                    nc.scalar.activation(du[:, half], delta[:, half], ACT.Exp, scale=-1.0).then_inc(step_exp.sem, 1)
                if s == STEP_U:
                    wait(act, step_exp, g, 1)
                    nc.scalar.activation(delta[:, half], du[:, half], ACT.Identity, bias=1.0).then_inc(step_u.sem, 1)
                if s == STEP_LN:
                    wait(act, step_u, g, 1)
                    wait(act, step_corr, g, 1)
                    nc.scalar.activation(delta[:, half], delta[:, half], ACT.Ln).then_inc(step_ln.sem, 1)

            def gate(s, ch):
                for part in range(3):
                    if s == ACT_Z[part]:
                        if part == 0:
                            wait(act, z_read, ch.g, MC)
                            wait(act, dbx_ready, ch.g, 0)
                        sigmoid(part, du[:, 1 - ch.half], sz[:, ch.half], z_sig, ch.g)

            def make_decay(ch):
                wait(act, weights_loaded, ch.stage, 16 * NW)
                nc.scalar.activation(decay[:, ch.back], decay[:, ch.back], ACT.Exp).then_inc(decay_step.sem, 1)
                wait(act, decay_step, ch.stage, 1)
                nc.scalar.mul(decay[:, ch.back], decay[:, ch.back], -1.0).then_inc(decay_step.sem, 1)

            def close(s, ch):
                if not ch.back and s in READ_OUT:
                    k = READ_OUT[s]
                    if k == 0:
                        wait(act, fwd_stored, ch.dir, 0)
                        wait(act, norm_step, ch.dir_start, 0)
                        if ch.st == 2:
                            wait(act, res_stored, ch.layer_start + CHUNKS, 0)
                    wait(act, close_full, ch.g, USE["out", k])
                    nc.scalar.copy(fo[:, k, :], close_bank[:, 0:HALF]
                                   ).then_inc(close_free.sem, 1 if k < KC - 1 else 1 + len(CLOSE) - KC)
                if ch.back and s == SQUARE:
                    wait(act, close_free, ch.g, USE["mean", 0])
                    wait(act, centred, ch.dir, 1)
                    nc.scalar.activation(sq[:, :, :], fo[:, :, :], ACT.Square).then_inc(sq_ready.sem, 1)
                if ch.back and s == RSTD:
                    wait(act, close_full, ch.g, USE["var", 0])
                    nc.scalar.activation(rstd[:, :], close_bank[:, 0:HALF], ACT.Ln, bias=eps5[:, 0:1]
                                         ).then_inc(close_free.sem, 1)
                    wait(act, close_free, ch.g, USE["var", 0])
                    nc.scalar.activation(rstd[:, :], rstd[:, :], ACT.Exp, scale=-0.5).then_inc(rstd_ready.sem, 1)

            def affine(s, ch):
                if ch.back and s == NORM + 1:
                    wait(act, norm_step, ch.dir, 1)
                    for k in range(KC):
                        nc.scalar.activation(fo[:, k, :], fo[:, k, :], ACT.Identity, bias=ln_b[:, k:k + 1],
                                             scale=ln_w[:, k:k + 1]).then_inc(norm_step.sem, 1)

            def start(ch):
                make_decay(ch)
                for s in range(DS):
                    prepare(s, ch)
                for s in range(2):
                    copy_b(ch, s)

            def round_(cur, nxt, prv):
                g = cur.g
                wait(act, delta_ready, g, 1)
                wait(act, decay_step, cur.stage, 2)
                for s in range(DS):
                    for c in range(MC):
                        n = s * MC + c
                        wait(act, scan_done, g, n - MC + 1)
                        nc.scalar.activation(a[:, c, :], delta[:, cur.half, c, :], ACT.Exp,
                                             scale=decay[:, cur.back, c, s:s + 1]).then_inc(a_ready.sem, 1)
                        if c == 0:
                            copy_b(cur, s + 2) if s + 2 < DS else copy_b(nxt, s + 2 - DS)
                            if s == 1 and nxt.st != cur.st:
                                make_decay(nxt)
                            if s > 0:
                                prepare(s - 1, nxt)
                                gate(s - 1, cur)
                                if prv is not None:
                                    close(s - 1, prv)
                                    affine(s - 1, prv)

            def end(ch):
                for s in range(DS):
                    close(s, ch)
                    affine(s, ch)

            rounds(act, start, round_, end)

        @block.vector
        def _(dve):
            nc.vector.memset(xin[:, :, 0:DCONV - 1], 0.0).then_inc(halo_zeroed, 1)
            dve.wait_ge(halo_zeroed, 1)
            dve.wait_ge(ln_halved, 2)

            def prepare(s, ch):
                g, half, back = ch.g, ch.half, ch.back
                xparts = READ_X.get(s, ())
                for m in xparts:
                    if m == 0:
                        wait(dve, halo_ready, g, 0)
                        wait(dve, weights_loaded, ch.stage, 16 * NW)
                    wait(dve, x_read, g, m + 1)
                    wait(dve, last_tap, g, m + 1)
                for tap in range(DCONV - 1):
                    for m in xparts:
                        if tap > 0:
                            wait(dve, conv_step, g, xparts[0] * (DCONV - 1) + (tap - 1) * len(xparts) + m - xparts[0] + 1)
                        nc.vector.scalar_tensor_tensor(out=xc[:, half, m, :], in0=xin[:, m, tap:tap + HALF],
                                                       scalar=taps[:, back, m, tap:tap + 1], in1=xc[:, half, m, :],
                                                       op0=ALU.mult, op1=ALU.add).then_inc(conv_step.sem, 1)
                if s == CLAMP_X:
                    wait(dve, conv_step, g, MC * (DCONV - 1))
                    nc.vector.tensor_scalar(xc[:, half], xc[:, half], LOW, None, ALU.max).then_inc(xpre_ready.sem, 1)
                    if half == 0:
                        nc.vector.tensor_copy(xin[:, :, 0:DCONV - 1], xin[:, :, HALF:HALF + DCONV - 1]
                                              ).then_inc(halo_ready.sem, 1)
                    else:
                        nc.vector.memset(xin[:, :, 0:DCONV - 1], 0.0).then_inc(halo_ready.sem, 1)
                for m in READ_Z.get(s, ()):
                    if m == 0:
                        wait(dve, close_full, g - 2, KC)
                    wait(dve, z_made, g, m + 1)
                    nc.vector.tensor_scalar(sz[:, half, m, :], projected(ch, m), LOW, None, ALU.max
                                            ).then_inc(z_read.sem, 1)
                if s == STEP_CORR:
                    wait(dve, step_u, g, 1)
                    nc.vector.scalar_tensor_tensor(out=du[:, half], in0=delta[:, half], scalar=1.0, in1=du[:, half],
                                                   op0=ALU.subtract, op1=ALU.subtract).then_inc(step_corr.sem, 1)
                if s == STEP_REST:
                    wait(dve, step_corr, g, 1)
                    wait(dve, step_read, g, MC)
                    nc.vector.tensor_tensor(tmp[:, :, :], tmp[:, :, :], du[:, half], ALU.subtract
                                            ).then_inc(step_rest.sem, 1)

            def times_c(ch, s):
                wait(dve, c_ready, ch.g, s + 1)
                wait(dve, scan_done, ch.g, MC * (s + 1))
                wait(dve, y_added, ch.g, s - 1)
                nc.vector.tensor_tensor(hc[:, s % 2], hs[:, s % 2], wide(c_bank[:, 0:HALF]), ALU.mult
                                        ).then_inc(cmul_done.sem, 1)
                if ch.half == 0:
                    nc.vector.tensor_copy(carry[:, s, :], hs[:, s % 2, :, HALF - 1]).then_inc(carry_saved.sem, 1)

            def skip_connection(ch):
                wait(dve, y_added, ch.g, DS)
                for m in range(MC):
                    nc.vector.scalar_tensor_tensor(out=xc[:, ch.half, m, :], in0=xc[:, ch.half, m, :],
                                                   scalar=skip[:, ch.back, m:m + 1],
                                                   in1=y_bank[:, m * HALF:(m + 1) * HALF], op0=ALU.mult, op1=ALU.add
                                                   ).then_inc(y_read.sem, 1)

            def close(s, ch):
                if not ch.back:
                    return
                if s in READ_OUT:
                    k = READ_OUT[s]
                    if k == 0:
                        wait(dve, fwd_loaded, ch.dir, 16)
                        wait(dve, fwd_stored, ch.dir_start + CHUNKS, 0)
                        if ch.blk == 0:
                            wait(dve, res_stored, ch.layer, 0)
                    wait(dve, close_full, ch.g, USE["out", k])
                    nc.vector.tensor_tensor(fo[:, k, :], close_bank[:, 0:HALF], fwd_in[:, k, :], ALU.add
                                            ).then_inc(close_free.sem, 1)
                if s == CENTRE:
                    wait(dve, close_full, ch.g, USE["mean", 0])
                    for k in range(KC):
                        nc.vector.tensor_tensor(fo[:, k, :], fo[:, k, :], close_bank[:, 0:HALF], ALU.subtract
                                                ).then_inc(centred.sem if k == 0 else close_free.sem, 1)
                if s == NORM:
                    wait(dve, rstd_ready, ch.dir, 1)
                    wait(dve, close_free, ch.g, USE["mean", 0])
                    wait(dve, sq_ready, ch.dir, 1)
                    nc.vector.tensor_tensor(fo[:, :, :], fo[:, :, :], wide(rstd[:, :], KC), ALU.mult
                                            ).then_inc(norm_step.sem, 1)
                if s == NORM + 1:
                    wait(dve, norm_step, ch.dir, 3)
                    if ch.blk == 0:
                        nc.vector.tensor_tensor(fo[:, :, :], fo[:, :, :], half_of(X[:, :, :], ch.b, ch.nh), ALU.add
                                                ).then_inc(norm_step.sem, 1)
                        return
                    wait(dve, res_loaded, ch.layer, 16)
                    to = res_in[:, 0] if ch.half == 0 else half_of(X[:, :, :], ch.b, ch.nh)
                    nc.vector.tensor_tensor(to, fo[:, :, :], res_in[:, ch.half], ALU.add).then_inc(norm_step.sem, 1)
                    if ch.half == 1:
                        wait(dve, norm_step, ch.dir, 4)
                        nc.vector.tensor_copy(half_of(X[:, :, :], ch.b, ch.half), res_in[:, 0]
                                              ).then_inc(x_written.sem, 1)

            def start(ch):
                for s in range(DS):
                    prepare(s, ch)

            def round_(cur, nxt, prv):
                g = cur.g
                for s in range(DS):
                    wait(dve, dbx_ready, g, s + 1)
                    if cur.half == 1:
                        wait(dve, carry_saved, cur.batch, min(DS - 1 + s, DS))
                    elif s > 1:
                        wait(dve, carry_saved, cur.batch, s - 1)
                    wait(dve, cmul_done, g, s - 1)
                    for c in range(MC):
                        n = s * MC + c
                        wait(dve, a_ready, g, n + 1)
                        nc.vector.tensor_tensor_scan(hs[:, s % 2, c, :], a[:, c, :],
                                                     dbx_buffer(cur, s)[:, c, :],
                                                     0.0 if cur.half == 0 else carry[:, s, c:c + 1],
                                                     ALU.mult, ALU.add).then_inc(scan_done.sem, 1)
                        if c == 0 and s > 0:
                            times_c(cur, s - 1)
                        elif c == 0 and prv is not None:
                            times_c(prv, DS - 1)
                    if s == 0 and prv is not None:
                        skip_connection(prv)
                    prepare(s, nxt)
                    if prv is not None:
                        close(s, prv)

            def end(ch):
                times_c(ch, DS - 1)
                skip_connection(ch)
                for s in range(DS):
                    close(s, ch)

            rounds(dve, start, round_, end)


def attention(nc, X, ident, eps5, w):
    KT = SEQ // P
    with ExitStack() as ctx:
        def sb(name, shape, dt=F32):
            return ctx.enter_context(nc.sbuf_tensor(name, shape, dt))

        def sem(name, per=1):
            return Sem(ctx.enter_context(nc.semaphore(name)), per)

        mean_w = sb("attn_mean_w", [P, P])
        ones = sb("ones", [P, P])
        w_h = sb("w_h", [P, KC, DM + 1])
        w_t = sb("w_t", [P, KC, DM])
        a_cols = sb("a_cols", [P, 2 * KC])
        wa = sb("wa", [P, 2, KC, P])
        z = sb("z", [P, KC, 2, HALF])
        sq = sb("attn_sq", [P, KC, 2, HALF])
        rstd = sb("attn_rstd", [P, 2, HALF])
        h_sb = sb("h_sb", [P, KT, DM + 1])
        f2_max = sb("f2_max", [P, 1])
        row_max = sb("row_max", [P, 2, HALF])
        score = sb("score", [P, 2, 2, HALF])
        prob = sb("prob", [P, 2, 2, HALF])
        rden = sb("rden", [P, 2, HALF])
        hp = sb("hp", [P, KC, 2, HALF])
        neg = sb("neg", [P, KC, 2, HALF])
        bank4 = ctx.enter_context(nc.psum_tensor("out_banks", [P, KC, 2, 512], F32))
        f1_bank = ctx.enter_context(nc.psum_tensor("f1_bank", [P, 2, 512], F32))
        den_bank = ctx.enter_context(nc.psum_tensor("den_bank", [P, 2, 512], F32))
        f1, den, outp = f1_bank[:, :, 0:HALF], den_bank[:, :, 0:HALF], bank4[:, :, :, 0:HALF]
        h_bank = [bank4[:, 0, 0, 0:DM + 1], bank4[:, 0, 1, 0:DM + 1]]

        loaded = ctx.enter_context(nc.semaphore("attn_loaded"))
        consts_set = ctx.enter_context(nc.semaphore("consts_set"))
        w_turned = ctx.enter_context(nc.semaphore("w_turned"))
        w_t_kept = ctx.enter_context(nc.semaphore("w_t_kept"))
        wa_made = ctx.enter_context(nc.semaphore("wa_made"))
        wa_kept = ctx.enter_context(nc.semaphore("wa_kept"))
        mean_made = sem("mean_made")
        centred = sem("attn_centred", 2)
        squared = sem("squared")
        var_made = sem("var_made")
        rstd_step = sem("rstd_step", 2)
        z_ready = sem("z_ready")
        h_made = sem("h_made", KT)
        h_kept = sem("h_kept", KT)
        f_made = sem("f_made")
        max_step = sem("max_step", 3)
        score_step = sem("score_step", 3 * KT)
        prob_ready = sem("prob_ready", KT)
        prob_used = sem("prob_used", KT)
        rden_ready = sem("rden_ready")
        hp_step = sem("hp_step", 3)
        neg_exp = sem("neg_exp")
        x_added = sem("x_added", 2)
        sems = [mean_made, centred, squared, var_made, rstd_step, z_ready, h_made, h_kept, f_made, max_step,
                score_step, prob_ready, prob_used, rden_ready, hp_step, neg_exp, x_added]
        ctx.enter_context(nc.allow_non_contiguous_dma(reason="vectors of a few hundred values"))
        block = ctx.enter_context(nc.Block())

        def wait(eng, s, b, n):
            eng.wait_ge(s.sem, s.at(b, n))

        def tokens(b):
            return X[:, :, :].rearrange("p k (b h n) -> p b k h n", b=NB, h=2)[:, b]

        def each_block(ap):
            return ap.unsqueeze(1).broadcast_to([P, KC, 2, HALF])

        @block.sync
        def _(sp):
            for s in sems:
                s.start(sp)
            sp.dma_start(w_h[:, :, 0:DM], w["W"].rearrange("(k p) n -> p k n", p=P)).then_inc(loaded, 16)
            sp.dma_start(a_cols[:, :], w["a"].rearrange("(c p) n -> p (c n)", p=P)).then_inc(loaded, 16)
            sp.wait_ge(loaded, 32)

        @block.gpsimd
        def _(pool):
            nc.gpsimd.memset(mean_w[:, :], 1.0 / DM).then_inc(consts_set, 1)
            nc.gpsimd.memset(ones[:, :], 1.0).then_inc(consts_set, 1)

        @block.tensor
        def _(pe):
            pe.wait_ge(consts_set, 2)
            pe.wait_ge(loaded, 32)
            for k in range(KC):
                for o in range(KC):
                    last = nc.tensor.transpose(den_bank[:, o, k * P:(k + 1) * P], w_h[:, k, o * P:(o + 1) * P],
                                               ident[:, :])
            last.then_inc(w_turned, 1)
            pe.wait_ge(w_t_kept, 1)
            for v in range(2):
                for k in range(KC):
                    for o in range(KC):
                        last = nc.tensor.matmul(f1_bank[:, v, k * P:(k + 1) * P], w_t[:, o, k * P:(k + 1) * P],
                                                a_cols[:, v * KC + o:v * KC + o + 1].broadcast_to([P, P]),
                                                start=(o == 0), stop=(o == KC - 1))
            last.then_inc(wa_made, 1)
            pe.wait_ge(wa_kept, 2)

            with pe.Fori(0, NB) as b:
                t = tokens(b)

                def over_features(dst, weight, src):
                    for h in range(2):
                        for k in range(KC):
                            last = nc.tensor.matmul(dst[:, h, 0:HALF], weight(k), src[:, k, h],
                                                    start=(k == 0), stop=(k == KC - 1))
                    return last

                wait(pe, rden_ready, b, 0)
                over_features(den_bank, lambda k: mean_w[:, :], t).then_inc(mean_made.sem, 1)
                wait(pe, squared, b, 1)
                wait(pe, centred, b, 2)
                over_features(den_bank, lambda k: mean_w[:, :], sq).then_inc(var_made.sem, 1)
                wait(pe, z_ready, b, 1)
                wait(pe, hp_step, b, 0)
                for j in range(KT):
                    if j >= 2:
                        wait(pe, h_kept, b, j - 1)
                    zj = z[:, :, :, :].rearrange("p k h n -> p k (h n)")
                    for k in range(KC):
                        last = nc.tensor.matmul(h_bank[j % 2], zj[:, k, j * P:(j + 1) * P], w_h[:, k, :],
                                                start=(k == 0), stop=(k == KC - 1))
                    last.then_inc(h_made.sem, 1)
                wait(pe, rstd_step, b, 2)
                wait(pe, score_step, b, 0)
                over_features(f1_bank, lambda k: wa[:, 0, k, :], z)
                over_features(den_bank, lambda k: wa[:, 1, k, :], z).then_inc(f_made.sem, 1)
                wait(pe, h_kept, b, KT)
                wait(pe, max_step, b, 1)
                for j in range(KT):
                    wait(pe, prob_ready, b, j + 1)
                    for h in range(2):
                        ph = prob[:, j % 2, h]
                        nc.tensor.matmul(den_bank[:, h, 0:HALF], ones[:, :], ph, start=(j == 0), stop=(j == KT - 1))
                        for k in range(KC):
                            last = nc.tensor.matmul(bank4[:, k, h, 0:HALF], h_sb[:, j, k * P:(k + 1) * P], ph,
                                                    start=(j == 0), stop=(j == KT - 1))
                    last.then_inc(prob_used.sem, 1)

        @block.scalar
        def _(act):
            nc.scalar.preload_act_table_set("natural_log_exp_and_others")
            act.wait_ge(w_turned, 1)
            nc.scalar.copy(w_t[:, :, :], den_bank[:, :, 0:DM]).then_inc(w_t_kept, 1)
            act.wait_ge(wa_made, 1)
            nc.scalar.copy(wa[:, :, :, :], f1_bank[:, :, 0:KC * P].rearrange("p v (k n) -> p v k n", k=KC)
                           ).then_inc(wa_kept, 1)
            act.wait_ge(wa_kept, 1)
            nc.scalar.copy(w_h[:, :, DM], wa[:, 1, :, 0]).then_inc(wa_kept, 1)
            with act.Fori(0, NB) as b:
                wait(act, centred, b, 2)
                nc.scalar.activation(sq[:, :, :, :], z[:, :, :, :], ACT.Square).then_inc(squared.sem, 1)
                wait(act, var_made, b, 1)
                nc.scalar.activation(rstd[:, :, :], den, ACT.Ln, bias=eps5[:, 0:1]).then_inc(rstd_step.sem, 1)
                wait(act, rstd_step, b, 1)
                nc.scalar.activation(rstd[:, :, :], rstd[:, :, :], ACT.Exp, scale=-0.5).then_inc(rstd_step.sem, 1)
                wait(act, prob_used, b, 0)
                for j in range(KT):
                    wait(act, h_made, b, j + 1)
                    nc.scalar.copy(h_sb[:, j, :], h_bank[j % 2]).then_inc(h_kept.sem, 1)
                for j in range(KT):
                    wait(act, score_step, b, 3 * j + 3)
                    wait(act, prob_used, b, j - 1)
                    nc.scalar.activation(prob[:, j % 2], score[:, j % 2], ACT.Exp).then_inc(prob_ready.sem, 1)
                wait(act, hp_step, b, 2)
                nc.scalar.activation(neg[:, :, :, :], neg[:, :, :, :], ACT.Exp).then_inc(neg_exp.sem, 1)

        @block.vector
        def _(dve):
            with dve.Fori(0, NB) as b:
                t = tokens(b)
                wait(dve, mean_made, b, 1)
                for h in range(2):
                    nc.vector.tensor_tensor(z[:, :, h], t[:, :, h],
                                            den_bank[:, h, 0:HALF].unsqueeze(1).broadcast_to([P, KC, HALF]),
                                            ALU.subtract).then_inc(centred.sem, 1)
                wait(dve, rstd_step, b, 2)
                wait(dve, squared, b, 1)
                nc.vector.tensor_tensor(z[:, :, :, :], z[:, :, :, :], each_block(rstd[:, :, :]), ALU.mult
                                        ).then_inc(z_ready.sem, 1)
                wait(dve, f_made, b, 1)
                nc.vector.tensor_reduce(f2_max[:, :], den, AX.XY, ALU.max).then_inc(max_step.sem, 1)
                wait(dve, max_step, b, 1)
                nc.vector.tensor_scalar(row_max[:, :, :], f1, f2_max[:, 0:1], None, ALU.add).then_inc(max_step.sem, 1)
                wait(dve, max_step, b, 2)
                nc.vector.scalar_tensor_tensor(out=row_max[:, :, :], in0=row_max[:, :, :], scalar=0.01,
                                               in1=row_max[:, :, :], op0=ALU.mult, op1=ALU.max
                                               ).then_inc(max_step.sem, 1)
                wait(dve, max_step, b, 3)
                wait(dve, h_kept, b, KT)
                for j in range(KT):
                    sc = score[:, j % 2]
                    wait(dve, prob_ready, b, j - 1)
                    nc.vector.tensor_scalar(sc, f1, h_sb[:, j, DM:DM + 1], None, ALU.add).then_inc(score_step.sem, 1)
                    wait(dve, score_step, b, 3 * j + 1)
                    nc.vector.scalar_tensor_tensor(out=sc, in0=sc, scalar=0.01, in1=sc, op0=ALU.mult, op1=ALU.max
                                                   ).then_inc(score_step.sem, 1)
                    wait(dve, score_step, b, 3 * j + 2)
                    nc.vector.tensor_tensor(sc, sc, row_max[:, :, :], ALU.subtract).then_inc(score_step.sem, 1)
                wait(dve, prob_used, b, KT)
                nc.vector.reciprocal(rden[:, :, :], den).then_inc(rden_ready.sem, 1)
                wait(dve, rden_ready, b, 1)
                nc.vector.tensor_tensor(hp[:, :, :, :], outp, each_block(rden[:, :, :]), ALU.mult
                                        ).then_inc(hp_step.sem, 1)
                wait(dve, hp_step, b, 1)
                nc.vector.tensor_scalar(neg[:, :, :, :], hp[:, :, :, :], 0.0, None, ALU.min).then_inc(hp_step.sem, 1)
                nc.vector.scalar_tensor_tensor(out=hp[:, :, :, :], in0=hp[:, :, :, :], scalar=0.0, in1=t,
                                               op0=ALU.max, op1=ALU.add).then_inc(hp_step.sem, 1)
                wait(dve, neg_exp, b, 1)
                wait(dve, hp_step, b, 3)
                nc.vector.tensor_scalar(neg[:, :, :, :], neg[:, :, :, :], -1.0, None, ALU.add
                                        ).then_inc(x_added.sem, 1)
                wait(dve, x_added, b, 1)
                nc.vector.tensor_tensor(t, hp[:, :, :, :], neg[:, :, :, :], ALU.add).then_inc(x_added.sem, 1)


def experts(nc, X, ident, eps5, w, out):
    TILES = HALF // P
    with ExitStack() as ctx:
        def sb(name, shape, dt=F32):
            return ctx.enter_context(nc.sbuf_tensor(name, shape, dt))

        def sem(name, per=1):
            return Sem(ctx.enter_context(nc.semaphore(name)), per)

        mean_w = sb("moe_mean_w", [P, P])
        router = sb("router", [NE, DM])
        router_t = sb("router_t", [P, KC, NE])
        w1 = sb("w1", [P, NE, KC, DM])
        w2 = sb("w2", [P, NE, KC, DM])
        b1 = sb("b1", [P, NE, KC])
        b2 = sb("b2", [NE, DM])
        number = sb("number", [P, NE])
        held = sb("held", [P, KC, HALF])
        n = sb("n", [P, KC, HALF])
        sq = sb("moe_sq", [P, KC, HALF])
        rstd = sb("moe_rstd", [P, HALF])
        logit = sb("logit", [P, TILES, NE])
        best = sb("best", [P, TILES, 8])
        best_at = sb("best_at", [P, TILES, 8], U32)
        at_f = sb("at_f", [P, TILES, 2])
        top = sb("top", [P, TILES, 2])
        total = sb("total", [P, TILES])
        weight = sb("weight", [P, TILES, NE])
        other = sb("other", [P, TILES, NE])
        weight_t = sb("weight_t", [NE, HALF])
        hg = sb("hg", [P, 2, KC, HALF])
        acc = sb("acc", [P, TILES, DM])
        h_bank = ctx.enter_context(nc.psum_tensor("h_bank", [P, 2, KC, 512], F32))
        y_bank = ctx.enter_context(nc.psum_tensor("y_out", [P, 2 * 512], F32))
        stat = ctx.enter_context(nc.psum_tensor("stat", [P, 512], F32))
        small = ctx.enter_context(nc.psum_tensor("small", [P, 512], F32))
        y_tile = [y_bank[:, i * DM:(i + 1) * DM] for i in range(TILES)]
        y_all = y_bank[:, 0:TILES * DM].rearrange("p (t n) -> p t n", t=TILES)

        loaded = ctx.enter_context(nc.semaphore("moe_loaded"))
        consts_set = ctx.enter_context(nc.semaphore("moe_consts_set"))
        router_turned = ctx.enter_context(nc.semaphore("router_turned"))
        router_kept = ctx.enter_context(nc.semaphore("router_kept"))
        passed = ctx.enter_context(nc.semaphore("moe_waits_passed"))
        x_held = sem("x_held")
        mean_made = sem("moe_mean_made")
        centred = sem("moe_centred")
        squared = sem("moe_squared")
        var_made = sem("moe_var_made")
        rstd_step = sem("moe_rstd_step", 2)
        n_ready = sem("n_ready")
        logits_made = sem("logits_made")
        route_step = sem("route_step", 13)
        top_exp = sem("top_exp")
        total_step = sem("total_step", 2)
        weight_ready = sem("weight_ready")
        weight_turned = sem("weight_turned")
        weight_t_kept = sem("weight_t_kept")
        x_turned = sem("x_turned")
        acc_step = sem("acc_step", 2 + TILES * NE)
        bias_made = sem("bias_made")
        h_made = sem("moe_h_made", NE)
        h_done = sem("moe_h_done", KC * NE)
        y_made = sem("y_made", NE)
        stored = sem("stored", 16)
        sems = [x_held, mean_made, centred, squared, var_made, rstd_step, n_ready, logits_made, route_step, top_exp, total_step,
                weight_ready, weight_turned, weight_t_kept, x_turned, acc_step, bias_made, h_made, h_done,
                y_made, stored]
        ctx.enter_context(nc.allow_non_contiguous_dma(reason="biases of a few thousand values"))
        block = ctx.enter_context(nc.Block())

        def wait(eng, s, g, k):
            eng.wait_ge(s.sem, s.at(g, k))

        def tokens(g):
            return X[:, :, :].rearrange("p k (g n) -> p g k n", n=HALF)[:, g]

        @block.sync
        def _(sp):
            for s in sems:
                s.start(sp)
            sp.dma_start(router[:, :], w["router_w"]).then_inc(loaded, 16)
            sp.dma_start(b1[:, :, :], w["b1"].rearrange("e (k p) -> p e k", p=P)).then_inc(loaded, 16)
            sp.dma_start(b2[:, :], w["b2"]).then_inc(loaded, 16)
            sp.dma_start(w1[:, :, :, :], w["w1"].rearrange("e (k p) n -> p e k n", p=P)).then_inc(loaded, 16)
            sp.dma_start(w2[:, :, :, :], w["w2"].rearrange("e (k p) n -> p e k n", p=P)).then_inc(loaded, 16)
            rows = out.rearrange("b o t d -> (b o t) d").rearrange("(g i p) d -> g p i d", p=P, i=TILES)
            with sp.Fori(0, CHUNKS) as g:
                wait_apart(sp, acc_step, g, 2 + TILES * NE, passed)
                sp.dma_start(rows[g], acc[:, :, :]).then_inc(stored.sem, 16)
            sp.wait_ge(stored.sem, stored.at(CHUNKS, 0))

        @block.gpsimd
        def _(pool):
            nc.gpsimd.memset(mean_w[:, :], 1.0 / DM).then_inc(consts_set, 1)
            nc.gpsimd.iota(number[:, :], pattern=[[1, NE]], base=0, channel_multiplier=0,
                           allow_small_or_imprecise_dtypes=True).then_inc(consts_set, 1)
            with pool.Fori(0, CHUNKS) as g:
                wait(pool, x_turned, g, 0)
                wait(pool, n_ready, g, 1)
                nc.gpsimd.tensor_tensor(held[:, :, :], tokens(g), n[:, :, :], ALU.add).then_inc(x_held.sem, 1)

        @block.tensor
        def _(pe):
            pe.wait_ge(consts_set, 2)
            pe.wait_ge(loaded, 16 * 5)
            for k in range(KC):
                last = nc.tensor.transpose(small[:, k * NE:(k + 1) * NE], router[:, k * P:(k + 1) * P],
                                           ident[0:NE, 0:NE])
            last.then_inc(router_turned, 1)
            pe.wait_ge(router_kept, 1)
            with pe.Fori(0, CHUNKS) as g:
                t = tokens(g)
                wait(pe, rstd_step, g, 0)
                for k in range(KC):
                    last = nc.tensor.matmul(stat[:, 0:HALF], mean_w[:, :], t[:, k], start=(k == 0), stop=(k == KC - 1))
                last.then_inc(mean_made.sem, 1)
                wait(pe, squared, g, 1)
                for k in range(KC):
                    last = nc.tensor.matmul(stat[:, 0:HALF], mean_w[:, :], sq[:, k, :],
                                            start=(k == 0), stop=(k == KC - 1))
                last.then_inc(var_made.sem, 1)
                wait(pe, n_ready, g, 1)
                wait(pe, weight_t_kept, g, 0)
                for i in range(TILES):
                    for k in range(KC):
                        last = nc.tensor.matmul(small[:, i * NE:(i + 1) * NE], n[:, k, i * P:(i + 1) * P],
                                                router_t[:, k, :], start=(k == 0), stop=(k == KC - 1))
                last.then_inc(logits_made.sem, 1)

                def hidden(e):
                    wait(pe, h_done, g, KC * (e - 1))
                    for m in range(KC):
                        for k in range(KC):
                            last = nc.tensor.matmul(h_bank[:, e % 2, m, 0:HALF], w1[:, e, k, m * P:(m + 1) * P],
                                                    n[:, k, :], start=(k == 0), stop=(k == KC - 1))
                    last.then_inc(h_made.sem, 1)

                hidden(0)
                wait(pe, acc_step, g, 0)
                wait(pe, x_held, g, 1)
                for i in range(TILES):
                    for k in range(KC):
                        last = nc.tensor.transpose(y_tile[i][:, k * P:(k + 1) * P], held[:, k, i * P:(i + 1) * P],
                                                   ident[:, :])
                last.then_inc(x_turned.sem, 1)
                wait(pe, weight_ready, g, 1)
                for i in range(TILES):
                    last = nc.tensor.transpose(small[0:NE, i * P:(i + 1) * P], weight[:, i, :], ident[:, :])
                last.then_inc(weight_turned.sem, 1)
                hidden(1)
                wait(pe, weight_t_kept, g, 1)
                wait(pe, acc_step, g, 1)
                for i in range(TILES):
                    last = nc.tensor.matmul(y_tile[i], weight_t[:, i * P:(i + 1) * P], b2[:, :], start=True, stop=True)
                last.then_inc(bias_made.sem, 1)
                for e in range(NE):
                    wait(pe, h_done, g, KC * (e + 1))
                    wait(pe, acc_step, g, 2 + TILES * e)
                    for i in range(TILES):
                        for k in range(KC):
                            last = nc.tensor.matmul(y_tile[i], hg[:, e % 2, k, i * P:(i + 1) * P], w2[:, e, k, :],
                                                    start=(k == 0), stop=(k == KC - 1))
                    last.then_inc(y_made.sem, 1)
                    if e + 2 < NE:
                        hidden(e + 2)

        @block.scalar
        def _(act):
            act.wait_ge(router_turned, 1)
            nc.scalar.copy(router_t[:, :, :], small[:, 0:KC * NE].rearrange("p (k e) -> p k e", k=KC)
                           ).then_inc(router_kept, 1)
            with act.Fori(0, CHUNKS) as g:
                wait(act, centred, g, 1)
                nc.scalar.activation(sq[:, :, :], n[:, :, :], ACT.Square).then_inc(squared.sem, 1)
                wait(act, var_made, g, 1)
                nc.scalar.activation(rstd[:, :], stat[:, 0:HALF], ACT.Ln, bias=eps5[:, 0:1]).then_inc(rstd_step.sem, 1)
                wait(act, rstd_step, g, 1)
                nc.scalar.activation(rstd[:, :], rstd[:, :], ACT.Exp, scale=-0.5).then_inc(rstd_step.sem, 1)
                wait(act, route_step, g, 7)
                nc.scalar.activation(logit[:, :, :], logit[:, :, :], ACT.Exp).then_inc(top_exp.sem, 1)
                for e in range(NE):
                    wait(act, h_made, g, e + 1)
                    wait(act, y_made, g, e - 1)
                    for m in range(KC):
                        nc.scalar.activation(hg[:, e % 2, m, :], h_bank[:, e % 2, m, 0:HALF], ACT.Gelu,
                                             bias=b1[:, e, m:m + 1]).then_inc(h_done.sem, 1)

        @block.vector
        def _(dve):
            dve.wait_ge(consts_set, 2)
            with dve.Fori(0, CHUNKS) as g:
                t = tokens(g)
                wait(dve, h_made, g, 0)
                wait(dve, x_held, g, 0)
                wait(dve, mean_made, g, 1)
                nc.vector.tensor_tensor(n[:, :, :], t, stat[:, 0:HALF].unsqueeze(1).broadcast_to([P, KC, HALF]),
                                        ALU.subtract).then_inc(centred.sem, 1)
                wait(dve, rstd_step, g, 2)
                wait(dve, squared, g, 1)
                nc.vector.tensor_tensor(n[:, :, :], n[:, :, :], rstd[:, :].unsqueeze(1).broadcast_to([P, KC, HALF]),
                                        ALU.mult).then_inc(n_ready.sem, 1)
                wait(dve, logits_made, g, 1)
                nc.vector.tensor_copy(logit[:, :, :], small[:, 0:TILES * NE].rearrange("p (i e) -> p i e", i=TILES)
                                      ).then_inc(route_step.sem, 1)
                wait_apart(dve, route_step, g, 1, passed)
                for i in range(TILES):
                    last = nc.vector.max(best[:, i, :], logit[:, i, :])
                last.then_inc(route_step.sem, 1)
                wait_apart(dve, route_step, g, 2, passed)
                for i in range(TILES):
                    last = nc.vector.max_index(best_at[:, i, :], best[:, i, :], logit[:, i, :])
                last.then_inc(route_step.sem, 1)
                wait(dve, route_step, g, 3)
                nc.vector.tensor_copy(at_f[:, :, :], best_at[:, :, 0:2]).then_inc(route_step.sem, 1)
                nc.vector.tensor_tensor(logit[:, :, :], logit[:, :, :], best[:, :, 0:1].broadcast_to([P, TILES, NE]),
                                        ALU.subtract).then_inc(route_step.sem, 3)
                wait(dve, top_exp, g, 1)
                nc.vector.tensor_reduce(total[:, :], logit[:, :, :], AX.X, ALU.add).then_inc(route_step.sem, 1)
                wait(dve, route_step, g, 8)
                nc.vector.reciprocal(total[:, :], total[:, :]).then_inc(route_step.sem, 1)
                wait(dve, route_step, g, 9)
                nc.vector.tensor_tensor(logit[:, :, :], logit[:, :, :],
                                        total[:, :].unsqueeze(2).broadcast_to([P, TILES, NE]), ALU.mult
                                        ).then_inc(route_step.sem, 1)
                wait(dve, route_step, g, 10)
                for i in range(TILES):
                    for r, dst in ((0, weight), (1, other)):
                        last = nc.vector.scalar_tensor_tensor(out=dst[:, i, :], in0=number[:, :],
                                                              scalar=at_f[:, i, r:r + 1], in1=logit[:, i, :],
                                                              op0=ALU.is_equal, op1=ALU.mult)
                last.then_inc(route_step.sem, 1)
                wait(dve, route_step, g, 11)
                wait(dve, weight_turned, g, 0)
                nc.vector.tensor_tensor(other[:, :, :], weight[:, :, :], other[:, :, :], ALU.add
                                        ).then_inc(route_step.sem, 1)
                wait(dve, route_step, g, 12)
                nc.vector.tensor_reduce(total[:, :], other[:, :, :], AX.X, ALU.add).then_inc(route_step.sem, 1)
                wait(dve, route_step, g, 13)
                nc.vector.tensor_scalar(total[:, :], total[:, :], 1e-12, None, ALU.max).then_inc(total_step.sem, 1)
                wait(dve, total_step, g, 1)
                nc.vector.reciprocal(total[:, :], total[:, :]).then_inc(total_step.sem, 1)
                wait(dve, total_step, g, 2)
                nc.vector.tensor_tensor(weight[:, :, :], other[:, :, :],
                                        total[:, :].unsqueeze(2).broadcast_to([P, TILES, NE]), ALU.mult
                                        ).then_inc(weight_ready.sem, 1)
                wait(dve, stored, g, 0)
                wait(dve, x_turned, g, 1)
                nc.vector.tensor_copy(acc[:, :, :], y_all).then_inc(acc_step.sem, 1)
                wait(dve, weight_turned, g, 1)
                nc.vector.tensor_copy(weight_t[:, :], small[0:NE, 0:HALF]).then_inc(weight_t_kept.sem, 1)
                wait(dve, bias_made, g, 1)
                wait(dve, acc_step, g, 1)
                nc.vector.tensor_tensor(acc[:, :, :], acc[:, :, :], y_all, ALU.add).then_inc(acc_step.sem, 1)
                wait(dve, weight_ready, g, 1)
                for e in range(NE):
                    wait(dve, y_made, g, e + 1)
                    wait(dve, acc_step, g, 2 + TILES * e)
                    for i in range(TILES):
                        nc.vector.scalar_tensor_tensor(out=acc[:, i, :], in0=y_tile[i], scalar=weight[:, i, e:e + 1],
                                                       in1=acc[:, i, :], op0=ALU.mult, op1=ALU.add
                                                       ).then_inc(acc_step.sem, 1)


def conv_attn_hybrid(nc, x, pe, ln_w, ln_b, in_proj, conv_w, conv_b, x_proj, dt_w, dt_b, A_log, Dp, out_proj,
                     W, a, router_w, w1, b1, w2, b2, out):
    with ExitStack() as ctx:
        X = ctx.enter_context(nc.sbuf_tensor("X", [P, KC, TOK], F32))
        ident = ctx.enter_context(nc.sbuf_tensor("ident", [P, P], F32))
        eps5 = ctx.enter_context(nc.sbuf_tensor("eps5", [P, 1], F32))
        load_tokens(nc, x, pe, X, ident, eps5)
        mamba(nc, X, ident, eps5, dict(ln_w=ln_w, ln_b=ln_b, in_proj=in_proj, conv_w=conv_w, conv_b=conv_b,
                                       x_proj=x_proj, dt_w=dt_w, dt_b=dt_b, A_log=A_log, Dp=Dp, out_proj=out_proj))
        attention(nc, X, ident, eps5, dict(W=W, a=a))
        experts(nc, X, ident, eps5, dict(router_w=router_w, w1=w1, b1=b1, w2=w2, b2=b2), out)


_INS = ["x"] + ["L0_conv_" + n for n in ("pe", "ln_w", "ln_b", "in_proj", "conv_w", "conv_b", "x_proj", "dt_w",
                                         "dt_b", "A_log", "Dp", "out_proj")] + \
    ["L1_attn_W", "L1_attn_a", "L1_ffn_router_w", "L1_ffn_w1", "L1_ffn_b1", "L1_ffn_w2", "L1_ffn_b2"]


def kernel(**inputs):
    import numpy as _np
    import concourse.bacc as _bacc
    from concourse import mybir as _mybir
    from concourse.bass_utils import run_bass_kernel_spmd as _run

    nc = _bacc.Bacc("TRN2", target_bir_lowering=False, num_devices=1)
    arrays, args = {}, []
    for name in _INS:
        arr = _np.ascontiguousarray(inputs[name])
        arrays[f"in_{name}"] = arr
        args.append(nc.dram_tensor(f"in_{name}", arr.shape, _mybir.dt.from_np(arr.dtype), kind="ExternalInput").ap())
    out = nc.dram_tensor("out_tokens", (NB, NO, NT, DM), _mybir.dt.float32, kind="ExternalOutput").ap()
    conv_attn_hybrid(nc, *args, out)
    r = _run(nc, [arrays], core_ids=[0])
    return r.results[0]["out_tokens"]
```
